# Optimizing a Trainium2 kernel written in Bass

```python
import numpy as np
import jax
import jax.numpy as jnp

def _softmax(x, axis=-1):
    return jax.nn.softmax(x, axis=axis)

def _gelu(x):
    return jax.nn.gelu(x, approximate=True)

def _silu(x):
    return jax.nn.silu(x)

def _sigmoid(x):
    return jax.nn.sigmoid(x)

def _layernorm(x, axis=-1, eps=1e-05):
    m = jnp.mean(x, axis=axis, keepdims=True)
    v = jnp.var(x, axis=axis, keepdims=True)
    return (x - m) / jnp.sqrt(v + eps)

def _scatter_add(tgt, idx, src, axis=0):
    return tgt.at[idx].add(src)

def _segment_sum(src, seg, n):
    return jax.ops.segment_sum(src, seg, n)
kernel_name = 'mk_flamingo_gated_d2_seqx_r4_602f6e'

def setup_inputs(seed: int=0):
    np.random.seed(seed)
    _w = jnp.asarray

    def _rec_inputs():
        import jax
        import jax.numpy as jnp
        _rk = jax.random.key(seed)
        x = -0.0003929 + 0.9999 * jax.random.normal(jax.random.fold_in(_rk, 1), (8, 256, 256), jnp.float32)
        _lenS = 256 - jax.random.randint(jax.random.fold_in(_rk, 7), (8,), 0, max(1, 256 // 4) + 1, jnp.int32)
        _lenS2 = 256 - jax.random.randint(jax.random.fold_in(_rk, 8), (8,), 0, max(1, 256 // 4) + 1, jnp.int32)
        _ctx_1024P = jax.random.normal(jax.random.fold_in(_rk, 11), (8, 16, 256), jnp.float32)
        _ctx_1024c = jax.random.dirichlet(jax.random.fold_in(_rk, 511), 0.3 * jnp.ones((16,), jnp.float32), (8, 256))
        _ctx_1024t = jnp.einsum('bsk,bkd->bsd', _ctx_1024c, _ctx_1024P)
        _ctx_1024t = _ctx_1024t * jax.lax.rsqrt(jnp.mean(jnp.square(_ctx_1024t)) + 1e-12) * 0.953939
        ctx_1024 = 2.81802e-05 + 1.00001 * (_ctx_1024t + 0.3 * jax.random.normal(jax.random.fold_in(_rk, 611), (8, 256, 256), jnp.float32))
        _validS = jnp.arange(256)[None, :] < _lenS[:, None]
        _validS2 = jnp.arange(256)[None, :] < _lenS2[:, None]
        _causal = jnp.tril(jnp.ones((256, 256), dtype=bool))
        mask_BxSxS2_ik0 = jnp.where(jnp.broadcast_to(_validS2[:, None, :], (8, 256, 256)), 0, 1).astype(jnp.int32)
        _g = jax.random.normal(jax.random.fold_in(_rk, 9001), (2, 2), jnp.float32)
        _g = jnp.sign(_g) * jnp.maximum(jnp.abs(_g), 1.0) + (_g == 0) * 1.0
        g_xattn = _g[0]
        g_ffn = _g[1]
        return (x, ctx_1024, mask_BxSxS2_ik0, g_xattn, g_ffn)
    x, ctx_1024, mask_BxSxS2_ik0, g_xattn, g_ffn = _rec_inputs()

    def _L0_xattn_setup():
        import jax, jax.numpy as jnp
        import numpy as np
        import math
        B, N, M, D, HID, OUT = (8, 512, 512, 256, 256, 256)
        key = jax.random.key(seed)
        k1, k2, k3, k4, k5, k6 = jax.random.split(key, 6)
        h1 = jax.random.normal(k1, (B, N, D), dtype=jnp.float32)
        h2 = jax.random.normal(k2, (B, M, D), dtype=jnp.float32)
        mask = jax.random.randint(k3, (B, N, M), 0, 2, dtype=jnp.int32)
        Wq = jax.random.normal(k4, (HID, D), dtype=jnp.float32) / math.sqrt(D)
        Wk = jax.random.normal(k5, (HID, D), dtype=jnp.float32) / math.sqrt(D)
        Wv = jax.random.normal(k6, (OUT, D), dtype=jnp.float32) / math.sqrt(D)
        return {'h1': h1, 'h2': h2, 'mask': mask, 'Wq': Wq, 'Wk': Wk, 'Wv': Wv}
    _L0_xattn_all = _L0_xattn_setup()
    _L0_xattn_in = {k: v for k, v in _L0_xattn_all.items() if k in ('Wq', 'Wk', 'Wv')}
    del _L0_xattn_all

    def _L0_ffn_setup():
        import jax, jax.numpy as jnp
        import numpy as np
        D_MODEL = 256
        E = 4
        MIN_E = 1
        TH_LO = 0.5
        TH_HI = 2.0
        key = jax.random.key(seed)
        ks = jax.random.split(key, 12)
        B, N, D, H = (4, 512, D_MODEL, 2 * D_MODEL)
        s = 0.02
        return {'x': jax.random.normal(ks[0], (B, N, D), dtype=jnp.float32), 'gate_w': jax.random.normal(ks[1], (D, E), dtype=jnp.float32) * s, 'gate_b': jnp.zeros((E,), dtype=jnp.float32), 'dp_w1': jax.random.normal(ks[2], (D, D // 2), dtype=jnp.float32) * s, 'dp_b1': jnp.zeros((D // 2,), dtype=jnp.float32), 'dp_w2': jax.random.normal(ks[3], (D // 2, 1), dtype=jnp.float32) * s, 'dp_b2': jnp.zeros((1,), dtype=jnp.float32), 'ew1': jax.random.normal(ks[4], (E, D, H), dtype=jnp.float32) * s, 'eb1': jnp.zeros((E, H), dtype=jnp.float32), 'ew2': jax.random.normal(ks[5], (E, H, D), dtype=jnp.float32) * s, 'eb2': jnp.zeros((E, D), dtype=jnp.float32)}
    _L0_ffn_all = _L0_ffn_setup()
    _L0_ffn_in = {k: v for k, v in _L0_ffn_all.items() if k in ('gate_w', 'gate_b', 'dp_w1', 'dp_b1', 'dp_w2', 'dp_b2', 'ew1', 'eb1', 'ew2', 'eb2')}
    del _L0_ffn_all

    def _L1_xattn_setup():
        import jax, jax.numpy as jnp
        import numpy as np
        D_MODEL = 256
        NUM_HEADS = 8
        GRID_SIZE = 5
        SPLINE_ORDER = 3
        LN_EPS = 1e-05

        def _grid():
            h = 2.0 / GRID_SIZE
            g = jnp.arange(-SPLINE_ORDER, GRID_SIZE + SPLINE_ORDER + 1, dtype=jnp.float32) * h - 1.0
            return jnp.broadcast_to(g, (D_MODEL, g.shape[0]))

        def _b_splines(x, grid):
            x = x[..., None]
            bases = ((x >= grid[:, :-1]) & (x < grid[:, 1:])).astype(x.dtype)
            for k in range(1, SPLINE_ORDER + 1):
                bases = (x - grid[:, :-(k + 1)]) / (grid[:, k:-1] - grid[:, :-(k + 1)]) * bases[..., :-1] + (grid[:, k + 1:] - x) / (grid[:, k + 1:] - grid[:, 1:-k]) * bases[..., 1:]
            return bases

        def _kan_linear(x, base_w, spline_w, spline_scaler, grid):
            shape = x.shape
            x2 = x.reshape(-1, D_MODEL)
            base = jax.nn.silu(x2) @ base_w.T
            scaled_sw = spline_w * spline_scaler[..., None]
            splines = _b_splines(x2, grid).reshape(x2.shape[0], -1)
            spl = splines @ scaled_sw.reshape(D_MODEL, -1).T
            return (base + spl).reshape(*shape[:-1], D_MODEL)

        def _layernorm(x, g, b):
            mu = jnp.mean(x, axis=-1, keepdims=True)
            var = jnp.mean(jnp.square(x - mu), axis=-1, keepdims=True)
            return (x - mu) * jax.lax.rsqrt(var + LN_EPS) * g + b
        key = jax.random.key(seed)
        ks = jax.random.split(key, 8)
        d = D_MODEL
        s = 0.02
        return {'visual_tokens': jax.random.normal(ks[0], (8, 256, d), jnp.float32), 'top_k_report_tokens': jax.random.normal(ks[1], (8, 32, d), jnp.float32), 'wq': jax.random.normal(ks[2], (d, d), jnp.float32) * s, 'bq': jnp.zeros((d,), jnp.float32), 'wk': jax.random.normal(ks[3], (d, d), jnp.float32) * s, 'bk': jnp.zeros((d,), jnp.float32), 'wv': jax.random.normal(ks[4], (d, d), jnp.float32) * s, 'bv': jnp.zeros((d,), jnp.float32), 'ln_g': jnp.ones((d,), jnp.float32), 'ln_b': jnp.zeros((d,), jnp.float32), 'kan_base_w': jax.random.normal(ks[5], (d, d), jnp.float32) * s, 'kan_spline_w': jax.random.normal(ks[6], (d, d, GRID_SIZE + SPLINE_ORDER), jnp.float32) * s, 'kan_spline_scaler': jax.random.normal(ks[7], (d, d), jnp.float32) * s + 1.0}
    _L1_xattn_all = _L1_xattn_setup()
    _L1_xattn_in = {k: v for k, v in _L1_xattn_all.items() if k in ('wq', 'bq', 'wk', 'bk', 'wv', 'bv', 'ln_g', 'ln_b', 'kan_base_w', 'kan_spline_w', 'kan_spline_scaler')}
    del _L1_xattn_all

    def _L1_ffn_setup():
        import jax, jax.numpy as jnp
        import numpy as np
        D = 256
        HD = 128
        EA = 8
        KA = 2
        EF = 16
        KF = 2
        FH = 128
        MAXP = 64
        B, S = (4, 256)
        EPS = 1e-05

        def _layer_norm(x, w, b):
            mu = x.mean(-1, keepdims=True)
            var = ((x - mu) ** 2).mean(-1, keepdims=True)
            return (x - mu) * jax.lax.rsqrt(var + EPS) * w + b

        def _topk_gates(logits, k):
            top_vals, top_idx = jax.lax.top_k(logits, k)
            g = jax.nn.softmax(top_vals, axis=-1)
            onehot = jax.nn.one_hot(top_idx, logits.shape[-1], dtype=logits.dtype)
            return jnp.einsum('...k,...ke->...e', g, onehot)

        def _moa(x, gate_w, q_w, q_b, k_w, k_b, v_w, v_b, o_w, o_b, rel_table):
            S_ = x.shape[1]
            gates = _topk_gates(x @ gate_w, KA)
            q = (jnp.einsum('bsd,edh->bseh', x, q_w) + q_b) * HD ** (-0.5)
            k = x @ k_w + k_b
            v = x @ v_w + v_b
            scores = jnp.einsum('bqeh,bkh->beqk', q, k)
            rel_s = jnp.einsum('bqeh,rh->beqr', q, rel_table)
            pos = jnp.arange(S_)
            rel_idx = jnp.clip(pos[None, :] - pos[:, None], -MAXP, MAXP) + MAXP
            scores = scores + jnp.take_along_axis(rel_s, rel_idx[None, None], axis=-1)
            p = jax.nn.softmax(scores, axis=-1)
            ctx = jnp.einsum('beqk,bkh->bqeh', p, v)
            out = jnp.einsum('bqeh,ehd,bqe->bqd', ctx, o_w, gates)
            return out + jnp.einsum('bqe,ed->bqd', gates, o_b)

        def _moe_ffn(x, gate_w, w1, b1, w2, b2):
            gates = _topk_gates(x @ gate_w, KF)
            h = jax.nn.relu(jnp.einsum('bsd,edh->bseh', x, w1) + b1)
            out = jnp.einsum('bseh,ehd,bse->bsd', h, w2, gates)
            return out + jnp.einsum('bse,ed->bsd', gates, b2)
        key = jax.random.key(seed)
        ks = jax.random.split(key, 12)
        r = lambda i, shape, scale=0.02: jax.random.normal(ks[i], shape, jnp.float32) * scale
        return {'src': jax.random.normal(ks[0], (B, S, D), jnp.float32), 'ln1_w': jnp.ones((D,), jnp.float32), 'ln1_b': jnp.zeros((D,), jnp.float32), 'ln2_w': jnp.ones((D,), jnp.float32), 'ln2_b': jnp.zeros((D,), jnp.float32), 'attn_gate_w': r(1, (D, EA)), 'q_w': r(2, (EA, D, HD)), 'q_b': jnp.zeros((EA, HD), jnp.float32), 'k_w': r(3, (D, HD)), 'k_b': jnp.zeros((HD,), jnp.float32), 'v_w': r(4, (D, HD)), 'v_b': jnp.zeros((HD,), jnp.float32), 'o_w': r(5, (EA, HD, D)), 'o_b': jnp.zeros((EA, D), jnp.float32), 'rel_table': r(6, (2 * MAXP + 1, HD)), 'ff_gate_w': r(7, (D, EF)), 'ff_w1': r(8, (EF, D, FH)), 'ff_b1': jnp.zeros((EF, FH), jnp.float32), 'ff_w2': r(9, (EF, FH, D)), 'ff_b2': jnp.zeros((EF, D), jnp.float32)}
    _L1_ffn_all = _L1_ffn_setup()
    _L1_ffn_in = {k: v for k, v in _L1_ffn_all.items() if k in ('ln1_w', 'ln1_b', 'ln2_w', 'ln2_b', 'attn_gate_w', 'q_w', 'q_b', 'k_w', 'k_b', 'v_w', 'v_b', 'o_w', 'o_b', 'rel_table', 'ff_gate_w', 'ff_w1', 'ff_b1', 'ff_w2', 'ff_b2')}
    del _L1_ffn_all
    return {'x': x, 'ctx_1024': ctx_1024, 'mask_BxSxS2_ik0': mask_BxSxS2_ik0, 'g_xattn': g_xattn, 'g_ffn': g_ffn, 'L0_xattn_Wq': _L0_xattn_in['Wq'], 'L0_xattn_Wk': _L0_xattn_in['Wk'], 'L0_xattn_Wv': _L0_xattn_in['Wv'], 'L0_ffn_gate_w': _L0_ffn_in['gate_w'], 'L0_ffn_gate_b': _L0_ffn_in['gate_b'], 'L0_ffn_dp_w1': _L0_ffn_in['dp_w1'], 'L0_ffn_dp_b1': _L0_ffn_in['dp_b1'], 'L0_ffn_dp_w2': _L0_ffn_in['dp_w2'], 'L0_ffn_dp_b2': _L0_ffn_in['dp_b2'], 'L0_ffn_ew1': _L0_ffn_in['ew1'], 'L0_ffn_eb1': _L0_ffn_in['eb1'], 'L0_ffn_ew2': _L0_ffn_in['ew2'], 'L0_ffn_eb2': _L0_ffn_in['eb2'], 'L1_xattn_wq': _L1_xattn_in['wq'], 'L1_xattn_bq': _L1_xattn_in['bq'], 'L1_xattn_wk': _L1_xattn_in['wk'], 'L1_xattn_bk': _L1_xattn_in['bk'], 'L1_xattn_wv': _L1_xattn_in['wv'], 'L1_xattn_bv': _L1_xattn_in['bv'], 'L1_xattn_ln_g': _L1_xattn_in['ln_g'], 'L1_xattn_ln_b': _L1_xattn_in['ln_b'], 'L1_xattn_kan_base_w': _L1_xattn_in['kan_base_w'], 'L1_xattn_kan_spline_w': _L1_xattn_in['kan_spline_w'], 'L1_xattn_kan_spline_scaler': _L1_xattn_in['kan_spline_scaler'], 'L1_ffn_ln1_w': _L1_ffn_in['ln1_w'], 'L1_ffn_ln1_b': _L1_ffn_in['ln1_b'], 'L1_ffn_ln2_w': _L1_ffn_in['ln2_w'], 'L1_ffn_ln2_b': _L1_ffn_in['ln2_b'], 'L1_ffn_attn_gate_w': _L1_ffn_in['attn_gate_w'], 'L1_ffn_q_w': _L1_ffn_in['q_w'], 'L1_ffn_q_b': _L1_ffn_in['q_b'], 'L1_ffn_k_w': _L1_ffn_in['k_w'], 'L1_ffn_k_b': _L1_ffn_in['k_b'], 'L1_ffn_v_w': _L1_ffn_in['v_w'], 'L1_ffn_v_b': _L1_ffn_in['v_b'], 'L1_ffn_o_w': _L1_ffn_in['o_w'], 'L1_ffn_o_b': _L1_ffn_in['o_b'], 'L1_ffn_rel_table': _L1_ffn_in['rel_table'], 'L1_ffn_ff_gate_w': _L1_ffn_in['ff_gate_w'], 'L1_ffn_ff_w1': _L1_ffn_in['ff_w1'], 'L1_ffn_ff_b1': _L1_ffn_in['ff_b1'], 'L1_ffn_ff_w2': _L1_ffn_in['ff_w2'], 'L1_ffn_ff_b2': _L1_ffn_in['ff_b2']}

def reference(x, ctx_1024, mask_BxSxS2_ik0, g_xattn, g_ffn, L0_xattn_Wq, L0_xattn_Wk, L0_xattn_Wv, L0_ffn_gate_w, L0_ffn_gate_b, L0_ffn_dp_w1, L0_ffn_dp_b1, L0_ffn_dp_w2, L0_ffn_dp_b2, L0_ffn_ew1, L0_ffn_eb1, L0_ffn_ew2, L0_ffn_eb2, L1_xattn_wq, L1_xattn_bq, L1_xattn_wk, L1_xattn_bk, L1_xattn_wv, L1_xattn_bv, L1_xattn_ln_g, L1_xattn_ln_b, L1_xattn_kan_base_w, L1_xattn_kan_spline_w, L1_xattn_kan_spline_scaler, L1_ffn_ln1_w, L1_ffn_ln1_b, L1_ffn_ln2_w, L1_ffn_ln2_b, L1_ffn_attn_gate_w, L1_ffn_q_w, L1_ffn_q_b, L1_ffn_k_w, L1_ffn_k_b, L1_ffn_v_w, L1_ffn_v_b, L1_ffn_o_w, L1_ffn_o_b, L1_ffn_rel_table, L1_ffn_ff_gate_w, L1_ffn_ff_w1, L1_ffn_ff_b1, L1_ffn_ff_w2, L1_ffn_ff_b2):
    import jax
    import jax.numpy as jnp

    def _L0_xattn_ref(h1, h2, mask, Wq, Wk, Wv):
        import jax, jax.numpy as jnp
        import numpy as np
        import math
        B, N, M, D, HID, OUT = (8, 512, 512, 256, 256, 256)
        Q = jnp.einsum('bnd,hd->bnh', h1, Wq)
        K = jnp.einsum('bmd,hd->bmh', h2, Wk)
        V = jnp.einsum('bmd,od->bmo', h2, Wv)
        E = jnp.einsum('bnh,bmh->bnm', Q, K)
        E = jnp.where(mask == 0, jnp.float32(-10000000000.0), E)
        A = jax.nn.softmax(E / math.sqrt(HID), axis=2)
        return jnp.einsum('bnm,bmo->bno', A, V)

    def _L0_ffn_ref(x, gate_w, gate_b, dp_w1, dp_b1, dp_w2, dp_b2, ew1, eb1, ew2, eb2):
        import jax, jax.numpy as jnp
        import numpy as np
        D_MODEL = 256
        E = 4
        MIN_E = 1
        TH_LO = 0.5
        TH_HI = 2.0
        B, N, D = x.shape
        xf = x.reshape(B * N, D)
        T = B * N
        h = jax.nn.relu(xf @ dp_w1 + dp_b1)
        entropy = jax.nn.softplus(h @ dp_w2 + dp_b2)[:, 0]
        norm = jnp.clip((entropy - TH_LO) / (TH_HI - TH_LO), 0.0, 1.0)
        k_tok = jnp.clip(jnp.round(MIN_E + norm * (E - MIN_E)).astype(jnp.int32), MIN_E, E)
        logits = xf @ gate_w + gate_b
        top_logits, top_idx = jax.lax.top_k(logits, E)
        pos = jnp.arange(E)
        sel = pos[None, :] < k_tok[:, None]
        masked = jnp.where(sel, top_logits, -jnp.inf)
        w_top = jax.nn.softmax(masked, axis=-1)
        dense_w = jnp.zeros((T, E), dtype=xf.dtype).at[jnp.arange(T)[:, None], top_idx].set(w_top)
        hid = jax.nn.relu(jnp.einsum('td,edh->teh', xf, ew1) + eb1[None, :, :])
        y = jnp.einsum('teh,ehd->ted', hid, ew2) + eb2[None, :, :]
        out = jnp.einsum('te,ted->td', dense_w, y)
        return out.reshape(B, N, D)

    def _L1_xattn_ref(visual_tokens, top_k_report_tokens, wq, bq, wk, bk, wv, bv, ln_g, ln_b, kan_base_w, kan_spline_w, kan_spline_scaler):
        import jax, jax.numpy as jnp
        import numpy as np
        D_MODEL = 256
        NUM_HEADS = 8
        GRID_SIZE = 5
        SPLINE_ORDER = 3
        LN_EPS = 1e-05

        def _grid():
            h = 2.0 / GRID_SIZE
            g = jnp.arange(-SPLINE_ORDER, GRID_SIZE + SPLINE_ORDER + 1, dtype=jnp.float32) * h - 1.0
            return jnp.broadcast_to(g, (D_MODEL, g.shape[0]))

        def _b_splines(x, grid):
            x = x[..., None]
            bases = ((x >= grid[:, :-1]) & (x < grid[:, 1:])).astype(x.dtype)
            for k in range(1, SPLINE_ORDER + 1):
                bases = (x - grid[:, :-(k + 1)]) / (grid[:, k:-1] - grid[:, :-(k + 1)]) * bases[..., :-1] + (grid[:, k + 1:] - x) / (grid[:, k + 1:] - grid[:, 1:-k]) * bases[..., 1:]
            return bases

        def _kan_linear(x, base_w, spline_w, spline_scaler, grid):
            shape = x.shape
            x2 = x.reshape(-1, D_MODEL)
            base = jax.nn.silu(x2) @ base_w.T
            scaled_sw = spline_w * spline_scaler[..., None]
            splines = _b_splines(x2, grid).reshape(x2.shape[0], -1)
            spl = splines @ scaled_sw.reshape(D_MODEL, -1).T
            return (base + spl).reshape(*shape[:-1], D_MODEL)

        def _layernorm(x, g, b):
            mu = jnp.mean(x, axis=-1, keepdims=True)
            var = jnp.mean(jnp.square(x - mu), axis=-1, keepdims=True)
            return (x - mu) * jax.lax.rsqrt(var + LN_EPS) * g + b
        B, Nv, d = visual_tokens.shape
        hd = d // NUM_HEADS
        q = visual_tokens @ wq.T + bq
        res = q
        k = top_k_report_tokens @ wk.T + bk
        v = top_k_report_tokens @ wv.T + bv
        qh = q.reshape(B, Nv, NUM_HEADS, hd).transpose(0, 2, 1, 3)
        kh = k.reshape(B, -1, NUM_HEADS, hd).transpose(0, 2, 1, 3)
        vh = v.reshape(B, -1, NUM_HEADS, hd).transpose(0, 2, 1, 3)
        attn = jax.nn.softmax(jnp.einsum('bhqd,bhkd->bhqk', qh, kh) * d ** (-0.5), axis=-1)
        out = jnp.einsum('bhqk,bhkd->bhqd', attn, vh)
        out = out.transpose(0, 2, 1, 3).reshape(B, Nv, d)
        out = _layernorm(res + out, ln_g, ln_b)
        return _kan_linear(out, kan_base_w, kan_spline_w, kan_spline_scaler, _grid())

    def _L1_ffn_ref(src, ln1_w, ln1_b, ln2_w, ln2_b, attn_gate_w, q_w, q_b, k_w, k_b, v_w, v_b, o_w, o_b, rel_table, ff_gate_w, ff_w1, ff_b1, ff_w2, ff_b2):
        import jax, jax.numpy as jnp
        import numpy as np
        D = 256
        HD = 128
        EA = 8
        KA = 2
        EF = 16
        KF = 2
        FH = 128
        MAXP = 64
        B, S = (4, 256)
        EPS = 1e-05

        def _layer_norm(x, w, b):
            mu = x.mean(-1, keepdims=True)
            var = ((x - mu) ** 2).mean(-1, keepdims=True)
            return (x - mu) * jax.lax.rsqrt(var + EPS) * w + b

        def _topk_gates(logits, k):
            top_vals, top_idx = jax.lax.top_k(logits, k)
            g = jax.nn.softmax(top_vals, axis=-1)
            onehot = jax.nn.one_hot(top_idx, logits.shape[-1], dtype=logits.dtype)
            return jnp.einsum('...k,...ke->...e', g, onehot)

        def _moa(x, gate_w, q_w, q_b, k_w, k_b, v_w, v_b, o_w, o_b, rel_table):
            S_ = x.shape[1]
            gates = _topk_gates(x @ gate_w, KA)
            q = (jnp.einsum('bsd,edh->bseh', x, q_w) + q_b) * HD ** (-0.5)
            k = x @ k_w + k_b
            v = x @ v_w + v_b
            scores = jnp.einsum('bqeh,bkh->beqk', q, k)
            rel_s = jnp.einsum('bqeh,rh->beqr', q, rel_table)
            pos = jnp.arange(S_)
            rel_idx = jnp.clip(pos[None, :] - pos[:, None], -MAXP, MAXP) + MAXP
            scores = scores + jnp.take_along_axis(rel_s, rel_idx[None, None], axis=-1)
            p = jax.nn.softmax(scores, axis=-1)
            ctx = jnp.einsum('beqk,bkh->bqeh', p, v)
            out = jnp.einsum('bqeh,ehd,bqe->bqd', ctx, o_w, gates)
            return out + jnp.einsum('bqe,ed->bqd', gates, o_b)

        def _moe_ffn(x, gate_w, w1, b1, w2, b2):
            gates = _topk_gates(x @ gate_w, KF)
            h = jax.nn.relu(jnp.einsum('bsd,edh->bseh', x, w1) + b1)
            out = jnp.einsum('bseh,ehd,bse->bsd', h, w2, gates)
            return out + jnp.einsum('bse,ed->bsd', gates, b2)
        res = src
        xn = _layer_norm(src, ln1_w, ln1_b)
        x = res + _moa(xn, attn_gate_w, q_w, q_b, k_w, k_b, v_w, v_b, o_w, o_b, rel_table)
        res = x
        xn = _layer_norm(x, ln2_w, ln2_b)
        return res + _moe_ffn(xn, ff_gate_w, ff_w1, ff_b1, ff_w2, ff_b2)
    x = x + jnp.tanh(g_xattn[0]) * _L0_xattn_ref(_layernorm(x, axis=-1), ctx_1024, mask_BxSxS2_ik0, L0_xattn_Wq, L0_xattn_Wk, L0_xattn_Wv)
    x = x + jnp.tanh(g_ffn[0]) * _L0_ffn_ref(_layernorm(x, axis=-1), L0_ffn_gate_w, L0_ffn_gate_b, L0_ffn_dp_w1, L0_ffn_dp_b1, L0_ffn_dp_w2, L0_ffn_dp_b2, L0_ffn_ew1, L0_ffn_eb1, L0_ffn_ew2, L0_ffn_eb2)
    x = x + jnp.tanh(g_xattn[1]) * _L1_xattn_ref(_layernorm(x, axis=-1), ctx_1024, L1_xattn_wq, L1_xattn_bq, L1_xattn_wk, L1_xattn_bk, L1_xattn_wv, L1_xattn_bv, L1_xattn_ln_g, L1_xattn_ln_b, L1_xattn_kan_base_w, L1_xattn_kan_spline_w, L1_xattn_kan_spline_scaler)
    x = x + jnp.tanh(g_ffn[1]) * _L1_ffn_ref(_layernorm(x, axis=-1), L1_ffn_ln1_w, L1_ffn_ln1_b, L1_ffn_ln2_w, L1_ffn_ln2_b, L1_ffn_attn_gate_w, L1_ffn_q_w, L1_ffn_q_b, L1_ffn_k_w, L1_ffn_k_b, L1_ffn_v_w, L1_ffn_v_b, L1_ffn_o_w, L1_ffn_o_b, L1_ffn_rel_table, L1_ffn_ff_gate_w, L1_ffn_ff_w1, L1_ffn_ff_b1, L1_ffn_ff_w2, L1_ffn_ff_b2)
    return x

_drawn_inputs = setup_inputs


def setup_inputs(seed=0):
    import zlib

    import numpy as np

    out = dict(_drawn_inputs(seed))
    spreads = {'g_ffn': (-1.0, 0.2),
     'L0_ffn_gate_b': (0.0, 0.1),
     'L0_ffn_dp_b1': (0.0, 0.8),
     'L0_ffn_eb1': (0.0, 0.1),
     'L0_ffn_eb2': (0.0, 0.1),
     'L1_xattn_bq': (0.0, 0.1),
     'L1_xattn_bk': (0.0, 2.0),
     'L1_xattn_bv': (0.0, 0.1),
     'L1_xattn_ln_g': (1.0, 0.2),
     'L1_xattn_ln_b': (0.0, 0.1),
     'L1_ffn_ln1_w': (1.0, 0.2),
     'L1_ffn_ln1_b': (0.0, 0.1),
     'L1_ffn_ln2_w': (1.0, 0.2),
     'L1_ffn_ln2_b': (0.0, 0.1),
     'L1_ffn_q_b': (0.0, 0.8),
     'L1_ffn_k_b': (0.0, 2.0),
     'L1_ffn_v_b': (0.0, 0.295),
     'L1_ffn_o_b': (0.0, 0.1),
     'L1_ffn_ff_b1': (0.0, 0.298),
     'L1_ffn_ff_b2': (0.0, 0.1)}
    factors = {'L0_ffn_dp_w1': 6.553,
     'L0_ffn_dp_w2': 6.753,
     'L1_xattn_wk': 3.851,
     'L1_xattn_kan_spline_scaler': 4.5,
     'L1_ffn_q_w': 8.0,
     'L1_ffn_k_w': 8.0,
     'L1_ffn_rel_table': 43.008}
    for name, (base, spread) in spreads.items():
        noise = np.random.default_rng([zlib.crc32(name.encode()), seed]).standard_normal(out[name].shape)
        drawn = base * np.exp(spread * noise) if base else spread * noise
        out[name] = jnp.asarray(drawn.astype(out[name].dtype))
    for name, factor in factors.items():
        out[name] = (out[name] * factor).astype(out[name].dtype)
    return out
```

```python
from contextlib import ExitStack

import numpy as np

import concourse.bass as bass
from concourse import mybir

F32 = mybir.dt.float32
I32 = mybir.dt.int32
U32 = mybir.dt.uint32
ALU = mybir.AluOpType
ACT = mybir.ActivationFunctionType
AX_X = mybir.AxisListType.X

P = 128
B, S, D = 8, 256, 256
T = S // P
C = D // P
STREAMS = 2
PAIRS = B // STREAMS
EPS = 1e-5
BIG = 3.0e38

A_SCALE = 1.0 / 16.0
MASKED = -1.0e10 * A_SCALE

E0, H0 = 4, 512
HC0 = H0 // P
K_THRESHOLDS = [-BIG] + [float(np.log(np.expm1(0.5 + 1.5 * (r - 0.5) / 3))) for r in range(1, E0)]

H1, HD1 = 8, 32
C_SCALE = D ** -0.5
KNOTS = 8
GRID_H = 2.0 / 5

EA, HD = 8, 128
MAXP = 64
REL = 2 * MAXP + 1
PADW = MAXP - 1
RW = REL + 2 * PADW
GROUP = 64
EF, FH = 16, 128
FG = 4

HEADS = 2
STEPS1 = T * H1 // HEADS
STEPSA = T * EA // HEADS

UNIT = 2048
SLOTS = 2
UNITS = E0 + EF // FG
SLOT_USES = UNITS // SLOTS

PACK = {}
_at = 0
for _name, _n in (("wq0", C * 256), ("wk0", C * 256), ("wv0", C * 256), ("dp_w1", C * 128),
                  ("dp_w2", 1), ("gate_w", C * E0), ("wq", C * 256), ("wk", C * 256), ("wv", C * 256),
                  ("base", C * 256), ("q_w", EA * C * HD), ("k_w", C * HD), ("v_w", C * HD),
                  ("o_w", EA * 256), ("rel", REL), ("agate", C * EA), ("fgate", C * EF),
                  ("dp_b1", 1), ("eb1", E0 * HC0), ("bk", C), ("ln_g", C), ("ln_b", C),
                  ("ln1_w", C), ("ln1_b", C), ("ln2_w", C), ("ln2_b", C), ("q_b", EA), ("k_b", 1),
                  ("ff_b1", EF)):
    PACK[_name] = (_at, _n)
    _at += _n
NPACK = _at
NRAW0 = 2 * C * 256

ROWS = {}
_at = 0
for _name, _n in (("bq", 256), ("bv", 256), ("v_b", HD), ("gate_b", E0), ("dp_b2", 1), ("g", 4)):
    ROWS[_name] = (_at, _n)
    _at += _n
NROWS = _at

CHAIN = {"dve": 264}

LN_A, LN_B, LN_C, LN_KAN, LN_MOA, LN_FF = range(1, 7)


class Signal:

    def __init__(self, sem, per):
        self.sem, self.per = sem, per

    def at(self, i, k):
        return self.sem, i * self.per + k


class StreamSignal:

    def __init__(self, sem, per, burst, stream):
        self.sem, self.per, self.burst, self.stream = sem, per, burst, stream

    def at(self, i, k):
        steps, within = divmod(k - 1, self.burst)
        return self.sem, i * (STREAMS * self.per) + (steps * STREAMS + self.stream) * self.burst + within + 1


def build_program(nc, x_in, ctx_t, mask, packed, rows, bias_e, bias_o, bias_f, spline_w, spline_s,
                  units, ident_in, out):
    with ExitStack() as ctx:
        def sb(name, shape, dt=F32):
            return ctx.enter_context(nc.sbuf_tensor(name, shape, dt))

        def sem(name):
            return ctx.enter_context(nc.semaphore(name))

        def signal(name, per, burst=1):
            one = sem(name)
            return [StreamSignal(one, per, burst, s) for s in range(STREAMS)]

        def dma_signal(name, per):
            return [Signal(sem(f"{name}_{s}"), per) for s in range(STREAMS)]

        W = sb("resident", [P, NPACK - NRAW0])
        G0 = sb("g0", [P, C, 256])
        SW = sb("spline_weights", [P, C, KNOTS, 256])
        SLOT = [sb(f"unit_slot{k}", [P, UNIT]) for k in range(SLOTS)]
        ROW = sb("bias_rows", [P, NROWS])
        BE = sb("expert_bias", [E0, 256])
        BO = sb("head_bias", [EA, 256])
        BF = sb("ff_bias", [EF, 256])
        ident = sb("ident", [P, P])
        iota_f = sb("iota_f", [P, EF])
        iota_u = sb("iota_u", [P, EF], I32)
        TG = sb("tanh_g", [P, 4])
        spare = sb("spare", [1, 2])
        minus_half = sb("minus_half", [P, T])
        pool_spare = sb("pool_spare", [1, 2])
        thresholds = sb("thresholds", [P, E0])
        knot_bias = sb("knot_bias", [P, KNOTS])
        qb_scaled = sb("qb_scaled", [P, EA])

        def w(name):
            a, n = PACK[name]
            return W[:, a - NRAW0:a - NRAW0 + n]

        def row(name):
            a, n = ROWS[name]
            return ROW[:, a:a + n]

        wv0 = w("wv0").rearrange("p (c o) -> p c o", c=C)
        dp_w1 = w("dp_w1").rearrange("p (c o) -> p c o", c=C)
        gate_w = w("gate_w").rearrange("p (c o) -> p c o", c=C)
        wq = w("wq").rearrange("p (c o) -> p c o", c=C)
        wk = w("wk").rearrange("p (c o) -> p c o", c=C)
        wv = w("wv").rearrange("p (c o) -> p c o", c=C)
        base = w("base").rearrange("p (c o) -> p c o", c=C)
        q_w = w("q_w").rearrange("p (e c h) -> p e c h", e=EA, c=C)
        k_w = w("k_w").rearrange("p (c h) -> p c h", c=C)
        v_w = w("v_w").rearrange("p (c h) -> p c h", c=C)
        o_w = w("o_w").rearrange("p (e o) -> p e o", e=EA)
        agate = w("agate").rearrange("p (c e) -> p c e", c=C)
        fgate = w("fgate").rearrange("p (c e) -> p c e", c=C)

        def each(name, shape, dt=F32):
            return [sb(f"{name}{s}", shape, dt) for s in range(STREAMS)]

        XIN = each("x_loaded", [P, T, 256])
        CT = each("ctx_columns", [P, C, 256])
        MASK = each("mask", [P, T, 256], I32)
        X = each("x", [P, T, 256])
        XN = each("normed_rows", [P, T, 256])
        XT = each("normed_columns", [P, C, 256])
        QT = each("q_columns", [P, C, 256])
        QR = each("q_rows", [P, T, 256])
        KT = each("k_columns", [P, C, 256])
        VA = each("v_layer0", [P, T, 256])
        VC = each("v_layer1", [P, T, 256])
        BIGB = each("scratch", [P, 5, 2048])
        st = each("bn_stats", [P, T, 6])
        mv = each("mean_var", [P, T, 2])
        rstd = each("rstd", [P, T])
        nmax = each("neg_max", [P, T * EA])
        sums = each("exp_sums", [P, T * EA])
        fac = each("row_factors", [P, T * EA])
        LG = each("logits", [P, T, EF])
        top = each("top8", [P, T, 8])
        topi = each("top8_index", [P, T, 8], U32)
        topf = each("top8_index_f", [P, T, 8])
        gw = each("top_weights", [P, T, E0])
        gs = each("top_sum", [P, T])
        gsel = each("gate_select", [P, T, EF * E0])
        gates = each("gates", [P, T, EF])
        zk = each("k_score", [P, T])
        gT = each("gates_columns", [EF, T, P])

        PA = [BIGB[s][:, 0, 0:512].rearrange("p (t k) -> p t k", t=T) for s in range(2)]
        PTA = [BIGB[s][:, 0, 512:1024].rearrange("p (c q) -> p c q", c=C) for s in range(2)]
        NM = [BIGB[s][:, 0, 1024:1536].rearrange("p (t k) -> p t k", t=T) for s in range(2)]
        HT = [BIGB[s][:, 1, 0:256] for s in range(2)]
        HID = [[BIGB[s][:, 2, 1024 * k:1024 * (k + 1)].rearrange("p (c q) -> p c q", c=4) for k in range(2)]
               for s in range(2)]
        PC = [[BIGB[s][:, 0, 512 * k:512 * (k + 1)].rearrange("p (h k) -> p h k", h=HEADS) for k in range(2)]
              for s in range(2)]
        PTG = [[BIGB[s][:, 1, 512 * k:512 * (k + 1)].rearrange("p (h c q) -> p h c q", h=HEADS, c=C)
                for k in range(2)] for s in range(2)]
        CTX = [[BIGB[s][:, 2, 256 * k:256 * (k + 1)].rearrange("p (h q) -> p h q", h=HEADS)
                for k in range(2)] for s in range(2)]
        SILU = [BIGB[s][:, 4, 0:512] for s in range(2)]
        SIG = [BIGB[s][:, 4, 512:1024] for s in range(2)]

        def spline_buf(s, q, k):
            return BIGB[s][:, k, 1024 * (q % 2):1024 * (q % 2 + 1)].rearrange("p (b n) -> p b n", b=2)

        RELR = [[BIGB[s][:, 1 + t, 0:EA * RW].rearrange("p (e r) -> p e r", e=EA) for t in range(T)]
                for s in range(2)]
        QD = [BIGB[s][:, 0, :].rearrange("p (e q) -> p e q", e=EA) for s in range(2)]
        BS = [[BIGB[s][:, 3 + t, :].rearrange("p (e k) -> p e k", e=EA) for t in range(T)] for s in range(2)]
        KD = [KT[s][:, 0, :] for s in range(2)]
        VD = [VC[s][:, 0, :].rearrange("p (c h) -> p c h", c=C) for s in range(2)]

        PS = [ctx.enter_context(nc.psum_tensor(f"psum{s}", [P, 4, 512], F32)) for s in range(STREAMS)]

        def tiles(s, bank):
            return PS[s][:, bank, :].rearrange("p (t n) -> p t n", t=2)

        rel_dram = nc.dram_tensor("rel_rows", (STREAMS, T, P, EA * RW), F32, kind="Internal").ap()

        weights_in = sem("weights_in")
        spline_in = sem("spline_in")
        consts_made = sem("consts_made")
        pool_spare_made = sem("pool_spare_made")
        g0_mm = sem("g0_mm")
        g0_ready = sem("g0_ready")
        spline_ready = sem("spline_ready")
        tanh_ready = sem("tanh_ready")
        dve_chain = Signal(sem("dve_chain"), CHAIN["dve"])
        unit_in = [Signal(sem(f"unit_in{k}"), 16 * SLOT_USES) for k in range(SLOTS)]
        unit_used = [Signal(sem(f"unit_used{k}"), SLOT_USES) for k in range(SLOTS)]
        x_loaded = dma_signal("x_loaded", 16)
        ctx_loaded = dma_signal("ctx_loaded", 16)
        mask_loaded = dma_signal("mask_loaded", 16)
        xin_used = signal("xin_used", 1)
        mask_used = signal("mask_used", 1)
        stored = dma_signal("stored", 16)
        out_ready = signal("out_ready", 1)

        moments_ready = signal("moments_ready", 7)
        rstd_ready = signal("rstd_ready", 7)
        xn_ready = signal("xn_ready", 6)
        xT_mm = signal("xT_mm", 6)
        xT_ready = signal("xT_ready", 6)
        va_mm = signal("va_mm", 1)
        va_ready = signal("va_ready", 1)
        kt_mm = signal("kt_mm", 1)
        kt_ready = signal("kt_ready", 1)
        vc_mm = signal("vc_mm", 1)
        vc_ready = signal("vc_ready", 1)
        qa_mm = signal("qa_mm", 1)
        qa_ready = signal("qa_ready", 1)
        sa_mm = signal("sa_mm", 1)
        nmax_a = signal("nmax_a", 1)
        exp_a = signal("exp_a", 1)
        pta_mm = signal("pta_mm", 1)
        pta_ready = signal("pta_ready", 1)
        pva_mm = signal("pva_mm", 1)
        dp_mm = signal("dp_mm", 1)
        dp_ready = signal("dp_ready", 1)
        logits_mm = signal("logits_mm", 3)
        z_mm = signal("z_mm", 1)
        top_ready = signal("top_ready", 3)
        top_exp = signal("top_exp", 3)
        gates_ready = signal("gates_ready", 3)
        gT_mm = signal("gT_mm", 3)
        gT_ready = signal("gT_ready", 3)
        bias_mm = signal("bias_mm", 3)
        bias_added = signal("bias_added", 3)
        up_mm = signal("up_mm", E0)
        hid_ready = signal("hid_ready", E0)
        down_mm = signal("down_mm", E0)
        down_added = signal("down_added", E0)
        qr_mm = signal("qr_mm", 1)
        qr_ready = signal("qr_ready", 1)
        qt_mm = signal("qt_mm", 1)
        qt_ready = signal("qt_ready", 1)
        sc_mm = signal("sc_mm", STEPS1)
        sc_max = signal("sc_max", STEPS1)
        sc_exp = signal("sc_exp", STEPS1)
        pt_mm = signal("pt_mm", STEPS1)
        pt_ready = signal("pt_ready", STEPS1)
        pv_mm = signal("pv_mm", STEPS1)
        silu_ready = signal("silu_ready", 1)
        tanh_half = signal("tanh_half", 1)
        distance = signal("distance", 4)
        clipped = signal("clipped", 4)
        squares = signal("squares", 4)
        far_cube = signal("far_cube", 4)
        spline_made = signal("spline_made", 4)
        spline_mm = signal("spline_mm", 4)
        kv_mm = signal("kv_mm", 1)
        kd_ready = signal("kd_ready", 1)
        vd_ready = signal("vd_ready", 1)
        qd_mm = signal("qd_mm", 2)
        qd_ready = signal("qd_ready", 2)
        rel_mm = signal("rel_mm", T)
        rel_band = signal("rel_band", T)
        rel_padded = signal("rel_padded", T)
        rel_half = signal("rel_half", T)
        rel_filled = signal("rel_filled", T)
        rel_written = dma_signal("rel_written", 16 * T)
        bias_in = dma_signal("bias_in", 32 * T)
        sd_mm = signal("sd_mm", STEPSA)
        sd_max = signal("sd_max", STEPSA)
        sd_exp = signal("sd_exp", STEPSA)
        pd_ready = signal("pd_ready", STEPSA)
        ptd_mm = signal("ptd_mm", STEPSA)
        ptd_ready = signal("ptd_ready", STEPSA)
        cx_mm = signal("cx_mm", STEPSA)
        cx_ready = signal("cx_ready", STEPSA)
        od_mm = signal("od_mm", T)
        od_added = signal("od_added", T, T)
        fu_mm = signal("fu_mm", EF // FG)
        fh_ready = signal("fh_ready", EF // FG)
        fd_mm = signal("fd_mm", EF, FG)
        fd_added = signal("fd_added", EF, FG)

        raw = BIGB[0][:, 0, 0:NRAW0].rearrange("p (w c o) -> p w c o", w=2, c=C)
        scaler = BIGB[1][:, 0, 0:C * 256].rearrange("p (c o) -> p c o", c=C)

        def window(g):
            return max(0, g * GROUP - MAXP), min(S, (g + 1) * GROUP + MAXP)

        block = ctx.enter_context(nc.Block())

        @block.sync
        def _(sp):
            def load_inputs(n, s):
                sp.dma_start(XIN[s][:, :, :], x_in[n].rearrange("(t p) d -> p t d", p=P)).then_inc(x_loaded[s].sem, 16)
                sp.dma_start(CT[s][:, :, :], ctx_t[n].rearrange("(c p) t -> p c t", p=P)).then_inc(ctx_loaded[s].sem, 16)
                sp.dma_start(MASK[s][:, :, :], mask[n].rearrange("(t p) k -> p t k", p=P)).then_inc(mask_loaded[s].sem, 16)

            def load_unit(i, u):
                k = u % SLOTS
                if u >= SLOTS:
                    sp.wait_ge(*unit_used[k].at(i, u // SLOTS))
                sp.dma_start(SLOT[k][:, :], units[u]).then_inc(unit_in[k].sem, 16)

            def next_units(i):
                for k in range(SLOTS):
                    sp.wait_ge(*unit_used[k].at(i, SLOT_USES))
                    sp.dma_start(SLOT[k][:, :], units[k]).then_inc(unit_in[k].sem, 16)

            def write_rel(i, s, t):
                sp.wait_ge(*rel_padded[s].at(i, t + 1))
                sp.dma_start(rel_dram[s, t], RELR[s][t].rearrange("p e r -> p (e r)")).then_inc(rel_written[s].sem, 16)

            def read_rel(i, s, t):
                sp.wait_ge(*rel_written[s].at(i, 16 * (t + 1)))
                for j in range(2):
                    g = 2 * t + j
                    lo, hi = window(g)
                    first = rel_dram[s, t]
                    off = first.offset + j * GROUP * EA * RW + lo - g * GROUP + RW // 2
                    src = bass.AP(first.tensor, off, [[EA * RW - 1, GROUP], [RW, EA], [1, hi - lo]])
                    sp.dma_start(BS[s][t][j * GROUP:(j + 1) * GROUP, :, lo:hi], src).then_inc(bias_in[s].sem, 16)

            def rel_and_units(i):
                for u in range(SLOTS, UNITS - SLOTS):
                    load_unit(i, u)
                order = [(s, t) for t in range(T) for s in range(STREAMS)]
                for k in range(len(order) + 1):
                    if k < len(order):
                        write_rel(i, *order[k])
                    if k:
                        read_rel(i, *order[k - 1])

            def store(i, n, s):
                sp.wait_ge(*out_ready[s].at(i, 1))
                sp.dma_start(out[n].rearrange("(t p) d -> p t d", p=P), VA[s][:, :, :]).then_inc(stored[s].sem, 16)

            sp.dma_start(raw, packed[:, 0:NRAW0].rearrange("p (w c o) -> p w c o", w=2, c=C)).then_inc(weights_in, 16)
            for s in range(STREAMS):
                load_inputs(s, s)
                sp.sem_inc(stored[s].sem, 16)
            sp.dma_start(W[:, :], packed[:, NRAW0:NPACK]).then_inc(weights_in, 16)
            sp.dma_start(ident[:, :], ident_in).then_inc(weights_in, 16)
            sp.dma_start(ROW[:, :], rows.partition_broadcast(P)).then_inc(weights_in, 16)
            sp.dma_start(BE[:, :], bias_e).then_inc(weights_in, 16)
            sp.dma_start(BO[:, :], bias_o).then_inc(weights_in, 16)
            sp.dma_start(BF[:, :], bias_f).then_inc(weights_in, 16)
            for u in range(SLOTS):
                load_unit(0, u)
            sp.dma_start(scaler, spline_s.rearrange("p (c o) -> p c o", c=C)).then_inc(spline_in, 16)
            sp.dma_start(SW[:, :, :, :], spline_w.rearrange("p (c b o) -> p c b o", c=C, b=KNOTS)).then_inc(spline_in, 16)

            with sp.Fori(0, PAIRS - 1) as i:
                rel_and_units(i)
                for s in range(STREAMS):
                    n = 2 * i + (STREAMS + s)
                    sp.wait_ge(*xin_used[s].at(i, 1))
                    sp.wait_ge(*mask_used[s].at(i, 1))
                    sp.wait_ge(*vc_mm[s].at(i, 1))
                    load_inputs(n, s)
                for u in range(UNITS - SLOTS, UNITS):
                    load_unit(i, u)
                for s in range(STREAMS):
                    store(i, 2 * i + s, s)
                next_units(i)
            last = PAIRS - 1
            rel_and_units(last)
            for u in range(UNITS - SLOTS, UNITS):
                load_unit(last, u)
            for s in range(STREAMS):
                store(last, 2 * last + s, s)
            for s in range(STREAMS):
                sp.wait_ge(*stored[s].at(PAIRS, 16))

        NWEIGHT_DMAS = 7

        @block.gpsimd
        def _(pool):
            nc.gpsimd.memset(pool_spare[:, :], 0.0).then_inc(pool_spare_made, 1)
            nc.gpsimd.memset(minus_half[:, :], -0.5).then_inc(pool_spare_made, 1)
            pool.wait_ge(pool_spare_made, 2)
            nc.gpsimd.iota(iota_u[:, :], pattern=[[1, EF]], base=0, channel_multiplier=0).then_inc(consts_made, 1)
            with pool.Fori(0, PAIRS) as i:
                def apart():
                    nc.gpsimd.tensor_tensor(pool_spare[:, 0:1], pool_spare[:, 1:2], pool_spare[:, 1:2], ALU.mult)

                def spline_far(s, q):
                    pool.wait_ge(*squares[s].at(i, q + 1))
                    pool.wait_ge(*clipped[s].at(i, q + 1))
                    b = spline_buf(s, q, 1)
                    nc.gpsimd.tensor_tensor(b, b, spline_buf(s, q, 2), ALU.mult).then_inc(far_cube[s].sem, 1)

                def rel_edges(s, t):
                    pool.wait_ge(*rel_band[s].at(i, t + 1))
                    r = RELR[s][t]
                    apart()
                    nc.gpsimd.tensor_copy(r[:, :, 0:PADW], r[:, :, PADW:PADW + 1].broadcast_to((P, EA, PADW)))
                    nc.gpsimd.tensor_copy(r[:, :, RW - PADW:RW],
                                          r[:, :, RW - PADW - 1:RW - PADW].broadcast_to((P, EA, PADW))
                                          ).then_inc(rel_padded[s].sem, 1)
                    for j in range(2):
                        if j == 0:
                            pool.wait_ge(*rel_padded[s].at(i, t + 1))
                        else:
                            pool.wait_ge(*rel_half[s].at(i, t + 1))
                        apart()
                        lo, hi = window(2 * t + j)
                        a, b = j * GROUP, (j + 1) * GROUP
                        zlo, zhi, edge = (0, lo, PADW) if lo else (hi, S, RW - PADW - 1)
                        ins = nc.gpsimd.tensor_copy(BS[s][t][a:b, :, zlo:zhi],
                                                    r[a:b, :, edge:edge + 1].broadcast_to((GROUP, EA, zhi - zlo)))
                        ins.then_inc((rel_filled if j else rel_half)[s].sem, 1)
                    pool.wait_ge(*rel_filled[s].at(i, t + 1))

                def power(k, s):
                    pool.wait_ge(*moments_ready[s].at(i, k))
                    nc.gpsimd.tensor_tensor(rstd[s][:, :], rstd[s][:, :], minus_half[:, :], ALU.pow
                                            ).then_inc(rstd_ready[s].sem, 1)

                for k in (1, 2, 3, 4):
                    for s in range(STREAMS):
                        power(k, s)
                for q in range(KNOTS // 2):
                    for s in range(STREAMS):
                        spline_far(s, q)
                for k in (5, 6):
                    for s in range(STREAMS):
                        power(k, s)
                for t in range(T):
                    for s in range(STREAMS):
                        rel_edges(s, t)
                for s in range(STREAMS):
                    power(7, s)

        @block.tensor
        def _(pe):
            def mm(o, a, b, start=True, stop=True):
                return pe.matmul(o, a, b, start=start, stop=stop)

            def rows_of(o, cols, weights, n):
                for t in range(T):
                    for c in range(C):
                        last = mm(o[:, t, 0:n], cols[:, c, t * P:(t + 1) * P], weights[:, c, :], c == 0, c == C - 1)
                return last

            pe.wait_ge(weights_in, 16 * NWEIGHT_DMAS)
            for a in range(C):
                for c in range(C):
                    last = mm(tiles(0, 0)[:, a, :], raw[:, 0, c, a * P:(a + 1) * P], raw[:, 1, c, :], c == 0, c == C - 1)
            last.then_inc(g0_mm, 1)
            pe.wait_ge(g0_ready, 1)

            with pe.Fori(0, PAIRS) as i:
                def turn(s, k):
                    pe.wait_ge(*xn_ready[s].at(i, k))
                    for c in range(C):
                        for t in range(T):
                            last = pe.transpose(tiles(s, 0)[:, c, t * P:(t + 1) * P],
                                                XN[s][:, t, c * P:(c + 1) * P], ident[:, :])
                    last.then_inc(xT_mm[s].sem, 1)

                def a_first(s):
                    pe.wait_ge(*ctx_loaded[s].at(i, 16))
                    rows_of(tiles(s, 3), CT[s], wv0, 256).then_inc(va_mm[s].sem, 1)
                    turn(s, LN_A)

                def a_query(s):
                    pe.wait_ge(*xT_ready[s].at(i, LN_A))
                    for a in range(C):
                        for c in range(C):
                            last = mm(tiles(s, 1)[:, a, :], G0[:, c, a * P:(a + 1) * P], XT[s][:, c, :], c == 0, c == C - 1)
                    last.then_inc(qa_mm[s].sem, 1)
                    for a in range(C):
                        for c in range(C):
                            last = mm(tiles(s, 2)[:, a, :], wk[:, c, a * P:(a + 1) * P], CT[s][:, c, :], c == 0, c == C - 1)
                    last.then_inc(kt_mm[s].sem, 1)

                def a_scores(s):
                    pe.wait_ge(*qa_ready[s].at(i, 1))
                    rows_of(tiles(s, 0), QT[s], CT[s], 256).then_inc(sa_mm[s].sem, 1)

                def a_turn(s):
                    pe.wait_ge(*va_ready[s].at(i, 1))
                    rows_of(tiles(s, 3), CT[s], wv, 256).then_inc(vc_mm[s].sem, 1)
                    pe.wait_ge(*exp_a[s].at(i, 1))
                    for c in range(C):
                        for t in range(T):
                            last = pe.transpose(tiles(s, 1)[:, c, t * P:(t + 1) * P],
                                                PA[s][:, t, c * P:(c + 1) * P], ident[:, :])
                    last.then_inc(pta_mm[s].sem, 1)

                def a_values(s):
                    pe.wait_ge(*kt_ready[s].at(i, 1))
                    pe.wait_ge(*pta_ready[s].at(i, 1))
                    rows_of(tiles(s, 2), PTA[s], VA[s], 256).then_inc(pva_mm[s].sem, 1)

                def b_turn(s):
                    turn(s, LN_B)

                def b_gate(s):
                    pe.wait_ge(*xT_ready[s].at(i, LN_B))
                    for c in range(C):
                        last = mm(tiles(s, 1)[:, 0, :], dp_w1[:, c, :], XT[s][:, c, :], c == 0, c == C - 1)
                    last.then_inc(dp_mm[s].sem, 1)
                    pe.wait_ge(*vc_ready[s].at(i, 1))
                    rows_of(tiles(s, 3), XT[s], gate_w, E0).then_inc(logits_mm[s].sem, 1)

                def gate_columns(s, k, n):
                    pe.wait_ge(*gates_ready[s].at(i, k))
                    for t in range(T):
                        last = mm(PS[s][0:n, 3, t * P:(t + 1) * P], gates[s][:, t, 0:n], ident[:, :])
                    last.then_inc(gT_mm[s].sem, 1)

                def gate_bias(s, k, n, weights):
                    pe.wait_ge(*gT_ready[s].at(i, k))
                    for t in range(T):
                        last = mm(tiles(s, 3)[:, t, :], gT[s][0:n, t, :], weights[:, :])
                    last.then_inc(bias_mm[s].sem, 1)

                def b_expert(s, e):
                    if e < E0:
                        k = e % SLOTS
                        pe.wait_ge(*unit_in[k].at(i, 16 * (e // SLOTS + 1)))
                        if e:
                            pe.wait_ge(*hid_ready[s].at(i, e))
                        else:
                            pe.wait_ge(*dp_ready[s].at(i, 1))
                        w1 = SLOT[k][:, 0:1024].rearrange("p (c h) -> p c h", c=C)
                        for h in range(HC0):
                            for c in range(C):
                                last = mm(PS[s][:, h // 2, (h % 2) * 256:(h % 2 + 1) * 256],
                                          w1[:, c, h * P:(h + 1) * P], XT[s][:, c, :], c == 0, c == C - 1)
                        last.then_inc(up_mm[s].sem, 1)
                    if e == 0:
                        pe.wait_ge(*top_ready[s].at(i, 1))
                        for t in range(T):
                            last = mm(tiles(s, 3)[:, t, E0:E0 + 1], HT[s][:, t * P:(t + 1) * P], w("dp_w2"))
                        last.then_inc(z_mm[s].sem, 1)
                    if e == 2:
                        gate_columns(s, 1, E0)
                    if e == 3:
                        gate_bias(s, 1, E0, BE)
                    if e:
                        k = (e - 1) % SLOTS
                        pe.wait_ge(*hid_ready[s].at(i, e))
                        if e > 1:
                            pe.wait_ge(*down_added[s].at(i, e - 1))
                        w2 = SLOT[k][:, 1024:2048].rearrange("p (c o) -> p c o", c=HC0)
                        for t in range(T):
                            for c in range(HC0):
                                last = mm(tiles(s, 2)[:, t, :], HID[s][(e - 1) % 2][:, c, t * P:(t + 1) * P],
                                          w2[:, c, :], c == 0, c == HC0 - 1)
                        last.then_inc(down_mm[s].sem, 1)
                        if s == STREAMS - 1:
                            pe.wait_ge(*down_mm[s].at(i, e))
                            pe.sem_inc(unit_used[k].sem, 1)

                def c_turn(s):
                    turn(s, LN_C)

                def c_query(s):
                    pe.wait_ge(*xT_ready[s].at(i, LN_C))
                    rows_of(tiles(s, 1), XT[s], wq, 256).then_inc(qr_mm[s].sem, 1)

                def c_query_turn(s):
                    pe.wait_ge(*qr_ready[s].at(i, 1))
                    for c in range(C):
                        for t in range(T):
                            last = pe.transpose(tiles(s, 0)[:, c, t * P:(t + 1) * P],
                                                QR[s][:, t, c * P:(c + 1) * P], ident[:, :])
                    last.then_inc(qt_mm[s].sem, 1)

                def c_step(s, j):
                    per_tile = H1 // HEADS
                    if j < STEPS1:
                        t, h0 = j // per_tile, (j % per_tile) * HEADS
                        if j:
                            pe.wait_ge(*sc_exp[s].at(i, j))
                        else:
                            pe.wait_ge(*qt_ready[s].at(i, 1))
                        for h in range(h0, h0 + HEADS):
                            r = (h % 4) * HD1
                            last = mm(PS[s][:, h - h0, 0:256], QT[s][r:r + HD1, h // 4, t * P:(t + 1) * P],
                                      KT[s][r:r + HD1, h // 4, :])
                        last.then_inc(sc_mm[s].sem, 1)
                    if 1 <= j <= STEPS1:
                        k = j - 1
                        pe.wait_ge(*sc_exp[s].at(i, k + 1))
                        if k:
                            pe.wait_ge(*pt_ready[s].at(i, k))
                        for h in range(HEADS):
                            for c in range(C):
                                a = (h * C + c) * P
                                last = pe.transpose(PS[s][:, 2, a:a + P], PC[s][k % 2][:, h, c * P:(c + 1) * P], ident[:, :])
                        last.then_inc(pt_mm[s].sem, 1)
                    if j >= 2:
                        k = j - 2
                        t, h0 = k // per_tile, (k % per_tile) * HEADS
                        pe.wait_ge(*pt_ready[s].at(i, k + 1))
                        for h in range(HEADS):
                            a = (h0 + h) * HD1
                            for c in range(C):
                                last = mm(tiles(s, 3)[:, t, a:a + HD1], PTG[s][k % 2][:, h, c, :],
                                          VC[s][:, c, a:a + HD1], c == 0, c == C - 1)
                        last.then_inc(pv_mm[s].sem, 1)

                def kan_turn(s):
                    turn(s, LN_KAN)

                def kan(s, q):
                    if q == 0:
                        pe.wait_ge(*silu_ready[s].at(i, 1))
                        for t in range(T):
                            for c in range(C):
                                a = c * 256 + t * P
                                mm(PS[s][:, 1 + t, 0:256], SILU[s][:, a:a + P], base[:, c, :], c == 0, False)
                    pe.wait_ge(*spline_made[s].at(i, q + 1))
                    for t in range(T):
                        for b in range(2):
                            for c in range(C):
                                a = c * 256 + t * P
                                last = mm(PS[s][:, 1 + t, 0:256], spline_buf(s, q, 3)[:, b, a:a + P],
                                          SW[:, c, 2 * q + b, :], False, q == 3 and b == 1 and c == C - 1)
                    last.then_inc(spline_mm[s].sem, 1)

                def d_turn(s):
                    turn(s, LN_MOA)

                def d_kv(s):
                    pe.wait_ge(*xT_ready[s].at(i, LN_MOA))
                    for c in range(C):
                        mm(PS[s][:, 3, 0:256], k_w[:, c, :], XT[s][:, c, :], c == 0, c == C - 1)
                    for t in range(T):
                        for c in range(C):
                            last = mm(PS[s][:, 3, 256 + t * P:256 + (t + 1) * P], XT[s][:, c, t * P:(t + 1) * P],
                                      v_w[:, c, :], c == 0, c == C - 1)
                    last.then_inc(kv_mm[s].sem, 1)
                    rows_of(tiles(s, 2), XT[s], agate, EA).then_inc(logits_mm[s].sem, 1)

                def d_queries(s, half):
                    if half:
                        pe.wait_ge(*qd_ready[s].at(i, half))
                    for e in range(4):
                        for c in range(C):
                            last = mm(PS[s][:, e // 2, (e % 2) * 256:(e % 2 + 1) * 256],
                                      q_w[:, half * 4 + e, c, :], XT[s][:, c, :], c == 0, c == C - 1)
                    last.then_inc(qd_mm[s].sem, 1)

                def d_rel(s, t):
                    if t == 0:
                        pe.wait_ge(*qd_ready[s].at(i, 2))
                        pe.wait_ge(*kd_ready[s].at(i, 1))
                        pe.wait_ge(*vd_ready[s].at(i, 1))
                        pe.wait_ge(*top_ready[s].at(i, 2))
                    else:
                        pe.wait_ge(*rel_band[s].at(i, t))
                    for e in range(EA):
                        last = mm(PS[s][:, e // 2, (e % 2) * 256:(e % 2) * 256 + REL],
                                  QD[s][:, e, t * P:(t + 1) * P], w("rel"))
                    last.then_inc(rel_mm[s].sem, 1)

                def d_step(s, j):
                    per_tile = EA // HEADS
                    if j < STEPSA:
                        t, e0 = j // per_tile, (j % per_tile) * HEADS
                        if j:
                            pe.wait_ge(*sd_max[s].at(i, j))
                        else:
                            pe.wait_ge(*rel_band[s].at(i, T))
                        for h in range(HEADS):
                            last = mm(tiles(s, 0)[:, h, :], QD[s][:, e0 + h, t * P:(t + 1) * P], KD[s])
                        last.then_inc(sd_mm[s].sem, 1)
                    if 1 <= j <= STEPSA:
                        k = j - 1
                        t, e0 = k // per_tile, (k % per_tile) * HEADS
                        pe.wait_ge(*pd_ready[s].at(i, k + 1))
                        if k:
                            pe.wait_ge(*ptd_ready[s].at(i, k))
                        for h in range(HEADS):
                            for c in range(C):
                                a = (h * C + c) * P
                                last = pe.transpose(PS[s][:, 1, a:a + P], BS[s][t][:, e0 + h, c * P:(c + 1) * P], ident[:, :])
                        last.then_inc(ptd_mm[s].sem, 1)
                    if 2 <= j <= STEPSA + 1:
                        k = j - 2
                        pe.wait_ge(*ptd_ready[s].at(i, k + 1))
                        if k:
                            pe.wait_ge(*cx_ready[s].at(i, k))
                        for h in range(HEADS):
                            for c in range(C):
                                last = mm(PS[s][:, 2, h * P:(h + 1) * P], VD[s][:, c, :], PTG[s][k % 2][:, h, c, :],
                                          c == 0, c == C - 1)
                        last.then_inc(cx_mm[s].sem, 1)
                    if j >= 3:
                        k = j - 3
                        t, e0 = k // per_tile, (k % per_tile) * HEADS
                        pe.wait_ge(*cx_ready[s].at(i, k + 1))
                        for h in range(HEADS):
                            last = mm(tiles(s, 3)[:, t, :], CTX[s][k % 2][:, h, :], o_w[:, e0 + h, :],
                                      e0 + h == 0, e0 + h == EA - 1)
                        if k % per_tile == per_tile - 1:
                            last.then_inc(od_mm[s].sem, 1)

                def d_gate_columns(s):
                    pe.wait_ge(*od_added[s].at(i, T))
                    gate_columns(s, 2, EA)

                def d_gate_bias(s):
                    gate_bias(s, 2, EA, BO)

                def f_turn(s):
                    turn(s, LN_FF)

                def f_gate(s):
                    pe.wait_ge(*xT_ready[s].at(i, LN_FF))
                    rows_of(tiles(s, 3), XT[s], fgate, EF).then_inc(logits_mm[s].sem, 1)

                def f_gate_columns(s):
                    gate_columns(s, 3, EF)

                def f_gate_bias(s):
                    gate_bias(s, 3, EF, BF)

                def f_experts(s, g):
                    if g < EF // FG:
                        u = E0 + g
                        pe.wait_ge(*unit_in[u % SLOTS].at(i, 16 * (u // SLOTS + 1)))
                        if g:
                            pe.wait_ge(*fh_ready[s].at(i, g))
                        w1 = SLOT[u % SLOTS][:, 0:1024].rearrange("p (e c h) -> p e c h", e=FG, c=C)
                        for e in range(FG):
                            for c in range(C):
                                last = mm(PS[s][:, e // 2, (e % 2) * 256:(e % 2 + 1) * 256],
                                          w1[:, e, c, :], XT[s][:, c, :], c == 0, c == C - 1)
                        last.then_inc(fu_mm[s].sem, 1)
                    if g == 0:
                        f_gate_columns(s)
                    if g == 1:
                        f_gate_bias(s)
                        pe.wait_ge(*bias_added[s].at(i, 3))
                    if g:
                        u = E0 + g - 1
                        pe.wait_ge(*fh_ready[s].at(i, g))
                        w2 = SLOT[u % SLOTS][:, 1024:2048].rearrange("p (e o) -> p e o", e=FG)
                        for e in range(FG):
                            n = (g - 1) * FG + e
                            if n >= 2:
                                pe.wait_ge(*fd_added[s].at(i, n - 1))
                            for t in range(T):
                                last = mm(tiles(s, 2 + n % 2)[:, t, :], HID[s][(g - 1) % 2][:, e, t * P:(t + 1) * P],
                                          w2[:, e, :])
                            last.then_inc(fd_mm[s].sem, 1)
                        if s == STREAMS - 1:
                            pe.wait_ge(*fd_mm[s].at(i, g * FG))
                            pe.sem_inc(unit_used[u % SLOTS].sem, 1)

                def both(step, *args):
                    for s in range(STREAMS):
                        step(s, *args)

                both(a_first)
                both(a_query)
                both(a_scores)
                both(a_turn)
                both(a_values)
                both(b_turn)
                both(b_gate)
                for e in range(E0 + 1):
                    both(b_expert, e)
                both(c_turn)
                both(c_query)
                both(c_query_turn)
                for j in range(STEPS1 + 2):
                    both(c_step, j)
                both(kan_turn)
                for q in range(KNOTS // 2):
                    both(kan, q)
                both(d_turn)
                both(d_kv)
                for half in range(2):
                    both(d_queries, half)
                for t in range(T):
                    both(d_rel, t)
                for j in range(STEPSA + 3):
                    both(d_step, j)
                both(d_gate_columns)
                both(d_gate_bias)
                both(f_turn)
                both(f_gate)
                for g in range(EF // FG + 1):
                    both(f_experts, g)

        @block.scalar
        def _(act):
            chained = [0]

            act.wait_ge(weights_in, 16 * NWEIGHT_DMAS)
            nc.scalar.activation(TG[:, :], row("g"), ACT.Tanh).then_inc(tanh_ready, 1)
            nc.scalar.activation(qb_scaled[:, :], w("q_b"), ACT.Copy, scale=HD ** -0.5).then_inc(tanh_ready, 1)
            act.wait_ge(g0_mm, 1)
            nc.scalar.activation(G0[:, :, :], tiles(0, 0), ACT.Copy).then_inc(g0_ready, 1)
            act.wait_ge(tanh_ready, 2)
            act.wait_ge(consts_made, CONSTS)

            with act.Fori(0, PAIRS) as i:
                def columns(s, k, scale=None, bias=None):
                    act.wait_ge(*xT_mm[s].at(i, k))
                    if scale is None:
                        last = nc.scalar.activation(XT[s][:, :, :], tiles(s, 0), ACT.Copy)
                    else:
                        for c in range(C):
                            last = nc.scalar.activation(XT[s][:, c, :], tiles(s, 0)[:, c, :], ACT.Identity,
                                                        scale=w(scale)[:, c:c + 1], bias=w(bias)[:, c:c + 1])
                    last.then_inc(xT_ready[s].sem, 1)

                def a_first(s):
                    columns(s, LN_A)
                    act.wait_ge(*va_mm[s].at(i, 1))
                    act.wait_ge(*stored[s].at(i, 16))
                    nc.scalar.activation(VA[s][:, :, :], tiles(s, 3), ACT.Copy).then_inc(va_ready[s].sem, 1)

                def a_query(s):
                    act.wait_ge(*qa_mm[s].at(i, 1))
                    nc.scalar.activation(QT[s][:, :, :], tiles(s, 1), ACT.Copy, scale=A_SCALE).then_inc(qa_ready[s].sem, 1)
                    act.wait_ge(*kt_mm[s].at(i, 1))
                    for c in range(C):
                        last = nc.scalar.activation(KT[s][:, c, :], tiles(s, 2)[:, c, :], ACT.Identity,
                                                    bias=w("bk")[:, c:c + 1])
                    last.then_inc(kt_ready[s].sem, 1)

                def a_scores(s):
                    act.wait_ge(*nmax_a[s].at(i, 1))
                    for t in range(T):
                        last = nc.scalar.activation(PA[s][:, t, :], PA[s][:, t, :], ACT.Exp,
                                                    bias=nmax[s][:, t:t + 1], accum_out=sums[s][:, t:t + 1])
                    last.then_inc(exp_a[s].sem, 1)

                def a_turn(s):
                    act.wait_ge(*pta_mm[s].at(i, 1))
                    nc.scalar.activation(PTA[s], tiles(s, 1), ACT.Copy).then_inc(pta_ready[s].sem, 1)

                def b_turn(s):
                    columns(s, LN_B)

                def b_gate(s):
                    act.wait_ge(*dp_mm[s].at(i, 1))
                    nc.scalar.activation(HT[s], tiles(s, 1)[:, 0, :], ACT.Relu, bias=w("dp_b1")).then_inc(dp_ready[s].sem, 1)

                def top_weights(s, k, n):
                    act.wait_ge(*top_ready[s].at(i, k))
                    nc.scalar.activation(gw[s][:, :, 0:n], gw[s][:, :, 0:n], ACT.Exp).then_inc(top_exp[s].sem, 1)

                def b_expert(s, e):
                    if e < E0:
                        act.wait_ge(*up_mm[s].at(i, e + 1))
                        if e >= 2:
                            act.wait_ge(*down_mm[s].at(i, e - 1))
                        for h in range(HC0):
                            last = nc.scalar.activation(HID[s][e % 2][:, h, :], PS[s][:, h // 2, (h % 2) * 256:(h % 2 + 1) * 256],
                                                        ACT.Relu, bias=w("eb1")[:, e * HC0 + h:e * HC0 + h + 1])
                        last.then_inc(hid_ready[s].sem, 1)
                    if e == 0:
                        top_weights(s, 1, E0)

                def c_turn(s):
                    columns(s, LN_C)

                def c_query_turn(s):
                    act.wait_ge(*qt_mm[s].at(i, 1))
                    nc.scalar.activation(QT[s][:, :, :], tiles(s, 0), ACT.Copy, scale=C_SCALE).then_inc(qt_ready[s].sem, 1)

                def c_step(s, j):
                    if j < STEPS1:
                        act.wait_ge(*sc_max[s].at(i, j + 1))
                        if j >= 2:
                            act.wait_ge(*pt_mm[s].at(i, j - 1))
                        for h in range(HEADS):
                            k = j * HEADS + h
                            last = nc.scalar.activation(PC[s][j % 2][:, h, :], PS[s][:, h, 0:256], ACT.Exp,
                                                        bias=nmax[s][:, k:k + 1], accum_out=sums[s][:, k:k + 1])
                        last.then_inc(sc_exp[s].sem, 1)

                def kan_turn(s):
                    columns(s, LN_KAN, "ln_g", "ln_b")
                    act.wait_ge(*xT_ready[s].at(i, LN_KAN))
                    y = XT[s][:, :, :].rearrange("p c n -> p (c n)")
                    nc.scalar.activation(SIG[s], y, ACT.Tanh, scale=0.5).then_inc(tanh_half[s].sem, 1)
                    kan_distance(s, 0)

                def kan_distance(s, q):
                    if q >= 2:
                        act.wait_ge(*spline_mm[s].at(i, q - 1))
                    y = XT[s][:, :, :].rearrange("p c n -> p (c n)")
                    for b in range(2):
                        n = 2 * q + b
                        last = nc.scalar.activation(spline_buf(s, q, 0)[:, b, :], y, ACT.Abs, scale=1.0 / GRID_H,
                                                    bias=knot_bias[:, n:n + 1])
                    last.then_inc(distance[s].sem, 1)

                def kan(s, q):
                    if q + 1 < KNOTS // 2:
                        kan_distance(s, q + 1)
                    act.wait_ge(*clipped[s].at(i, q + 1))
                    nc.scalar.activation(spline_buf(s, q, 2), spline_buf(s, q, 1), ACT.Square, scale=(1 / 6) ** 0.5)
                    nc.scalar.activation(spline_buf(s, q, 3), spline_buf(s, q, 0), ACT.Square,
                                         scale=(4 / 6) ** 0.5).then_inc(squares[s].sem, 1)

                def d_turn(s):
                    columns(s, LN_MOA, "ln1_w", "ln1_b")

                def d_kv(s):
                    act.wait_ge(*vd_ready[s].at(i, 1))
                    nc.scalar.activation(KD[s], PS[s][:, 3, 0:256], ACT.Identity, bias=w("k_b")).then_inc(kd_ready[s].sem, 1)
                    top_weights(s, 2, 2)

                def d_queries(s, half):
                    act.wait_ge(*qd_mm[s].at(i, half + 1))
                    for e in range(4):
                        n = half * 4 + e
                        last = nc.scalar.activation(QD[s][:, n, :], PS[s][:, e // 2, (e % 2) * 256:(e % 2 + 1) * 256],
                                                    ACT.Identity, scale=HD ** -0.5, bias=qb_scaled[:, n:n + 1])
                    last.then_inc(qd_ready[s].sem, 1)

                def d_step(s, j):
                    per_tile = EA // HEADS
                    if j < STEPSA:
                        t, e0 = j // per_tile, (j % per_tile) * HEADS
                        act.wait_ge(*sd_max[s].at(i, j + 1))
                        for h in range(HEADS):
                            k = j * HEADS + h
                            last = nc.scalar.activation(BS[s][t][:, e0 + h, :], BS[s][t][:, e0 + h, :], ACT.Exp,
                                                        bias=nmax[s][:, k:k + 1], accum_out=sums[s][:, k:k + 1])
                        last.then_inc(sd_exp[s].sem, 1)
                    if 2 <= j <= STEPSA + 1:
                        k = j - 2
                        if k == 0:
                            act.wait_ge(*rel_filled[s].at(i, T))
                            act.wait_ge(*rel_written[s].at(i, 16 * T))
                        act.wait_ge(*cx_mm[s].at(i, k + 1))
                        nc.scalar.activation(CTX[s][k % 2], PS[s][:, 2, 0:256].rearrange("p (h q) -> p h q", h=HEADS),
                                             ACT.Copy).then_inc(cx_ready[s].sem, 1)

                def f_turn(s):
                    columns(s, LN_FF, "ln2_w", "ln2_b")

                def f_experts(s, g):
                    if g == 0:
                        top_weights(s, 3, 2)
                    if g < EF // FG:
                        act.wait_ge(*fu_mm[s].at(i, g + 1))
                        if g >= 2:
                            act.wait_ge(*fd_mm[s].at(i, (g - 1) * FG))
                        for e in range(FG):
                            n = g * FG + e
                            last = nc.scalar.activation(HID[s][g % 2][:, e, :], PS[s][:, e // 2, (e % 2) * 256:(e % 2 + 1) * 256],
                                                        ACT.Relu, bias=w("ff_b1")[:, n:n + 1])
                        last.then_inc(fh_ready[s].sem, 1)

                def both(step, *args):
                    for s in range(STREAMS):
                        step(s, *args)

                both(a_first)
                both(a_query)
                both(a_scores)
                both(a_turn)
                both(b_turn)
                both(b_gate)
                for e in range(E0 + 1):
                    both(b_expert, e)
                both(c_turn)
                both(c_query_turn)
                for j in range(STEPS1 + 2):
                    both(c_step, j)
                both(kan_turn)
                for q in range(KNOTS // 2):
                    both(kan, q)
                both(d_turn)
                both(d_kv)
                for half in range(2):
                    both(d_queries, half)
                for j in range(STEPSA + 3):
                    both(d_step, j)
                both(f_turn)
                for g in range(EF // FG + 1):
                    both(f_experts, g)

        @block.vector
        def _(dve):
            chained = [0]
            rnd = [None]

            def keep(ins):
                chained[0] += 1
                return ins.then_inc(dve_chain.sem, 1)

            def settle():
                dve.wait_ge(*dve_chain.at(rnd[0], chained[0]))

            def apart():
                v.memset(spare[0:1, 0:1], 0.0)

            v = nc.vector
            for k in range(E0):
                v.memset(thresholds[:, k:k + 1], K_THRESHOLDS[k]).then_inc(consts_made, 1)
            for k in range(KNOTS):
                v.memset(knot_bias[:, k:k + 1], 1.0 / GRID_H - (k - 1)).then_inc(consts_made, 1)
            dve.wait_ge(consts_made, CONSTS - 1)
            v.tensor_copy(iota_f[:, :], iota_u[:, :]).then_inc(consts_made, 1)
            dve.wait_ge(consts_made, CONSTS)
            dve.wait_ge(spline_in, 32)
            for c in range(C):
                for b in range(KNOTS):
                    ins = v.tensor_tensor(SW[:, c, b, :], SW[:, c, b, :], scaler[:, c, :], ALU.mult)
            ins.then_inc(spline_ready, 1)
            dve.wait_ge(spline_ready, 1)
            dve.wait_ge(tanh_ready, 2)
            dve.wait_ge(weights_in, 16 * NWEIGHT_DMAS)

            with dve.Fori(0, PAIRS) as i:
                rnd[0] = i
                chained[0] = 0
                normed = [0, 0]

                def layernorm(s, dst, src):
                    settle()
                    apart()
                    for t in range(T):
                        ins = keep(v.bn_stats(st[s][:, t, :], src[:, t, :]))
                    settle()
                    apart()
                    for t in range(T):
                        ins = keep(v.bn_aggr(mv[s][:, t, :], st[s][:, t, :]))
                    settle()
                    v.tensor_scalar(rstd[s][:, :], mv[s][:, :, 1], EPS, None, ALU.add).then_inc(moments_ready[s].sem, 1)
                    normed[s] += 1
                    dve.wait_ge(*rstd_ready[s].at(i, normed[s]))
                    for t in range(T):
                        ins = v.tensor_scalar(dst[:, t, :], src[:, t, :], mv[s][:, t, 0:1], rstd[s][:, t:t + 1],
                                              ALU.subtract, ALU.mult)
                        if t < T - 1:
                            keep(ins)
                    return ins

                def a_norm(s):
                    dve.wait_ge(*x_loaded[s].at(i, 16))
                    layernorm(s, XN[s], XIN[s]).then_inc(xn_ready[s].sem, 1)
                    dve.wait_ge(*mask_loaded[s].at(i, 16))
                    keep(v.tensor_scalar(NM[s], MASK[s][:, :, :], 0.0, BIG, ALU.not_equal, ALU.mult)
                         )
                    settle()
                    v.tensor_scalar(NM[s], NM[s], MASKED, None, ALU.add).then_inc(mask_used[s].sem, 1)

                def a_scores(s):
                    dve.wait_ge(*mask_used[s].at(i, 1))
                    dve.wait_ge(*sa_mm[s].at(i, 1))
                    keep(v.tensor_tensor(PA[s], tiles(s, 0), NM[s], ALU.min))
                    settle()
                    v.tensor_reduce(nmax[s][:, 0:T], PA[s], AX_X, ALU.max, negate=True).then_inc(nmax_a[s].sem, 1)

                def a_turn(s):
                    dve.wait_ge(*vc_mm[s].at(i, 1))
                    for t in range(T):
                        ins = v.tensor_tensor(VC[s][:, t, :], tiles(s, 3)[:, t, :], row("bv"), ALU.add)
                    ins.then_inc(vc_ready[s].sem, 1)
                    dve.wait_ge(*exp_a[s].at(i, 1))
                    keep(v.reciprocal(fac[s][:, 0:T], sums[s][:, 0:T]))
                    settle()
                    keep(v.tensor_scalar(fac[s][:, 0:T], fac[s][:, 0:T], TG[:, 0:1], None, ALU.mult))

                def a_values(s):
                    settle()
                    dve.wait_ge(*pva_mm[s].at(i, 1))
                    for t in range(T):
                        ins = v.scalar_tensor_tensor(X[s][:, t, :], tiles(s, 2)[:, t, :], fac[s][:, t:t + 1],
                                                     XIN[s][:, t, :], ALU.mult, ALU.add)
                    ins.then_inc(xin_used[s].sem, 1)
                    dve.wait_ge(*xin_used[s].at(i, 1))
                    layernorm(s, XN[s], X[s]).then_inc(xn_ready[s].sem, 1)

                def best(s, k, n, r, bias=None):
                    bank = {1: 3, 2: 2, 3: 3}[k]
                    dve.wait_ge(*logits_mm[s].at(i, k))
                    if bias is None:
                        keep(v.tensor_copy(LG[s][:, :, 0:n], tiles(s, bank)[:, :, 0:n]))
                    else:
                        keep(v.tensor_tensor(LG[s][:, :, 0:n], tiles(s, bank)[:, :, 0:n],
                                             bias.rearrange("p (a e) -> p a e", a=1).broadcast_to((P, T, n)), ALU.add))
                    wide = max(n, 8)
                    if n < wide:
                        keep(v.memset(LG[s][:, :, n:wide], -BIG))
                    settle()
                    apart()
                    for t in range(T):
                        keep(v.max(top[s][:, t, :], LG[s][:, t, 0:wide]))
                    settle()
                    apart()
                    for t in range(T):
                        keep(v.max_index(topi[s][:, t, :], top[s][:, t, :], LG[s][:, t, 0:wide]))
                    v.tensor_tensor(gw[s][:, :, 0:r], top[s][:, :, 0:r], top[s][:, :, 0:1].broadcast_to((P, T, r)),
                                    ALU.subtract).then_inc(top_ready[s].sem, 1)
                    settle()
                    keep(v.tensor_copy(topf[s][:, :, 0:r], topi[s][:, :, 0:r]))

                def spread(s, k, n, r, scale=None):
                    dve.wait_ge(*top_exp[s].at(i, k))
                    if k == 1:
                        keep(v.tensor_tensor(gw[s][:, :, 0:r], gw[s][:, :, 0:r], gsel[s][:, :, 0:r], ALU.mult))
                        settle()
                    keep(v.tensor_reduce(gs[s][:, :], gw[s][:, :, 0:r], AX_X, ALU.add))
                    settle()
                    keep(v.reciprocal(gs[s][:, :], gs[s][:, :]))
                    settle()
                    keep(v.tensor_tensor(gw[s][:, :, 0:r], gw[s][:, :, 0:r],
                                         gs[s][:, :].rearrange("p (t a) -> p t a", a=1).broadcast_to((P, T, r)), ALU.mult))
                    for t in range(T):
                        sel = gsel[s][:, t, 0:n * r].rearrange("p (e r) -> p e r", e=n)
                        keep(v.tensor_tensor(sel, iota_f[:, 0:n].rearrange("p (e a) -> p e a", a=1).broadcast_to((P, n, r)),
                                             topf[s][:, t, 0:r].rearrange("p (a r) -> p a r", a=1).broadcast_to((P, n, r)),
                                             ALU.is_equal))
                    settle()
                    for t in range(T):
                        sel = gsel[s][:, t, 0:n * r].rearrange("p (e r) -> p e r", e=n)
                        keep(v.tensor_tensor(sel, sel, gw[s][:, t, 0:r].rearrange("p (a r) -> p a r", a=1)
                                             .broadcast_to((P, n, r)), ALU.mult))
                    settle()
                    ins = v.tensor_reduce(gates[s][:, :, 0:n],
                                          gsel[s][:, :, 0:n * r].rearrange("p t (e r) -> p t e r", e=n), AX_X, ALU.add)
                    if scale is None:
                        ins.then_inc(gates_ready[s].sem, 1)
                    else:
                        keep(ins)
                        settle()
                        v.tensor_scalar(gates[s][:, :, 0:n], gates[s][:, :, 0:n], scale, None,
                                        ALU.mult).then_inc(gates_ready[s].sem, 1)

                def b_gate(s):
                    best(s, 1, E0, E0, row("gate_b"))

                def gates_to_columns(s, k, n):
                    dve.wait_ge(*gT_mm[s].at(i, k))
                    v.tensor_copy(gT[s][0:n, :, :], PS[s][0:n, 3, 0:T * P].rearrange("p (t q) -> p t q", t=T)
                                  ).then_inc(gT_ready[s].sem, 1)

                def add_bias(s, k, acc):
                    dve.wait_ge(*bias_mm[s].at(i, k))
                    ins = v.tensor_tensor(acc[:, :, :], acc[:, :, :], tiles(s, 3), ALU.add)
                    ins.then_inc(bias_added[s].sem, 1)
                    dve.wait_ge(*bias_added[s].at(i, k))

                def b_expert(s, e):
                    if e == 0:
                        dve.wait_ge(*z_mm[s].at(i, 1))
                        keep(v.tensor_scalar(zk[s][:, :], tiles(s, 3)[:, :, E0], row("dp_b2"), None, ALU.add))
                        settle()
                        for t in range(T):
                            keep(v.tensor_scalar(gsel[s][:, t, 0:E0], thresholds[:, :], zk[s][:, t:t + 1], None, ALU.is_le))
                        settle()
                        spread(s, 1, E0, E0, TG[:, 2:3])
                        dve.wait_ge(*gates_ready[s].at(i, 1))
                    if e == 2:
                        gates_to_columns(s, 1, E0)
                    if e == 3:
                        dve.wait_ge(*down_added[s].at(i, e - 1))
                        add_bias(s, 1, X[s])
                    if e:
                        dve.wait_ge(*down_mm[s].at(i, e))
                        if e > 1:
                            dve.wait_ge(*down_added[s].at(i, e - 1))
                        for t in range(T):
                            ins = v.scalar_tensor_tensor(X[s][:, t, :], tiles(s, 2)[:, t, :], gates[s][:, t, e - 1:e],
                                                         X[s][:, t, :], ALU.mult, ALU.add)
                        ins.then_inc(down_added[s].sem, 1)

                def c_norm(s):
                    dve.wait_ge(*down_added[s].at(i, E0))
                    layernorm(s, XN[s], X[s]).then_inc(xn_ready[s].sem, 1)

                def c_query(s):
                    dve.wait_ge(*qr_mm[s].at(i, 1))
                    for t in range(T):
                        ins = v.tensor_tensor(QR[s][:, t, :], tiles(s, 1)[:, t, :], row("bq"), ALU.add)
                    ins.then_inc(qr_ready[s].sem, 1)

                def c_step(s, j):
                    if j < STEPS1:
                        dve.wait_ge(*sc_mm[s].at(i, j + 1))
                        v.tensor_reduce(nmax[s][:, j * HEADS:(j + 1) * HEADS], PS[s][:, 0:HEADS, 0:256], AX_X, ALU.max,
                                        negate=True).then_inc(sc_max[s].sem, 1)
                    if 1 <= j <= STEPS1:
                        k = j - 1
                        dve.wait_ge(*pt_mm[s].at(i, k + 1))
                        if k >= 2:
                            dve.wait_ge(*pv_mm[s].at(i, k - 1))
                        v.tensor_copy(PTG[s][k % 2].rearrange("p h c q -> p (h c q)"), PS[s][:, 2, :]
                                      ).then_inc(pt_ready[s].sem, 1)

                def kan_norm(s):
                    dve.wait_ge(*sc_exp[s].at(i, STEPS1))
                    keep(v.reciprocal(fac[s][:, :], sums[s][:, :]))
                    settle()
                    dve.wait_ge(*pv_mm[s].at(i, STEPS1))
                    for t in range(T):
                        keep(v.tensor_tensor(XN[s][:, t, :].rearrange("p (h d) -> p h d", h=H1),
                                             tiles(s, 3)[:, t, :].rearrange("p (h d) -> p h d", h=H1),
                                             fac[s][:, t * H1:(t + 1) * H1].rearrange("p (h a) -> p h a", a=1)
                                             .broadcast_to((P, H1, HD1)), ALU.mult))
                    settle()
                    keep(v.tensor_tensor(QR[s][:, :, :], QR[s][:, :, :], XN[s][:, :, :], ALU.add))
                    layernorm(s, XN[s], QR[s]).then_inc(xn_ready[s].sem, 1)

                def kan_silu(s):
                    dve.wait_ge(*tanh_half[s].at(i, 1))
                    keep(v.tensor_scalar(SIG[s], SIG[s], 0.5, 0.5, ALU.mult, ALU.add))
                    settle()
                    v.tensor_tensor(SILU[s], SIG[s], XT[s][:, :, :].rearrange("p c n -> p (c n)"),
                                    ALU.mult).then_inc(silu_ready[s].sem, 1)
                    kan_clip(s, 0)

                def kan_clip(s, q):
                    dve.wait_ge(*distance[s].at(i, q + 1))
                    u, far = spline_buf(s, q, 0), spline_buf(s, q, 1)
                    keep(v.tensor_scalar(far, u, -2.0, 0.0, ALU.add, ALU.min))
                    v.tensor_scalar(u, u, -1.0, 0.0, ALU.add, ALU.min).then_inc(clipped[s].sem, 1)

                def kan(s, q):
                    if q + 1 < KNOTS // 2:
                        kan_clip(s, q + 1)
                    u, far, near2 = (spline_buf(s, q, k) for k in (0, 1, 3))
                    dve.wait_ge(*squares[s].at(i, q + 1))
                    keep(v.tensor_tensor(near2, near2, u, ALU.mult))
                    settle()
                    dve.wait_ge(*far_cube[s].at(i, q + 1))
                    v.tensor_tensor(near2, near2, far, ALU.subtract).then_inc(spline_made[s].sem, 1)

                def d_source(s):
                    dve.wait_ge(*spline_mm[s].at(i, 4))
                    for t in range(T):
                        keep(v.scalar_tensor_tensor(X[s][:, t, :], PS[s][:, 1 + t, 0:256], TG[:, 1:2], X[s][:, t, :],
                                                    ALU.mult, ALU.add))
                    keep(layernorm(s, QR[s], X[s]))

                def d_norm(s):
                    layernorm(s, XN[s], QR[s]).then_inc(xn_ready[s].sem, 1)

                def d_kv(s):
                    dve.wait_ge(*kv_mm[s].at(i, 1))
                    v.tensor_tensor(VD[s], PS[s][:, 3, 256:512].rearrange("p (c h) -> p c h", c=C),
                                    row("v_b").rearrange("p (a h) -> p a h", a=1).broadcast_to((P, C, HD)),
                                    ALU.add).then_inc(vd_ready[s].sem, 1)
                    best(s, 2, EA, 2)

                def d_gates(s):
                    spread(s, 2, EA, 2)
                    dve.wait_ge(*gates_ready[s].at(i, 2))

                def d_rel(s, t):
                    dve.wait_ge(*rel_mm[s].at(i, t + 1))
                    v.tensor_copy(RELR[s][t][:, :, PADW:PADW + REL],
                                  PS[s][:, :, :].rearrange("p b (h n) -> p (b h) n", h=2)[:, :, 0:REL]
                                  ).then_inc(rel_band[s].sem, 1)

                def d_step(s, j):
                    per_tile = EA // HEADS
                    if j < STEPSA:
                        t, e0 = j // per_tile, (j % per_tile) * HEADS
                        if j % per_tile == 0:
                            dve.wait_ge(*bias_in[s].at(i, 32 * (t + 1)))
                            dve.wait_ge(*rel_filled[s].at(i, t + 1))
                        dve.wait_ge(*sd_mm[s].at(i, j + 1))
                        apart()
                        for h in range(HEADS):
                            k = j * HEADS + h
                            keep(v.tensor_tensor_reduce(BS[s][t][:, e0 + h, :], tiles(s, 0)[:, h, :], BS[s][t][:, e0 + h, :],
                                                        1.0, -BIG, ALU.add, ALU.max, nmax[s][:, k:k + 1]))
                        settle()
                        k = j * HEADS
                        v.tensor_scalar(nmax[s][:, k:k + HEADS], nmax[s][:, k:k + HEADS], -1.0, None,
                                        ALU.mult).then_inc(sd_max[s].sem, 1)
                    if 1 <= j <= STEPSA:
                        n = j - 1
                        t, e0 = n // per_tile, (n % per_tile) * HEADS
                        k = n * HEADS
                        dve.wait_ge(*sd_exp[s].at(i, n + 1))
                        keep(v.reciprocal(fac[s][:, k:k + HEADS], sums[s][:, k:k + HEADS]))
                        settle()
                        keep(v.tensor_tensor(fac[s][:, k:k + HEADS], fac[s][:, k:k + HEADS],
                                             gates[s][:, t, e0:e0 + HEADS], ALU.mult))
                        settle()
                        for h in range(HEADS):
                            ins = v.tensor_scalar(BS[s][t][:, e0 + h, :], BS[s][t][:, e0 + h, :], fac[s][:, k + h:k + h + 1],
                                                  None, ALU.mult)
                        ins.then_inc(pd_ready[s].sem, 1)
                    if 2 <= j <= STEPSA + 1:
                        n = j - 2
                        dve.wait_ge(*ptd_mm[s].at(i, n + 1))
                        if n >= 2:
                            dve.wait_ge(*cx_mm[s].at(i, n - 1))
                        v.tensor_copy(PTG[s][n % 2].rearrange("p h c q -> p (h c q)"), PS[s][:, 1, :]
                                      ).then_inc(ptd_ready[s].sem, 1)

                def d_out(s):
                    dve.wait_ge(*od_mm[s].at(i, T))
                    for t in range(T):
                        v.tensor_tensor(QR[s][:, t, :], QR[s][:, t, :], tiles(s, 3)[:, t, :],
                                        ALU.add).then_inc(od_added[s].sem, 1)
                    gates_to_columns(s, 2, EA)

                def f_norm(s):
                    dve.wait_ge(*od_added[s].at(i, T))
                    add_bias(s, 2, QR[s])
                    layernorm(s, XN[s], QR[s]).then_inc(xn_ready[s].sem, 1)

                def f_gate(s):
                    best(s, 3, EF, 2)

                def f_gates(s):
                    spread(s, 3, EF, 2)
                    dve.wait_ge(*gates_ready[s].at(i, 3))
                    gates_to_columns(s, 3, EF)

                def f_experts(s, g):
                    if g == 1:
                        add_bias(s, 3, QR[s])
                    for e in range(FG):
                        n = (g - 1) * FG + e
                        dve.wait_ge(*fd_mm[s].at(i, n + 1))
                        if n:
                            dve.wait_ge(*fd_added[s].at(i, n))
                        for t in range(T):
                            ins = v.scalar_tensor_tensor(QR[s][:, t, :], tiles(s, 2 + n % 2)[:, t, :],
                                                         gates[s][:, t, n:n + 1], QR[s][:, t, :], ALU.mult, ALU.add)
                        ins.then_inc(fd_added[s].sem, 1)

                def finish(s):
                    dve.wait_ge(*fd_added[s].at(i, EF))
                    v.scalar_tensor_tensor(VA[s][:, :, :], QR[s][:, :, :], TG[:, 3:4], X[s][:, :, :],
                                           ALU.mult, ALU.add).then_inc(out_ready[s].sem, 1)

                def both(step, *args):
                    for s in range(STREAMS):
                        step(s, *args)

                both(a_norm)
                both(a_scores)
                both(a_turn)
                both(a_values)
                both(b_gate)
                for e in range(E0 + 1):
                    both(b_expert, e)
                both(c_norm)
                both(c_query)
                for j in range(STEPS1 + 2):
                    both(c_step, j)
                both(kan_norm)
                both(kan_silu)
                for q in range(KNOTS // 2):
                    both(kan, q)
                both(d_source)
                both(d_norm)
                both(d_kv)
                for t in range(T):
                    both(d_rel, t)
                    if t == 0:
                        both(d_gates)
                for j in range(STEPSA + 3):
                    both(d_step, j)
                both(d_out)
                both(f_norm)
                both(f_gate)
                both(f_gates)
                for g in range(1, EF // FG + 1):
                    both(f_experts, g)
                both(finish)
            assert chained[0] == CHAIN["dve"], chained[0]


CONSTS = E0 + KNOTS + 1 + 1


def kernel(**inputs):
    import numpy as np
    import concourse.bacc as bacc
    from concourse import mybir as _mybir
    from concourse.bass_utils import run_bass_kernel_spmd

    a = {k: np.ascontiguousarray(v) for k, v in inputs.items()}

    def chunks(m):
        r, n = m.shape
        return m.reshape(r // P, P, n).transpose(1, 0, 2).reshape(P, -1)

    def column(v):
        return v.reshape(-1, P).T

    parts = {
        "wq0": chunks(a["L0_xattn_Wq"]), "wk0": chunks(a["L0_xattn_Wk"]), "wv0": chunks(a["L0_xattn_Wv"].T),
        "dp_w1": chunks(a["L0_ffn_dp_w1"]), "dp_w2": a["L0_ffn_dp_w2"], "gate_w": chunks(a["L0_ffn_gate_w"]),
        "wq": chunks(a["L1_xattn_wq"].T), "wk": chunks(a["L1_xattn_wk"].T), "wv": chunks(a["L1_xattn_wv"].T),
        "base": chunks(a["L1_xattn_kan_base_w"].T),
        "q_w": np.concatenate([chunks(m) for m in a["L1_ffn_q_w"]], 1),
        "k_w": chunks(a["L1_ffn_k_w"]), "v_w": chunks(a["L1_ffn_v_w"]),
        "o_w": np.concatenate(list(a["L1_ffn_o_w"]), 1), "rel": a["L1_ffn_rel_table"].T,
        "agate": chunks(a["L1_ffn_attn_gate_w"]), "fgate": chunks(a["L1_ffn_ff_gate_w"]),
        "dp_b1": column(a["L0_ffn_dp_b1"]), "eb1": column(a["L0_ffn_eb1"]), "bk": column(a["L1_xattn_bk"]),
        "ln_g": column(a["L1_xattn_ln_g"]), "ln_b": column(a["L1_xattn_ln_b"]),
        "ln1_w": column(a["L1_ffn_ln1_w"]), "ln1_b": column(a["L1_ffn_ln1_b"]),
        "ln2_w": column(a["L1_ffn_ln2_w"]), "ln2_b": column(a["L1_ffn_ln2_b"]),
        "q_b": column(a["L1_ffn_q_b"]), "k_b": column(a["L1_ffn_k_b"]), "ff_b1": column(a["L1_ffn_ff_b1"]),
    }
    packed = np.concatenate([parts[name] for name in PACK], 1)
    row_parts = {
        "bq": a["L1_xattn_bq"], "bv": a["L1_xattn_bv"], "v_b": a["L1_ffn_v_b"], "gate_b": a["L0_ffn_gate_b"],
        "dp_b2": a["L0_ffn_dp_b2"], "g": np.stack([a["g_xattn"], a["g_ffn"]]).reshape(-1),
    }
    unit_list = [np.concatenate([chunks(w1), chunks(w2)], 1) for w1, w2 in zip(a["L0_ffn_ew1"], a["L0_ffn_ew2"])]
    for g in range(EF // FG):
        es = range(g * FG, (g + 1) * FG)
        unit_list.append(np.concatenate([chunks(a["L1_ffn_ff_w1"][e]) for e in es] + [a["L1_ffn_ff_w2"][e] for e in es], 1))
    spline = a["L1_xattn_kan_spline_w"].transpose(1, 2, 0).reshape(D, KNOTS * D)
    arrays = {
        "x_in": a["x"], "ctx_t": a["ctx_1024"].transpose(0, 2, 1), "mask": a["mask_BxSxS2_ik0"],
        "packed": packed, "rows": np.concatenate([row_parts[name] for name in ROWS]),
        "bias_e": a["L0_ffn_eb2"], "bias_o": a["L1_ffn_o_b"], "bias_f": a["L1_ffn_ff_b2"],
        "spline_w": chunks(spline), "spline_s": chunks(a["L1_xattn_kan_spline_scaler"].T),
        "units": np.stack(unit_list), "ident": np.eye(P, dtype=np.float32),
    }
    arrays = {k: np.ascontiguousarray(v) for k, v in arrays.items()}
    nc = bacc.Bacc("TRN2", target_bir_lowering=False, num_devices=1)
    args = [nc.dram_tensor(f"in_{k}", v.shape, _mybir.dt.from_np(v.dtype), kind="ExternalInput").ap()
            for k, v in arrays.items()]
    args.append(nc.dram_tensor("out_0", (B, S, D), _mybir.dt.float32, kind="ExternalOutput").ap())
    build_program(nc, *args)
    r = run_bass_kernel_spmd(nc, [{f"in_{k}": v for k, v in arrays.items()}], core_ids=[0])
    return r.results[0]["out_0"]
```

```python
from contextlib import ExitStack

import numpy as np

import concourse.bass as bass
from concourse import mybir

F32 = mybir.dt.float32
I32 = mybir.dt.int32
U32 = mybir.dt.uint32
ALU = mybir.AluOpType
ACT = mybir.ActivationFunctionType
AX_X = mybir.AxisListType.X

P = 128
B, S, D = 8, 256, 256
T = S // P
C = D // P
STREAMS = 2
PAIRS = B // STREAMS
EPS = 1e-5
BIG = 3.0e38

A_SCALE = 1.0 / 16.0
MASKED = -1.0e10 * A_SCALE

E0, H0 = 4, 512
HC0 = H0 // P
K_THRESHOLDS = [-BIG] + [float(np.log(np.expm1(0.5 + 1.5 * (r - 0.5) / 3))) for r in range(1, E0)]

H1, HD1 = 8, 32
C_SCALE = D ** -0.5
KNOTS = 8
GRID_H = 2.0 / 5

EA, HD = 8, 128
MAXP = 64
REL = 2 * MAXP + 1
PADW = MAXP - 1
RW = REL + 2 * PADW
GROUP = 64
EF, FH = 16, 128
FG = 4

HEADS = 2
STEPS1 = T * H1 // HEADS
STEPSA = T * EA // HEADS

UNIT = 2048
SLOTS = 2
UNITS = E0 + EF // FG
SLOT_USES = UNITS // SLOTS

PACK = {}
_at = 0
for _name, _n in (("wq0", C * 256), ("wk0", C * 256), ("wv0", C * 256), ("dp_w1", C * 128),
                  ("dp_w2", 1), ("gate_w", C * E0), ("wq", C * 256), ("wk", C * 256), ("wv", C * 256),
                  ("base", C * 256), ("q_w", EA * C * HD), ("k_w", C * HD), ("v_w", C * HD),
                  ("o_w", EA * 256), ("rel", REL), ("agate", C * EA), ("fgate", C * EF),
                  ("dp_b1", 1), ("eb1", E0 * HC0), ("bk", C), ("ln_g", C), ("ln_b", C),
                  ("ln1_w", C), ("ln1_b", C), ("ln2_w", C), ("ln2_b", C), ("q_b", EA), ("k_b", 1),
                  ("ff_b1", EF)):
    PACK[_name] = (_at, _n)
    _at += _n
NPACK = _at
NRAW0 = 2 * C * 256

ROWS = {}
_at = 0
for _name, _n in (("bq", 256), ("bv", 256), ("v_b", HD), ("gate_b", E0), ("dp_b2", 1), ("g", 4)):
    ROWS[_name] = (_at, _n)
    _at += _n
NROWS = _at

CHAIN = {"dve": 248}

LN_A, LN_B, LN_C, LN_KAN, LN_MOA, LN_FF = range(1, 7)


class Signal:

    def __init__(self, sem, per):
        self.sem, self.per = sem, per

    def at(self, i, k):
        return self.sem, i * self.per + k


STEPS = (
    [("a_norm", (), 0, 6), ("a_first", (), 2.0, 1), ("a_query", (), 3.4, 1), ("a_scores", (), 1.7, 4),
     ("a_turn", (), 2.0, 1), ("a_values", (), 1.7, 8), ("b_turn", (), 0.3, 1.5), ("b_gate", (), 1.2, 1)]
    + [("b_expert", (e,), 3.4 if e in (0, E0) else 6.8, 2) for e in range(E0 + 1)]
    + [("c_norm", (), 0, 6), ("c_turn", (), 0.3, 1.5), ("c_query", (), 1.7, 1.5), ("c_query_turn", (), 0.3, 1.5)]
    + [("c_step", (j,), 1.5, 1) for j in range(STEPS1 + 2)]
    + [("kan_norm", (), 0, 8), ("kan_turn", (), 0.3, 3), ("kan_silu", (), 0, 4)]
    + [("kan", (q,), 3.4, 1) for q in range(KNOTS // 2)]
    + [("d_source", (), 0, 7), ("d_norm", (), 0, 6), ("d_turn", (), 0.3, 1.5), ("d_kv", (), 1.8, 0)]
    + [("d_queries", (h,), 3.4, 0) for h in range(2)]
    + [("d_rel", (0,), 1.7, 1), ("d_gates", (), 0, 0), ("d_rel", (1,), 1.7, 1)]
    + [("d_step", (j,), 2.8, 1) for j in range(STEPSA + 3)]
    + [("d_out", (), 0, 1), ("d_gate_columns", (), 0.2, 1), ("d_gate_bias", (), 0.8, 0),
       ("f_norm", (), 0, 6), ("f_turn", (), 0.3, 1.5), ("f_gate", (), 0.3, 1), ("f_gates", (), 0, 0)]
    + [("f_experts", (g,), 3.4 if g in (0, EF // FG) else 6.8, 2) for g in range(EF // FG + 1)]
    + [("finish", (), 0, 0)])
OFFSET = 12.0


def merged():
    experts = [n for n, step in enumerate(STEPS) if step[0] in ("b_expert", "f_experts")]
    order, at, ready, now = [], [0, 0], [0.0, OFFSET], 0.0

    def may(s):
        n = experts.index(at[s]) if at[s] in experts else 0
        return at[s] < len(STEPS) and (s == 1 or n < SLOTS or experts[n - SLOTS] < at[1])

    while any(n < len(STEPS) for n in at):
        s = min(filter(may, range(STREAMS)), key=lambda s: (max(ready[s], now), ready[s]))
        name, args, busy, wait = STEPS[at[s]]
        now = max(now, ready[s]) + busy
        ready[s] = now + wait
        at[s] += 1
        order.append((name, args, s))
    return order


SCHEDULE = merged()


class StreamSignal:

    def __init__(self, sem, order, stream):
        self.sem, self.per = sem, len(order)
        self.places = [n + 1 for n, s in enumerate(order) if s == stream]

    def at(self, i, k):
        return self.sem, i * self.per + self.places[k - 1]


def step_keys(name, first, end):
    return [(name, (j,)) for j in range(first, end)]


def build_program(nc, x_in, ctx_t, mask, packed, rows, bias_e, bias_o, bias_f, spline_w, spline_s,
                  units, ident_in, out):
    with ExitStack() as ctx:
        def sb(name, shape, dt=F32):
            return ctx.enter_context(nc.sbuf_tensor(name, shape, dt))

        def sem(name):
            return ctx.enter_context(nc.semaphore(name))

        def signal(name, raised_in):
            keys = [(k, ()) if isinstance(k, str) else k for k in raised_in]
            order = [s for step, args, s in SCHEDULE for key in keys if key == (step, args)]
            one = sem(name)
            return [StreamSignal(one, order, s) for s in range(STREAMS)]

        def dma_signal(name, per):
            return [Signal(sem(f"{name}_{s}"), per) for s in range(STREAMS)]

        W = sb("resident", [P, NPACK - NRAW0])
        G0 = sb("g0", [P, C, 256])
        SW = sb("spline_weights", [P, C, KNOTS, 256])
        W1 = [sb(f"w1_slot{k}", [P, UNIT // 2]) for k in range(SLOTS)]
        W2 = [sb(f"w2_slot{k}", [P, UNIT // 2]) for k in range(SLOTS)]
        ROW = sb("bias_rows", [P, NROWS])
        BE = sb("expert_bias", [E0, 256])
        BO = sb("head_bias", [EA, 256])
        BF = sb("ff_bias", [EF, 256])
        ident = sb("ident", [P, P])
        iota_f = sb("iota_f", [P, EF])
        iota_u = sb("iota_u", [P, EF], I32)
        TG = sb("tanh_g", [P, 4])
        spare = sb("spare", [1, 2])
        minus_half = sb("minus_half", [P, T])
        thresholds = sb("thresholds", [P, E0])
        knot_bias = sb("knot_bias", [P, KNOTS])
        qb_scaled = sb("qb_scaled", [P, EA])

        def w(name):
            a, n = PACK[name]
            return W[:, a - NRAW0:a - NRAW0 + n]

        def row(name):
            a, n = ROWS[name]
            return ROW[:, a:a + n]

        wv0 = w("wv0").rearrange("p (c o) -> p c o", c=C)
        dp_w1 = w("dp_w1").rearrange("p (c o) -> p c o", c=C)
        gate_w = w("gate_w").rearrange("p (c o) -> p c o", c=C)
        wq = w("wq").rearrange("p (c o) -> p c o", c=C)
        wk = w("wk").rearrange("p (c o) -> p c o", c=C)
        wv = w("wv").rearrange("p (c o) -> p c o", c=C)
        base = w("base").rearrange("p (c o) -> p c o", c=C)
        q_w = w("q_w").rearrange("p (e c h) -> p e c h", e=EA, c=C)
        k_w = w("k_w").rearrange("p (c h) -> p c h", c=C)
        v_w = w("v_w").rearrange("p (c h) -> p c h", c=C)
        o_w = w("o_w").rearrange("p (e o) -> p e o", e=EA)
        agate = w("agate").rearrange("p (c e) -> p c e", c=C)
        fgate = w("fgate").rearrange("p (c e) -> p c e", c=C)

        def each(name, shape, dt=F32):
            return [sb(f"{name}{s}", shape, dt) for s in range(STREAMS)]

        XIN = each("x_loaded", [P, T, 256])
        CT = each("ctx_columns", [P, C, 256])
        MASK = each("mask", [P, T, 256], I32)
        X = each("x", [P, T, 256])
        XN = each("normed_rows", [P, T, 256])
        XT = each("normed_columns", [P, C, 256])
        QT = each("q_columns", [P, C, 256])
        QR = each("q_rows", [P, T, 256])
        KT = each("k_columns", [P, C, 256])
        VA = each("v_layer0", [P, T, 256])
        VC = each("v_layer1", [P, T, 256])
        BIGB = each("scratch", [P, 5, 2048])
        st = each("bn_stats", [P, T, 6])
        mv = each("mean_var", [P, T, 2])
        rstd = each("rstd", [P, T])
        nmax = each("neg_max", [P, T * EA])
        sums = each("exp_sums", [P, T * EA])
        fac = each("row_factors", [P, T * EA])
        LG = each("logits", [P, T, EF])
        top = each("top8", [P, T, 8])
        topi = each("top8_index", [P, T, 8], U32)
        topf = each("top8_index_f", [P, T, 8])
        gw = each("top_weights", [P, T, E0])
        gs = each("top_sum", [P, T])
        gsel = each("gate_select", [P, T, EF * E0])
        gates = each("gates", [P, T, EF])
        zk = each("k_score", [P, T])
        gT = each("gates_columns", [EF, T, P])

        PA = [BIGB[s][:, 0, 0:512].rearrange("p (t k) -> p t k", t=T) for s in range(2)]
        PTA = [BIGB[s][:, 0, 512:1024].rearrange("p (c q) -> p c q", c=C) for s in range(2)]
        NM = [BIGB[s][:, 0, 1024:1536].rearrange("p (t k) -> p t k", t=T) for s in range(2)]
        HT = [BIGB[s][:, 1, 0:256] for s in range(2)]
        HID = [[BIGB[s][:, 2, 1024 * k:1024 * (k + 1)].rearrange("p (c q) -> p c q", c=4) for k in range(2)]
               for s in range(2)]
        PC = [[BIGB[s][:, 0, 512 * k:512 * (k + 1)].rearrange("p (h k) -> p h k", h=HEADS) for k in range(2)]
              for s in range(2)]
        PTG = [[BIGB[s][:, 1, 512 * k:512 * (k + 1)].rearrange("p (h c q) -> p h c q", h=HEADS, c=C)
                for k in range(2)] for s in range(2)]
        CTX = [[BIGB[s][:, 2, 256 * k:256 * (k + 1)].rearrange("p (h q) -> p h q", h=HEADS)
                for k in range(2)] for s in range(2)]
        SILU = [BIGB[s][:, 4, 0:512] for s in range(2)]
        SIG = [BIGB[s][:, 4, 512:1024] for s in range(2)]

        def spline_buf(s, q, k):
            return BIGB[s][:, k, 1024 * (q % 2):1024 * (q % 2 + 1)].rearrange("p (b n) -> p b n", b=2)

        RELR = [[BIGB[s][:, 1 + t, 0:EA * RW].rearrange("p (e r) -> p e r", e=EA) for t in range(T)]
                for s in range(2)]
        QD = [BIGB[s][:, 0, :].rearrange("p (e q) -> p e q", e=EA) for s in range(2)]
        BS = [[BIGB[s][:, 3 + t, :].rearrange("p (e k) -> p e k", e=EA) for t in range(T)] for s in range(2)]
        KD = [KT[s][:, 0, :] for s in range(2)]
        VD = [VC[s][:, 0, :].rearrange("p (c h) -> p c h", c=C) for s in range(2)]

        PS = [ctx.enter_context(nc.psum_tensor(f"psum{s}", [P, 4, 512], F32)) for s in range(STREAMS)]

        def tiles(s, bank):
            return PS[s][:, bank, :].rearrange("p (t n) -> p t n", t=2)

        rel_dram = nc.dram_tensor("rel_rows", (STREAMS, T, P, EA * RW), F32, kind="Internal").ap()

        weights_in = sem("weights_in")
        spline_in = sem("spline_in")
        consts_made = sem("consts_made")
        minus_half_made = sem("minus_half_made")
        g0_mm = sem("g0_mm")
        g0_ready = sem("g0_ready")
        spline_ready = sem("spline_ready")
        tanh_ready = sem("tanh_ready")
        dve_chain = Signal(sem("dve_chain"), CHAIN["dve"])
        w1_in = [Signal(sem(f"w1_in{k}"), 16 * SLOT_USES) for k in range(SLOTS)]
        w2_in = [Signal(sem(f"w2_in{k}"), 16 * SLOT_USES) for k in range(SLOTS)]
        x_loaded = dma_signal("x_loaded", 16)
        ctx_loaded = dma_signal("ctx_loaded", 16)
        mask_loaded = dma_signal("mask_loaded", 16)
        stored = dma_signal("stored", 16)
        rel_written = [dma_signal(f"rel_written_tile{t}", 16) for t in range(T)]
        bias_in = [dma_signal(f"bias_in_tile{t}", 32) for t in range(T)]

        norms = ["a_norm", "a_values", "c_norm", "kan_norm", "d_source", "d_norm", "f_norm"]
        xturns = ["a_first", "b_turn", "c_turn", "kan_turn", "d_turn", "f_turn"]
        moments_ready = signal("moments_ready", norms)
        rstd_ready = signal("rstd_ready", norms)
        xn_ready = signal("xn_ready", [k for k in norms if k != "d_source"])
        xT_mm = signal("xT_mm", xturns)
        xT_ready = signal("xT_ready", xturns)
        xin_used = signal("xin_used", ["a_values"])
        mask_used = signal("mask_used", ["a_norm"])
        va_mm = signal("va_mm", ["a_first"])
        va_ready = signal("va_ready", ["a_first"])
        kt_mm = signal("kt_mm", ["a_query"])
        kt_ready = signal("kt_ready", ["a_query"])
        vc_mm = signal("vc_mm", ["a_turn"])
        vc_ready = signal("vc_ready", ["a_turn"])
        qa_mm = signal("qa_mm", ["a_query"])
        qa_ready = signal("qa_ready", ["a_query"])
        sa_mm = signal("sa_mm", ["a_scores"])
        nmax_a = signal("nmax_a", ["a_scores"])
        exp_a = signal("exp_a", ["a_scores"])
        pta_mm = signal("pta_mm", ["a_turn"])
        pta_ready = signal("pta_ready", ["a_turn"])
        pva_mm = signal("pva_mm", ["a_values"])
        dp_mm = signal("dp_mm", ["b_gate"])
        dp_ready = signal("dp_ready", ["b_gate"])
        logits_mm = signal("logits_mm", ["b_gate", "d_kv", "f_gate"])
        z_mm = signal("z_mm", [("b_expert", (0,))])
        top_ready = signal("top_ready", ["b_gate", "d_kv", "f_gate"])
        top_exp = signal("top_exp", [("b_expert", (0,)), "d_kv", "f_gate"])
        gates_ready = signal("gates_ready", [("b_expert", (0,)), "d_gates", "f_gates"])
        gT_mm = signal("gT_mm", [("b_expert", (2,)), "d_gate_columns", ("f_experts", (0,))])
        gT_ready = signal("gT_ready", [("b_expert", (2,)), "d_gate_columns", ("f_experts", (0,))])
        bias_mm = signal("bias_mm", [("b_expert", (3,)), "d_gate_bias", ("f_experts", (1,))])
        bias_added = signal("bias_added", [("b_expert", (3,)), "f_norm", ("f_experts", (1,))])
        ups = step_keys("b_expert", 0, E0)
        downs = step_keys("b_expert", 1, E0 + 1)
        up_mm = signal("up_mm", ups)
        hid_ready = signal("hid_ready", ups)
        down_mm = signal("down_mm", downs)
        down_added = signal("down_added", downs)
        qr_mm = signal("qr_mm", ["c_query"])
        qr_ready = signal("qr_ready", ["c_query"])
        qt_mm = signal("qt_mm", ["c_query_turn"])
        qt_ready = signal("qt_ready", ["c_query_turn"])
        sc_mm = signal("sc_mm", step_keys("c_step", 0, STEPS1))
        sc_max = signal("sc_max", step_keys("c_step", 0, STEPS1))
        sc_exp = signal("sc_exp", step_keys("c_step", 0, STEPS1))
        pt_mm = signal("pt_mm", step_keys("c_step", 1, STEPS1 + 1))
        pt_ready = signal("pt_ready", step_keys("c_step", 1, STEPS1 + 1))
        pv_mm = signal("pv_mm", step_keys("c_step", 2, STEPS1 + 2))
        silu_ready = signal("silu_ready", ["kan_silu"])
        tanh_half = signal("tanh_half", ["kan_turn"])
        pairs_of_knots = step_keys("kan", 0, KNOTS // 2)
        distance = signal("distance", ["kan_turn"] + pairs_of_knots[:-1])
        clipped = signal("clipped", ["kan_silu"] + pairs_of_knots[:-1])
        squares = signal("squares", pairs_of_knots)
        far_cube = signal("far_cube", pairs_of_knots)
        spline_made = signal("spline_made", pairs_of_knots)
        spline_mm = signal("spline_mm", pairs_of_knots)
        kv_mm = signal("kv_mm", ["d_kv"])
        kd_ready = signal("kd_ready", ["d_kv"])
        vd_ready = signal("vd_ready", ["d_kv"])
        qd_mm = signal("qd_mm", step_keys("d_queries", 0, 2))
        qd_ready = signal("qd_ready", step_keys("d_queries", 0, 2))
        rel_mm = signal("rel_mm", step_keys("d_rel", 0, T))
        rel_band = signal("rel_band", step_keys("d_rel", 0, T))
        rel_padded = signal("rel_padded", step_keys("d_rel", 0, T))
        rel_filled = signal("rel_filled", step_keys("d_rel", 0, T))
        sd_mm = signal("sd_mm", step_keys("d_step", 0, STEPSA))
        sd_max = signal("sd_max", step_keys("d_step", 0, STEPSA))
        sd_exp = signal("sd_exp", step_keys("d_step", 0, STEPSA))
        pd_ready = signal("pd_ready", step_keys("d_step", 1, STEPSA + 1))
        ptd_mm = signal("ptd_mm", step_keys("d_step", 1, STEPSA + 1))
        ptd_ready = signal("ptd_ready", step_keys("d_step", 1, STEPSA + 1))
        cx_mm = signal("cx_mm", step_keys("d_step", 2, STEPSA + 2))
        cx_ready = signal("cx_ready", step_keys("d_step", 2, STEPSA + 2))
        od_mm = signal("od_mm", [("d_step", ((t + 1) * (EA // HEADS) + 2,)) for t in range(T)])
        od_added = signal("od_added", ["d_out"] * T)
        fu_mm = signal("fu_mm", step_keys("f_experts", 0, EF // FG))
        fh_ready = signal("fh_ready", step_keys("f_experts", 0, EF // FG))
        ff_downs = [("f_experts", (g,)) for g in range(1, EF // FG + 1) for _ in range(FG)]
        fd_mm = signal("fd_mm", ff_downs)
        fd_added = signal("fd_added", ff_downs)
        out_ready = signal("out_ready", ["finish"])

        raw = BIGB[0][:, 0, 0:NRAW0].rearrange("p (w c o) -> p w c o", w=2, c=C)
        scaler = BIGB[1][:, 0, 0:C * 256].rearrange("p (c o) -> p c o", c=C)

        def window(g):
            return max(0, g * GROUP - MAXP), min(S, (g + 1) * GROUP + MAXP)

        def take_turns(steps):
            for name, args, s in SCHEDULE:
                if name in steps:
                    step = steps[name]
                    step(s, *args)

        block = ctx.enter_context(nc.Block())

        @block.sync
        def _(sp):
            def load_inputs(n, s):
                sp.dma_start(XIN[s][:, :, :], x_in[n].rearrange("(t p) d -> p t d", p=P)).then_inc(x_loaded[s].sem, 16)
                sp.dma_start(CT[s][:, :, :], ctx_t[n].rearrange("(c p) t -> p c t", p=P)).then_inc(ctx_loaded[s].sem, 16)
                sp.dma_start(MASK[s][:, :, :], mask[n].rearrange("(t p) k -> p t k", p=P)).then_inc(mask_loaded[s].sem, 16)

            def load_w1(u):
                sp.dma_start(W1[u % SLOTS][:, :], units[u, :, 0:UNIT // 2]).then_inc(w1_in[u % SLOTS].sem, 16)

            def load_w2(u):
                sp.dma_start(W2[u % SLOTS][:, :], units[u, :, UNIT // 2:UNIT]).then_inc(w2_in[u % SLOTS].sem, 16)

            def write_rel(i, s, t):
                sp.wait_ge(*rel_padded[s].at(i, t + 1))
                sp.dma_start(rel_dram[s, t], RELR[s][t].rearrange("p e r -> p (e r)")).then_inc(rel_written[t][s].sem, 16)

            def read_rel(i, s, t):
                sp.wait_ge(*rel_written[t][s].at(i, 16))
                for j in range(2):
                    g = 2 * t + j
                    lo, hi = window(g)
                    first = rel_dram[s, t]
                    off = first.offset + j * GROUP * EA * RW + lo - g * GROUP + RW // 2
                    src = bass.AP(first.tensor, off, [[EA * RW - 1, GROUP], [RW, EA], [1, hi - lo]])
                    sp.dma_start(BS[s][t][j * GROUP:(j + 1) * GROUP, :, lo:hi], src).then_inc(bias_in[t][s].sem, 16)

            def a_round(i, last):
                def reload(u, load, used):
                    if u < UNITS or not last:
                        sp.wait_ge(*used)
                        load(u % UNITS)

                def b_expert(s, e):
                    if s == STREAMS - 1 and e < E0:
                        reload(e + SLOTS, load_w1, up_mm[s].at(i, e + 1))
                    if s == STREAMS - 1 and e:
                        reload(e - 1 + SLOTS, load_w2, down_mm[s].at(i, e))

                def f_experts(s, g):
                    if s == STREAMS - 1 and g < EF // FG:
                        reload(E0 + g + SLOTS, load_w1, fu_mm[s].at(i, g + 1))
                    if s == STREAMS - 1 and g:
                        reload(E0 + g - 1 + SLOTS, load_w2, fd_mm[s].at(i, g * FG))

                def c_norm(s):
                    if not last:
                        sp.wait_ge(*xin_used[s].at(i, 1))
                        sp.wait_ge(*mask_used[s].at(i, 1))
                        sp.wait_ge(*vc_mm[s].at(i, 1))
                        load_inputs(2 * i + (STREAMS + s), s)

                def d_rel(s, t):
                    write_rel(i, s, t)
                    if t:
                        read_rel(i, s, t - 1)

                def d_step(s, j):
                    if j == 0:
                        read_rel(i, s, T - 1)

                def finish(s):
                    sp.wait_ge(*out_ready[s].at(i, 1))
                    sp.dma_start(out[2 * i + s].rearrange("(t p) d -> p t d", p=P), VA[s][:, :, :]
                                 ).then_inc(stored[s].sem, 16)

                take_turns({"b_expert": b_expert, "f_experts": f_experts, "c_norm": c_norm, "d_rel": d_rel,
                            "d_step": d_step, "finish": finish})

            sp.dma_start(raw, packed[:, 0:NRAW0].rearrange("p (w c o) -> p w c o", w=2, c=C)).then_inc(weights_in, 16)
            for s in range(STREAMS):
                load_inputs(s, s)
                sp.sem_inc(stored[s].sem, 16)
            sp.dma_start(W[:, :], packed[:, NRAW0:NPACK]).then_inc(weights_in, 16)
            sp.dma_start(ident[:, :], ident_in).then_inc(weights_in, 16)
            sp.dma_start(ROW[:, :], rows.partition_broadcast(P)).then_inc(weights_in, 16)
            sp.dma_start(BE[:, :], bias_e).then_inc(weights_in, 16)
            sp.dma_start(BO[:, :], bias_o).then_inc(weights_in, 16)
            sp.dma_start(BF[:, :], bias_f).then_inc(weights_in, 16)
            for u in range(SLOTS):
                load_w1(u)
                load_w2(u)
            sp.dma_start(scaler, spline_s.rearrange("p (c o) -> p c o", c=C)).then_inc(spline_in, 16)
            sp.dma_start(SW[:, :, :, :], spline_w.rearrange("p (c b o) -> p c b o", c=C, b=KNOTS)).then_inc(spline_in, 16)

            with sp.Fori(0, PAIRS - 1) as i:
                a_round(i, False)
            a_round(PAIRS - 1, True)
            for s in range(STREAMS):
                sp.wait_ge(*stored[s].at(PAIRS, 16))

        NWEIGHT_DMAS = 7

        @block.gpsimd
        def _(pool):
            nc.gpsimd.memset(minus_half[:, :], -0.5).then_inc(minus_half_made, 1)
            pool.wait_ge(minus_half_made, 1)
            nc.gpsimd.iota(iota_u[:, :], pattern=[[1, EF]], base=0, channel_multiplier=0).then_inc(consts_made, 1)
            with pool.Fori(0, PAIRS) as i:
                def spline_far(s, q):
                    pool.wait_ge(*squares[s].at(i, q + 1))
                    pool.wait_ge(*clipped[s].at(i, q + 1))
                    b = spline_buf(s, q, 1)
                    nc.gpsimd.tensor_tensor(b, b, spline_buf(s, q, 2), ALU.mult).then_inc(far_cube[s].sem, 1)

                def power(k):
                    def step(s):
                        pool.wait_ge(*moments_ready[s].at(i, k))
                        nc.gpsimd.tensor_tensor(rstd[s][:, :], rstd[s][:, :], minus_half[:, :], ALU.pow
                                                ).then_inc(rstd_ready[s].sem, 1)
                    return step

                steps = {name: power(k + 1) for k, name in enumerate(norms)}
                take_turns({**steps, "kan": spline_far})

        @block.tensor
        def _(pe):
            def mm(o, a, b, start=True, stop=True):
                return pe.matmul(o, a, b, start=start, stop=stop)

            def rows_of(o, cols, weights, n):
                for t in range(T):
                    for c in range(C):
                        last = mm(o[:, t, 0:n], cols[:, c, t * P:(t + 1) * P], weights[:, c, :], c == 0, c == C - 1)
                return last

            pe.wait_ge(weights_in, 16 * NWEIGHT_DMAS)
            for a in range(C):
                for c in range(C):
                    last = mm(tiles(0, 0)[:, a, :], raw[:, 0, c, a * P:(a + 1) * P], raw[:, 1, c, :], c == 0, c == C - 1)
            last.then_inc(g0_mm, 1)
            pe.wait_ge(g0_ready, 1)

            with pe.Fori(0, PAIRS) as i:
                def turn(s, k):
                    pe.wait_ge(*xn_ready[s].at(i, k))
                    for c in range(C):
                        for t in range(T):
                            last = pe.transpose(tiles(s, 0)[:, c, t * P:(t + 1) * P],
                                                XN[s][:, t, c * P:(c + 1) * P], ident[:, :])
                    last.then_inc(xT_mm[s].sem, 1)

                def a_first(s):
                    pe.wait_ge(*ctx_loaded[s].at(i, 16))
                    rows_of(tiles(s, 3), CT[s], wv0, 256).then_inc(va_mm[s].sem, 1)
                    turn(s, LN_A)

                def a_query(s):
                    pe.wait_ge(*xT_ready[s].at(i, LN_A))
                    for a in range(C):
                        for c in range(C):
                            last = mm(tiles(s, 1)[:, a, :], G0[:, c, a * P:(a + 1) * P], XT[s][:, c, :], c == 0, c == C - 1)
                    last.then_inc(qa_mm[s].sem, 1)
                    for a in range(C):
                        for c in range(C):
                            last = mm(tiles(s, 2)[:, a, :], wk[:, c, a * P:(a + 1) * P], CT[s][:, c, :], c == 0, c == C - 1)
                    last.then_inc(kt_mm[s].sem, 1)

                def a_scores(s):
                    pe.wait_ge(*qa_ready[s].at(i, 1))
                    rows_of(tiles(s, 0), QT[s], CT[s], 256).then_inc(sa_mm[s].sem, 1)

                def a_turn(s):
                    pe.wait_ge(*va_ready[s].at(i, 1))
                    rows_of(tiles(s, 3), CT[s], wv, 256).then_inc(vc_mm[s].sem, 1)
                    pe.wait_ge(*exp_a[s].at(i, 1))
                    for c in range(C):
                        for t in range(T):
                            last = pe.transpose(tiles(s, 1)[:, c, t * P:(t + 1) * P],
                                                PA[s][:, t, c * P:(c + 1) * P], ident[:, :])
                    last.then_inc(pta_mm[s].sem, 1)

                def a_values(s):
                    pe.wait_ge(*kt_ready[s].at(i, 1))
                    pe.wait_ge(*pta_ready[s].at(i, 1))
                    rows_of(tiles(s, 2), PTA[s], VA[s], 256).then_inc(pva_mm[s].sem, 1)

                def b_turn(s):
                    turn(s, LN_B)

                def b_gate(s):
                    pe.wait_ge(*xT_ready[s].at(i, LN_B))
                    for c in range(C):
                        last = mm(tiles(s, 1)[:, 0, :], dp_w1[:, c, :], XT[s][:, c, :], c == 0, c == C - 1)
                    last.then_inc(dp_mm[s].sem, 1)
                    pe.wait_ge(*vc_ready[s].at(i, 1))
                    rows_of(tiles(s, 3), XT[s], gate_w, E0).then_inc(logits_mm[s].sem, 1)

                def gate_columns(s, k, n):
                    pe.wait_ge(*gates_ready[s].at(i, k))
                    for t in range(T):
                        last = mm(PS[s][0:n, 3, t * P:(t + 1) * P], gates[s][:, t, 0:n], ident[:, :])
                    last.then_inc(gT_mm[s].sem, 1)

                def gate_bias(s, k, n, weights):
                    pe.wait_ge(*gT_ready[s].at(i, k))
                    for t in range(T):
                        last = mm(tiles(s, 3)[:, t, :], gT[s][0:n, t, :], weights[:, :])
                    last.then_inc(bias_mm[s].sem, 1)

                def b_expert(s, e):
                    if e < E0:
                        k = e % SLOTS
                        pe.wait_ge(*w1_in[k].at(i, 16 * (e // SLOTS + 1)))
                        if e:
                            pe.wait_ge(*hid_ready[s].at(i, e))
                        else:
                            pe.wait_ge(*dp_ready[s].at(i, 1))
                        w1 = W1[k][:, :].rearrange("p (c h) -> p c h", c=C)
                        for h in range(HC0):
                            for c in range(C):
                                last = mm(PS[s][:, h // 2, (h % 2) * 256:(h % 2 + 1) * 256],
                                          w1[:, c, h * P:(h + 1) * P], XT[s][:, c, :], c == 0, c == C - 1)
                        last.then_inc(up_mm[s].sem, 1)
                    if e == 0:
                        pe.wait_ge(*top_ready[s].at(i, 1))
                        for t in range(T):
                            last = mm(tiles(s, 3)[:, t, E0:E0 + 1], HT[s][:, t * P:(t + 1) * P], w("dp_w2"))
                        last.then_inc(z_mm[s].sem, 1)
                    if e == 2:
                        gate_columns(s, 1, E0)
                    if e == 3:
                        gate_bias(s, 1, E0, BE)
                    if e:
                        k = (e - 1) % SLOTS
                        pe.wait_ge(*hid_ready[s].at(i, e))
                        if e > 1:
                            pe.wait_ge(*down_added[s].at(i, e - 1))
                        pe.wait_ge(*w2_in[k].at(i, 16 * ((e - 1) // SLOTS + 1)))
                        w2 = W2[k][:, :].rearrange("p (c o) -> p c o", c=HC0)
                        for t in range(T):
                            for c in range(HC0):
                                last = mm(tiles(s, 2)[:, t, :], HID[s][(e - 1) % 2][:, c, t * P:(t + 1) * P],
                                          w2[:, c, :], c == 0, c == HC0 - 1)
                        last.then_inc(down_mm[s].sem, 1)

                def c_turn(s):
                    turn(s, LN_C)

                def c_query(s):
                    pe.wait_ge(*xT_ready[s].at(i, LN_C))
                    rows_of(tiles(s, 1), XT[s], wq, 256).then_inc(qr_mm[s].sem, 1)

                def c_query_turn(s):
                    pe.wait_ge(*qr_ready[s].at(i, 1))
                    for c in range(C):
                        for t in range(T):
                            last = pe.transpose(tiles(s, 0)[:, c, t * P:(t + 1) * P],
                                                QR[s][:, t, c * P:(c + 1) * P], ident[:, :])
                    last.then_inc(qt_mm[s].sem, 1)

                def c_step(s, j):
                    per_tile = H1 // HEADS
                    if j < STEPS1:
                        t, h0 = j // per_tile, (j % per_tile) * HEADS
                        if j:
                            pe.wait_ge(*sc_exp[s].at(i, j))
                        else:
                            pe.wait_ge(*qt_ready[s].at(i, 1))
                        for h in range(h0, h0 + HEADS):
                            r = (h % 4) * HD1
                            last = mm(PS[s][:, h - h0, 0:256], QT[s][r:r + HD1, h // 4, t * P:(t + 1) * P],
                                      KT[s][r:r + HD1, h // 4, :])
                        last.then_inc(sc_mm[s].sem, 1)
                    if j >= 2:
                        k = j - 2
                        t, h0 = k // per_tile, (k % per_tile) * HEADS
                        pe.wait_ge(*pt_ready[s].at(i, k + 1))
                        for h in range(HEADS):
                            a = (h0 + h) * HD1
                            for c in range(C):
                                last = mm(tiles(s, 3)[:, t, a:a + HD1], PTG[s][k % 2][:, h, c, :],
                                          VC[s][:, c, a:a + HD1], c == 0, c == C - 1)
                        last.then_inc(pv_mm[s].sem, 1)
                    if 1 <= j <= STEPS1:
                        k = j - 1
                        pe.wait_ge(*sc_exp[s].at(i, k + 1))
                        if k:
                            pe.wait_ge(*pt_ready[s].at(i, k))
                        for h in range(HEADS):
                            for c in range(C):
                                a = (h * C + c) * P
                                last = pe.transpose(PS[s][:, 2, a:a + P], PC[s][k % 2][:, h, c * P:(c + 1) * P], ident[:, :])
                        last.then_inc(pt_mm[s].sem, 1)

                def kan_turn(s):
                    turn(s, LN_KAN)

                def kan(s, q):
                    if q == 0:
                        pe.wait_ge(*silu_ready[s].at(i, 1))
                        for t in range(T):
                            for c in range(C):
                                a = c * 256 + t * P
                                mm(PS[s][:, 1 + t, 0:256], SILU[s][:, a:a + P], base[:, c, :], c == 0, False)
                    pe.wait_ge(*spline_made[s].at(i, q + 1))
                    for t in range(T):
                        for b in range(2):
                            for c in range(C):
                                a = c * 256 + t * P
                                last = mm(PS[s][:, 1 + t, 0:256], spline_buf(s, q, 3)[:, b, a:a + P],
                                          SW[:, c, 2 * q + b, :], False, q == 3 and b == 1 and c == C - 1)
                    last.then_inc(spline_mm[s].sem, 1)

                def d_turn(s):
                    turn(s, LN_MOA)

                def d_kv(s):
                    pe.wait_ge(*xT_ready[s].at(i, LN_MOA))
                    for c in range(C):
                        mm(PS[s][:, 3, 0:256], k_w[:, c, :], XT[s][:, c, :], c == 0, c == C - 1)
                    for t in range(T):
                        for c in range(C):
                            last = mm(PS[s][:, 3, 256 + t * P:256 + (t + 1) * P], XT[s][:, c, t * P:(t + 1) * P],
                                      v_w[:, c, :], c == 0, c == C - 1)
                    last.then_inc(kv_mm[s].sem, 1)
                    rows_of(tiles(s, 2), XT[s], agate, EA).then_inc(logits_mm[s].sem, 1)

                def d_queries(s, half):
                    if half:
                        pe.wait_ge(*qd_ready[s].at(i, half))
                    for e in range(4):
                        for c in range(C):
                            last = mm(PS[s][:, e // 2, (e % 2) * 256:(e % 2 + 1) * 256],
                                      q_w[:, half * 4 + e, c, :], XT[s][:, c, :], c == 0, c == C - 1)
                    last.then_inc(qd_mm[s].sem, 1)

                def d_rel(s, t):
                    if t == 0:
                        pe.wait_ge(*qd_ready[s].at(i, 2))
                        pe.wait_ge(*kd_ready[s].at(i, 1))
                        pe.wait_ge(*vd_ready[s].at(i, 1))
                        pe.wait_ge(*top_ready[s].at(i, 2))
                    else:
                        pe.wait_ge(*rel_band[s].at(i, t))
                    for e in range(EA):
                        last = mm(PS[s][:, e // 2, (e % 2) * 256:(e % 2) * 256 + REL],
                                  QD[s][:, e, t * P:(t + 1) * P], w("rel"))
                    last.then_inc(rel_mm[s].sem, 1)

                def d_step(s, j):
                    per_tile = EA // HEADS
                    if j < STEPSA:
                        t, e0 = j // per_tile, (j % per_tile) * HEADS
                        if j:
                            pe.wait_ge(*sd_max[s].at(i, j))
                        else:
                            pe.wait_ge(*rel_band[s].at(i, T))
                        for h in range(HEADS):
                            last = mm(tiles(s, 0)[:, h, :], QD[s][:, e0 + h, t * P:(t + 1) * P], KD[s])
                        last.then_inc(sd_mm[s].sem, 1)
                    if 2 <= j <= STEPSA + 1:
                        k = j - 2
                        pe.wait_ge(*ptd_ready[s].at(i, k + 1))
                        if k:
                            pe.wait_ge(*cx_ready[s].at(i, k))
                        for h in range(HEADS):
                            for c in range(C):
                                last = mm(PS[s][:, 2, h * P:(h + 1) * P], VD[s][:, c, :], PTG[s][k % 2][:, h, c, :],
                                          c == 0, c == C - 1)
                        last.then_inc(cx_mm[s].sem, 1)
                    if j >= 3:
                        k = j - 3
                        t, e0 = k // per_tile, (k % per_tile) * HEADS
                        pe.wait_ge(*cx_ready[s].at(i, k + 1))
                        for h in range(HEADS):
                            last = mm(tiles(s, 3)[:, t, :], CTX[s][k % 2][:, h, :], o_w[:, e0 + h, :],
                                      e0 + h == 0, e0 + h == EA - 1)
                        if k % per_tile == per_tile - 1:
                            last.then_inc(od_mm[s].sem, 1)
                    if 1 <= j <= STEPSA:
                        k = j - 1
                        t, e0 = k // per_tile, (k % per_tile) * HEADS
                        pe.wait_ge(*pd_ready[s].at(i, k + 1))
                        if k:
                            pe.wait_ge(*ptd_ready[s].at(i, k))
                        for h in range(HEADS):
                            for c in range(C):
                                a = (h * C + c) * P
                                last = pe.transpose(PS[s][:, 1, a:a + P], BS[s][t][:, e0 + h, c * P:(c + 1) * P], ident[:, :])
                        last.then_inc(ptd_mm[s].sem, 1)

                def d_gate_columns(s):
                    pe.wait_ge(*od_added[s].at(i, T))
                    gate_columns(s, 2, EA)

                def d_gate_bias(s):
                    gate_bias(s, 2, EA, BO)

                def f_turn(s):
                    turn(s, LN_FF)

                def f_gate(s):
                    pe.wait_ge(*xT_ready[s].at(i, LN_FF))
                    rows_of(tiles(s, 3), XT[s], fgate, EF).then_inc(logits_mm[s].sem, 1)

                def f_gate_columns(s):
                    gate_columns(s, 3, EF)

                def f_gate_bias(s):
                    gate_bias(s, 3, EF, BF)

                def f_experts(s, g):
                    if g < EF // FG:
                        u = E0 + g
                        pe.wait_ge(*w1_in[u % SLOTS].at(i, 16 * (u // SLOTS + 1)))
                        if g:
                            pe.wait_ge(*fh_ready[s].at(i, g))
                        w1 = W1[u % SLOTS][:, :].rearrange("p (e c h) -> p e c h", e=FG, c=C)
                        for e in range(FG):
                            for c in range(C):
                                last = mm(PS[s][:, e // 2, (e % 2) * 256:(e % 2 + 1) * 256],
                                          w1[:, e, c, :], XT[s][:, c, :], c == 0, c == C - 1)
                        last.then_inc(fu_mm[s].sem, 1)
                    if g == 0:
                        f_gate_columns(s)
                    if g == 1:
                        f_gate_bias(s)
                        pe.wait_ge(*bias_added[s].at(i, 3))
                    if g:
                        u = E0 + g - 1
                        pe.wait_ge(*fh_ready[s].at(i, g))
                        pe.wait_ge(*w2_in[u % SLOTS].at(i, 16 * (u // SLOTS + 1)))
                        w2 = W2[u % SLOTS][:, :].rearrange("p (e o) -> p e o", e=FG)
                        for e in range(FG):
                            n = (g - 1) * FG + e
                            if n >= 2:
                                pe.wait_ge(*fd_added[s].at(i, n - 1))
                            for t in range(T):
                                last = mm(tiles(s, 2 + n % 2)[:, t, :], HID[s][(g - 1) % 2][:, e, t * P:(t + 1) * P],
                                          w2[:, e, :])
                            last.then_inc(fd_mm[s].sem, 1)

                take_turns({"a_first": a_first, "a_query": a_query, "a_scores": a_scores, "a_turn": a_turn, "a_values": a_values, "b_turn": b_turn, "b_gate": b_gate, "b_expert": b_expert, "c_turn": c_turn, "c_query": c_query, "c_query_turn": c_query_turn, "c_step": c_step, "kan_turn": kan_turn, "kan": kan, "d_turn": d_turn, "d_kv": d_kv, "d_queries": d_queries, "d_rel": d_rel, "d_step": d_step, "d_gate_columns": d_gate_columns, "d_gate_bias": d_gate_bias, "f_turn": f_turn, "f_gate": f_gate, "f_experts": f_experts})

        @block.scalar
        def _(act):
            chained = [0]

            act.wait_ge(weights_in, 16 * NWEIGHT_DMAS)
            nc.scalar.activation(TG[:, :], row("g"), ACT.Tanh).then_inc(tanh_ready, 1)
            nc.scalar.activation(qb_scaled[:, :], w("q_b"), ACT.Copy, scale=HD ** -0.5).then_inc(tanh_ready, 1)
            act.wait_ge(g0_mm, 1)
            nc.scalar.activation(G0[:, :, :], tiles(0, 0), ACT.Copy).then_inc(g0_ready, 1)
            act.wait_ge(tanh_ready, 2)
            act.wait_ge(consts_made, CONSTS)

            with act.Fori(0, PAIRS) as i:
                def columns(s, k, scale=None, bias=None):
                    act.wait_ge(*xT_mm[s].at(i, k))
                    if scale is None:
                        last = nc.scalar.activation(XT[s][:, :, :], tiles(s, 0), ACT.Copy)
                    else:
                        for c in range(C):
                            last = nc.scalar.activation(XT[s][:, c, :], tiles(s, 0)[:, c, :], ACT.Identity,
                                                        scale=w(scale)[:, c:c + 1], bias=w(bias)[:, c:c + 1])
                    last.then_inc(xT_ready[s].sem, 1)

                def a_first(s):
                    columns(s, LN_A)
                    act.wait_ge(*va_mm[s].at(i, 1))
                    act.wait_ge(*stored[s].at(i, 16))
                    nc.scalar.activation(VA[s][:, :, :], tiles(s, 3), ACT.Copy).then_inc(va_ready[s].sem, 1)

                def a_query(s):
                    act.wait_ge(*qa_mm[s].at(i, 1))
                    nc.scalar.activation(QT[s][:, :, :], tiles(s, 1), ACT.Copy, scale=A_SCALE).then_inc(qa_ready[s].sem, 1)
                    act.wait_ge(*kt_mm[s].at(i, 1))
                    for c in range(C):
                        last = nc.scalar.activation(KT[s][:, c, :], tiles(s, 2)[:, c, :], ACT.Identity,
                                                    bias=w("bk")[:, c:c + 1])
                    last.then_inc(kt_ready[s].sem, 1)

                def a_scores(s):
                    act.wait_ge(*nmax_a[s].at(i, 1))
                    for t in range(T):
                        last = nc.scalar.activation(PA[s][:, t, :], PA[s][:, t, :], ACT.Exp,
                                                    bias=nmax[s][:, t:t + 1], accum_out=sums[s][:, t:t + 1])
                    last.then_inc(exp_a[s].sem, 1)

                def a_turn(s):
                    act.wait_ge(*pta_mm[s].at(i, 1))
                    nc.scalar.activation(PTA[s], tiles(s, 1), ACT.Copy).then_inc(pta_ready[s].sem, 1)

                def b_turn(s):
                    columns(s, LN_B)

                def b_gate(s):
                    act.wait_ge(*dp_mm[s].at(i, 1))
                    nc.scalar.activation(HT[s], tiles(s, 1)[:, 0, :], ACT.Relu, bias=w("dp_b1")).then_inc(dp_ready[s].sem, 1)

                def top_weights(s, k, n):
                    act.wait_ge(*top_ready[s].at(i, k))
                    nc.scalar.activation(gw[s][:, :, 0:n], gw[s][:, :, 0:n], ACT.Exp).then_inc(top_exp[s].sem, 1)

                def b_expert(s, e):
                    if e < E0:
                        act.wait_ge(*up_mm[s].at(i, e + 1))
                        if e >= 2:
                            act.wait_ge(*down_mm[s].at(i, e - 1))
                        for h in range(HC0):
                            last = nc.scalar.activation(HID[s][e % 2][:, h, :], PS[s][:, h // 2, (h % 2) * 256:(h % 2 + 1) * 256],
                                                        ACT.Relu, bias=w("eb1")[:, e * HC0 + h:e * HC0 + h + 1])
                        last.then_inc(hid_ready[s].sem, 1)
                    if e == 0:
                        top_weights(s, 1, E0)

                def c_turn(s):
                    columns(s, LN_C)

                def c_query_turn(s):
                    act.wait_ge(*qt_mm[s].at(i, 1))
                    nc.scalar.activation(QT[s][:, :, :], tiles(s, 0), ACT.Copy, scale=C_SCALE).then_inc(qt_ready[s].sem, 1)

                def c_step(s, j):
                    if j < STEPS1:
                        act.wait_ge(*sc_max[s].at(i, j + 1))
                        if j >= 2:
                            act.wait_ge(*pt_mm[s].at(i, j - 1))
                        for h in range(HEADS):
                            k = j * HEADS + h
                            last = nc.scalar.activation(PC[s][j % 2][:, h, :], PS[s][:, h, 0:256], ACT.Exp,
                                                        bias=nmax[s][:, k:k + 1], accum_out=sums[s][:, k:k + 1])
                        last.then_inc(sc_exp[s].sem, 1)

                def kan_turn(s):
                    columns(s, LN_KAN, "ln_g", "ln_b")
                    act.wait_ge(*xT_ready[s].at(i, LN_KAN))
                    y = XT[s][:, :, :].rearrange("p c n -> p (c n)")
                    nc.scalar.activation(SIG[s], y, ACT.Tanh, scale=0.5).then_inc(tanh_half[s].sem, 1)
                    kan_distance(s, 0)

                def kan_distance(s, q):
                    if q >= 2:
                        act.wait_ge(*spline_mm[s].at(i, q - 1))
                    y = XT[s][:, :, :].rearrange("p c n -> p (c n)")
                    for b in range(2):
                        n = 2 * q + b
                        last = nc.scalar.activation(spline_buf(s, q, 0)[:, b, :], y, ACT.Abs, scale=1.0 / GRID_H,
                                                    bias=knot_bias[:, n:n + 1])
                    last.then_inc(distance[s].sem, 1)

                def kan(s, q):
                    if q + 1 < KNOTS // 2:
                        kan_distance(s, q + 1)
                    act.wait_ge(*clipped[s].at(i, q + 1))
                    nc.scalar.activation(spline_buf(s, q, 2), spline_buf(s, q, 1), ACT.Square, scale=(1 / 6) ** 0.5)
                    nc.scalar.activation(spline_buf(s, q, 3), spline_buf(s, q, 0), ACT.Square,
                                         scale=(4 / 6) ** 0.5).then_inc(squares[s].sem, 1)

                def d_turn(s):
                    columns(s, LN_MOA, "ln1_w", "ln1_b")

                def d_kv(s):
                    act.wait_ge(*vd_ready[s].at(i, 1))
                    nc.scalar.activation(KD[s], PS[s][:, 3, 0:256], ACT.Identity, bias=w("k_b")).then_inc(kd_ready[s].sem, 1)
                    top_weights(s, 2, 2)

                def d_queries(s, half):
                    act.wait_ge(*qd_mm[s].at(i, half + 1))
                    for e in range(4):
                        n = half * 4 + e
                        last = nc.scalar.activation(QD[s][:, n, :], PS[s][:, e // 2, (e % 2) * 256:(e % 2 + 1) * 256],
                                                    ACT.Identity, scale=HD ** -0.5, bias=qb_scaled[:, n:n + 1])
                    last.then_inc(qd_ready[s].sem, 1)

                def d_rel(s, t):
                    act.wait_ge(*rel_band[s].at(i, t + 1))
                    r = RELR[s][t]
                    nc.scalar.activation(r[:, :, 0:PADW], r[:, :, PADW:PADW + 1].broadcast_to((P, EA, PADW)), ACT.Copy)
                    nc.scalar.activation(r[:, :, RW - PADW:RW],
                                         r[:, :, RW - PADW - 1:RW - PADW].broadcast_to((P, EA, PADW)), ACT.Copy
                                         ).then_inc(rel_padded[s].sem, 1)
                    for j in range(2):
                        lo, hi = window(2 * t + j)
                        a, b = j * GROUP, (j + 1) * GROUP
                        zlo, zhi, edge = (0, lo, PADW) if lo else (hi, S, RW - PADW - 1)
                        ins = nc.scalar.activation(BS[s][t][a:b, :, zlo:zhi],
                                                   r[a:b, :, edge:edge + 1].broadcast_to((GROUP, EA, zhi - zlo)), ACT.Copy)
                    ins.then_inc(rel_filled[s].sem, 1)

                def d_step(s, j):
                    per_tile = EA // HEADS
                    if j < STEPSA:
                        t, e0 = j // per_tile, (j % per_tile) * HEADS
                        act.wait_ge(*sd_max[s].at(i, j + 1))
                        for h in range(HEADS):
                            k = j * HEADS + h
                            last = nc.scalar.activation(BS[s][t][:, e0 + h, :], BS[s][t][:, e0 + h, :], ACT.Exp,
                                                        bias=nmax[s][:, k:k + 1], accum_out=sums[s][:, k:k + 1])
                        last.then_inc(sd_exp[s].sem, 1)
                    if 2 <= j <= STEPSA + 1:
                        k = j - 2
                        if k == 0:
                            act.wait_ge(*rel_filled[s].at(i, T))
                            for tile in rel_written:
                                act.wait_ge(*tile[s].at(i, 16))
                        act.wait_ge(*cx_mm[s].at(i, k + 1))
                        nc.scalar.activation(CTX[s][k % 2], PS[s][:, 2, 0:256].rearrange("p (h q) -> p h q", h=HEADS),
                                             ACT.Copy).then_inc(cx_ready[s].sem, 1)

                def f_turn(s):
                    columns(s, LN_FF, "ln2_w", "ln2_b")

                def f_gate(s):
                    top_weights(s, 3, 2)

                def f_experts(s, g):
                    if g < EF // FG:
                        act.wait_ge(*fu_mm[s].at(i, g + 1))
                        if g >= 2:
                            act.wait_ge(*fd_mm[s].at(i, (g - 1) * FG))
                        for e in range(FG):
                            n = g * FG + e
                            last = nc.scalar.activation(HID[s][g % 2][:, e, :], PS[s][:, e // 2, (e % 2) * 256:(e % 2 + 1) * 256],
                                                        ACT.Relu, bias=w("ff_b1")[:, n:n + 1])
                        last.then_inc(fh_ready[s].sem, 1)

                take_turns({"a_first": a_first, "a_query": a_query, "a_scores": a_scores, "a_turn": a_turn, "b_turn": b_turn, "b_gate": b_gate, "b_expert": b_expert, "c_turn": c_turn, "c_query_turn": c_query_turn, "c_step": c_step, "kan_turn": kan_turn, "kan": kan, "d_turn": d_turn, "d_kv": d_kv, "d_queries": d_queries, "d_rel": d_rel, "d_step": d_step, "f_turn": f_turn, "f_gate": f_gate, "f_experts": f_experts})

        @block.vector
        def _(dve):
            chained = [0]
            rnd = [None]

            def keep(ins):
                chained[0] += 1
                return ins.then_inc(dve_chain.sem, 1)

            def settle():
                dve.wait_ge(*dve_chain.at(rnd[0], chained[0]))

            def apart():
                v.memset(spare[0:1, 0:1], 0.0)

            v = nc.vector
            for k in range(E0):
                v.memset(thresholds[:, k:k + 1], K_THRESHOLDS[k]).then_inc(consts_made, 1)
            for k in range(KNOTS):
                v.memset(knot_bias[:, k:k + 1], 1.0 / GRID_H - (k - 1)).then_inc(consts_made, 1)
            dve.wait_ge(consts_made, CONSTS - 1)
            v.tensor_copy(iota_f[:, :], iota_u[:, :]).then_inc(consts_made, 1)
            dve.wait_ge(consts_made, CONSTS)
            dve.wait_ge(spline_in, 32)
            for c in range(C):
                for b in range(KNOTS):
                    ins = v.tensor_tensor(SW[:, c, b, :], SW[:, c, b, :], scaler[:, c, :], ALU.mult)
            ins.then_inc(spline_ready, 1)
            dve.wait_ge(spline_ready, 1)
            dve.wait_ge(tanh_ready, 2)
            dve.wait_ge(weights_in, 16 * NWEIGHT_DMAS)

            with dve.Fori(0, PAIRS) as i:
                rnd[0] = i
                chained[0] = 0
                normed = [0, 0]

                def layernorm(s, dst, src):
                    settle()
                    apart()
                    for t in range(T):
                        ins = keep(v.bn_stats(st[s][:, t, :], src[:, t, :]))
                    settle()
                    apart()
                    for t in range(T):
                        ins = keep(v.bn_aggr(mv[s][:, t, :], st[s][:, t, :]))
                    settle()
                    v.tensor_scalar(rstd[s][:, :], mv[s][:, :, 1], EPS, None, ALU.add).then_inc(moments_ready[s].sem, 1)
                    normed[s] += 1
                    dve.wait_ge(*rstd_ready[s].at(i, normed[s]))
                    for t in range(T):
                        ins = v.tensor_scalar(dst[:, t, :], src[:, t, :], mv[s][:, t, 0:1], rstd[s][:, t:t + 1],
                                              ALU.subtract, ALU.mult)
                        if t < T - 1:
                            keep(ins)
                    return ins

                def a_norm(s):
                    dve.wait_ge(*x_loaded[s].at(i, 16))
                    layernorm(s, XN[s], XIN[s]).then_inc(xn_ready[s].sem, 1)
                    dve.wait_ge(*mask_loaded[s].at(i, 16))
                    keep(v.tensor_scalar(NM[s], MASK[s][:, :, :], 0.0, BIG, ALU.not_equal, ALU.mult)
                         )
                    settle()
                    v.tensor_scalar(NM[s], NM[s], MASKED, None, ALU.add).then_inc(mask_used[s].sem, 1)

                def a_scores(s):
                    dve.wait_ge(*mask_used[s].at(i, 1))
                    dve.wait_ge(*sa_mm[s].at(i, 1))
                    keep(v.tensor_tensor(PA[s], tiles(s, 0), NM[s], ALU.min))
                    settle()
                    v.tensor_reduce(nmax[s][:, 0:T], PA[s], AX_X, ALU.max, negate=True).then_inc(nmax_a[s].sem, 1)

                def a_turn(s):
                    dve.wait_ge(*vc_mm[s].at(i, 1))
                    for t in range(T):
                        ins = v.tensor_tensor(VC[s][:, t, :], tiles(s, 3)[:, t, :], row("bv"), ALU.add)
                    ins.then_inc(vc_ready[s].sem, 1)
                    dve.wait_ge(*exp_a[s].at(i, 1))
                    keep(v.reciprocal(fac[s][:, 0:T], sums[s][:, 0:T]))
                    settle()
                    keep(v.tensor_scalar(fac[s][:, 0:T], fac[s][:, 0:T], TG[:, 0:1], None, ALU.mult))

                def a_values(s):
                    settle()
                    dve.wait_ge(*pva_mm[s].at(i, 1))
                    for t in range(T):
                        ins = v.scalar_tensor_tensor(X[s][:, t, :], tiles(s, 2)[:, t, :], fac[s][:, t:t + 1],
                                                     XIN[s][:, t, :], ALU.mult, ALU.add)
                    ins.then_inc(xin_used[s].sem, 1)
                    dve.wait_ge(*xin_used[s].at(i, 1))
                    layernorm(s, XN[s], X[s]).then_inc(xn_ready[s].sem, 1)

                def best(s, k, n, r, bias=None):
                    bank = {1: 3, 2: 2, 3: 3}[k]
                    dve.wait_ge(*logits_mm[s].at(i, k))
                    if bias is None:
                        keep(v.tensor_copy(LG[s][:, :, 0:n], tiles(s, bank)[:, :, 0:n]))
                    else:
                        keep(v.tensor_tensor(LG[s][:, :, 0:n], tiles(s, bank)[:, :, 0:n],
                                             bias.rearrange("p (a e) -> p a e", a=1).broadcast_to((P, T, n)), ALU.add))
                    wide = max(n, 8)
                    if n < wide:
                        keep(v.memset(LG[s][:, :, n:wide], -BIG))
                    settle()
                    apart()
                    for t in range(T):
                        keep(v.max(top[s][:, t, :], LG[s][:, t, 0:wide]))
                    settle()
                    apart()
                    for t in range(T):
                        keep(v.max_index(topi[s][:, t, :], top[s][:, t, :], LG[s][:, t, 0:wide]))
                    v.tensor_tensor(gw[s][:, :, 0:r], top[s][:, :, 0:r], top[s][:, :, 0:1].broadcast_to((P, T, r)),
                                    ALU.subtract).then_inc(top_ready[s].sem, 1)
                    settle()
                    keep(v.tensor_copy(topf[s][:, :, 0:r], topi[s][:, :, 0:r]))

                def spread(s, k, n, r, scale=None):
                    dve.wait_ge(*top_exp[s].at(i, k))
                    if k == 1:
                        keep(v.tensor_tensor(gw[s][:, :, 0:r], gw[s][:, :, 0:r], gsel[s][:, :, 0:r], ALU.mult))
                        settle()
                    keep(v.tensor_reduce(gs[s][:, :], gw[s][:, :, 0:r], AX_X, ALU.add))
                    settle()
                    keep(v.reciprocal(gs[s][:, :], gs[s][:, :]))
                    settle()
                    keep(v.tensor_tensor(gw[s][:, :, 0:r], gw[s][:, :, 0:r],
                                         gs[s][:, :].rearrange("p (t a) -> p t a", a=1).broadcast_to((P, T, r)), ALU.mult))
                    for t in range(T):
                        sel = gsel[s][:, t, 0:n * r].rearrange("p (e r) -> p e r", e=n)
                        keep(v.tensor_tensor(sel, iota_f[:, 0:n].rearrange("p (e a) -> p e a", a=1).broadcast_to((P, n, r)),
                                             topf[s][:, t, 0:r].rearrange("p (a r) -> p a r", a=1).broadcast_to((P, n, r)),
                                             ALU.is_equal))
                    settle()
                    for t in range(T):
                        sel = gsel[s][:, t, 0:n * r].rearrange("p (e r) -> p e r", e=n)
                        keep(v.tensor_tensor(sel, sel, gw[s][:, t, 0:r].rearrange("p (a r) -> p a r", a=1)
                                             .broadcast_to((P, n, r)), ALU.mult))
                    settle()
                    ins = v.tensor_reduce(gates[s][:, :, 0:n],
                                          gsel[s][:, :, 0:n * r].rearrange("p t (e r) -> p t e r", e=n), AX_X, ALU.add)
                    if scale is None:
                        ins.then_inc(gates_ready[s].sem, 1)
                    else:
                        keep(ins)
                        settle()
                        v.tensor_scalar(gates[s][:, :, 0:n], gates[s][:, :, 0:n], scale, None,
                                        ALU.mult).then_inc(gates_ready[s].sem, 1)

                def b_gate(s):
                    best(s, 1, E0, E0, row("gate_b"))

                def gates_to_columns(s, k, n):
                    dve.wait_ge(*gT_mm[s].at(i, k))
                    v.tensor_copy(gT[s][0:n, :, :], PS[s][0:n, 3, 0:T * P].rearrange("p (t q) -> p t q", t=T)
                                  ).then_inc(gT_ready[s].sem, 1)

                def add_bias(s, k, acc):
                    dve.wait_ge(*bias_mm[s].at(i, k))
                    ins = v.tensor_tensor(acc[:, :, :], acc[:, :, :], tiles(s, 3), ALU.add)
                    ins.then_inc(bias_added[s].sem, 1)
                    dve.wait_ge(*bias_added[s].at(i, k))

                def b_expert(s, e):
                    if e == 0:
                        dve.wait_ge(*z_mm[s].at(i, 1))
                        keep(v.tensor_scalar(zk[s][:, :], tiles(s, 3)[:, :, E0], row("dp_b2"), None, ALU.add))
                        settle()
                        for t in range(T):
                            keep(v.tensor_scalar(gsel[s][:, t, 0:E0], thresholds[:, :], zk[s][:, t:t + 1], None, ALU.is_le))
                        settle()
                        spread(s, 1, E0, E0, TG[:, 2:3])
                        dve.wait_ge(*gates_ready[s].at(i, 1))
                    if e == 2:
                        gates_to_columns(s, 1, E0)
                    if e == 3:
                        dve.wait_ge(*down_added[s].at(i, e - 1))
                        add_bias(s, 1, X[s])
                    if e:
                        dve.wait_ge(*down_mm[s].at(i, e))
                        if e > 1:
                            dve.wait_ge(*down_added[s].at(i, e - 1))
                        for t in range(T):
                            ins = v.scalar_tensor_tensor(X[s][:, t, :], tiles(s, 2)[:, t, :], gates[s][:, t, e - 1:e],
                                                         X[s][:, t, :], ALU.mult, ALU.add)
                        ins.then_inc(down_added[s].sem, 1)

                def c_norm(s):
                    dve.wait_ge(*down_added[s].at(i, E0))
                    layernorm(s, XN[s], X[s]).then_inc(xn_ready[s].sem, 1)

                def c_query(s):
                    dve.wait_ge(*qr_mm[s].at(i, 1))
                    for t in range(T):
                        ins = v.tensor_tensor(QR[s][:, t, :], tiles(s, 1)[:, t, :], row("bq"), ALU.add)
                    ins.then_inc(qr_ready[s].sem, 1)

                def c_step(s, j):
                    if j < STEPS1:
                        dve.wait_ge(*sc_mm[s].at(i, j + 1))
                        v.tensor_reduce(nmax[s][:, j * HEADS:(j + 1) * HEADS], PS[s][:, 0:HEADS, 0:256], AX_X, ALU.max,
                                        negate=True).then_inc(sc_max[s].sem, 1)
                    if 1 <= j <= STEPS1:
                        k = j - 1
                        dve.wait_ge(*pt_mm[s].at(i, k + 1))
                        if k >= 2:
                            dve.wait_ge(*pv_mm[s].at(i, k - 1))
                        v.tensor_copy(PTG[s][k % 2].rearrange("p h c q -> p (h c q)"), PS[s][:, 2, :]
                                      ).then_inc(pt_ready[s].sem, 1)

                def kan_norm(s):
                    dve.wait_ge(*sc_exp[s].at(i, STEPS1))
                    keep(v.reciprocal(fac[s][:, :], sums[s][:, :]))
                    settle()
                    dve.wait_ge(*pv_mm[s].at(i, STEPS1))
                    for t in range(T):
                        keep(v.tensor_tensor(XN[s][:, t, :].rearrange("p (h d) -> p h d", h=H1),
                                             tiles(s, 3)[:, t, :].rearrange("p (h d) -> p h d", h=H1),
                                             fac[s][:, t * H1:(t + 1) * H1].rearrange("p (h a) -> p h a", a=1)
                                             .broadcast_to((P, H1, HD1)), ALU.mult))
                    settle()
                    keep(v.tensor_tensor(QR[s][:, :, :], QR[s][:, :, :], XN[s][:, :, :], ALU.add))
                    layernorm(s, XN[s], QR[s]).then_inc(xn_ready[s].sem, 1)

                def kan_silu(s):
                    dve.wait_ge(*tanh_half[s].at(i, 1))
                    keep(v.tensor_scalar(SIG[s], SIG[s], 0.5, 0.5, ALU.mult, ALU.add))
                    settle()
                    v.tensor_tensor(SILU[s], SIG[s], XT[s][:, :, :].rearrange("p c n -> p (c n)"),
                                    ALU.mult).then_inc(silu_ready[s].sem, 1)
                    kan_clip(s, 0)

                def kan_clip(s, q):
                    dve.wait_ge(*distance[s].at(i, q + 1))
                    u, far = spline_buf(s, q, 0), spline_buf(s, q, 1)
                    keep(v.tensor_scalar(far, u, -2.0, 0.0, ALU.add, ALU.min))
                    v.tensor_scalar(u, u, -1.0, 0.0, ALU.add, ALU.min).then_inc(clipped[s].sem, 1)

                def kan(s, q):
                    if q + 1 < KNOTS // 2:
                        kan_clip(s, q + 1)
                    u, far, near2 = (spline_buf(s, q, k) for k in (0, 1, 3))
                    dve.wait_ge(*squares[s].at(i, q + 1))
                    keep(v.tensor_tensor(near2, near2, u, ALU.mult))
                    settle()
                    dve.wait_ge(*far_cube[s].at(i, q + 1))
                    v.tensor_tensor(near2, near2, far, ALU.subtract).then_inc(spline_made[s].sem, 1)

                def d_source(s):
                    dve.wait_ge(*spline_mm[s].at(i, 4))
                    for t in range(T):
                        keep(v.scalar_tensor_tensor(X[s][:, t, :], PS[s][:, 1 + t, 0:256], TG[:, 1:2], X[s][:, t, :],
                                                    ALU.mult, ALU.add))
                    keep(layernorm(s, QR[s], X[s]))

                def d_norm(s):
                    layernorm(s, XN[s], QR[s]).then_inc(xn_ready[s].sem, 1)

                def d_kv(s):
                    dve.wait_ge(*kv_mm[s].at(i, 1))
                    v.tensor_tensor(VD[s], PS[s][:, 3, 256:512].rearrange("p (c h) -> p c h", c=C),
                                    row("v_b").rearrange("p (a h) -> p a h", a=1).broadcast_to((P, C, HD)),
                                    ALU.add).then_inc(vd_ready[s].sem, 1)
                    best(s, 2, EA, 2)

                def d_gates(s):
                    spread(s, 2, EA, 2)
                    dve.wait_ge(*gates_ready[s].at(i, 2))

                def d_rel(s, t):
                    dve.wait_ge(*rel_mm[s].at(i, t + 1))
                    v.tensor_copy(RELR[s][t][:, :, PADW:PADW + REL],
                                  PS[s][:, :, :].rearrange("p b (h n) -> p (b h) n", h=2)[:, :, 0:REL]
                                  ).then_inc(rel_band[s].sem, 1)

                def d_step(s, j):
                    per_tile = EA // HEADS
                    if 1 <= j <= STEPSA:
                        n = j - 1
                        t, e0 = n // per_tile, (n % per_tile) * HEADS
                        k = n * HEADS
                        dve.wait_ge(*sd_exp[s].at(i, n + 1))
                        keep(v.reciprocal(fac[s][:, k:k + HEADS], sums[s][:, k:k + HEADS]))
                        settle()
                        for h in range(HEADS):
                            ins = v.tensor_scalar(BS[s][t][:, e0 + h, :], BS[s][t][:, e0 + h, :], fac[s][:, k + h:k + h + 1],
                                                  gates[s][:, t, e0 + h:e0 + h + 1], ALU.mult, ALU.mult)
                        ins.then_inc(pd_ready[s].sem, 1)
                    if j < STEPSA:
                        t, e0 = j // per_tile, (j % per_tile) * HEADS
                        if j % per_tile == 0:
                            dve.wait_ge(*bias_in[t][s].at(i, 32))
                            dve.wait_ge(*rel_filled[s].at(i, t + 1))
                        dve.wait_ge(*sd_mm[s].at(i, j + 1))
                        apart()
                        for h in range(HEADS):
                            k = j * HEADS + h
                            keep(v.tensor_tensor_reduce(BS[s][t][:, e0 + h, :], tiles(s, 0)[:, h, :], BS[s][t][:, e0 + h, :],
                                                        1.0, -BIG, ALU.add, ALU.max, nmax[s][:, k:k + 1]))
                        settle()
                        k = j * HEADS
                        v.tensor_scalar(nmax[s][:, k:k + HEADS], nmax[s][:, k:k + HEADS], -1.0, None,
                                        ALU.mult).then_inc(sd_max[s].sem, 1)
                    if 1 <= j <= STEPSA:
                        n = j - 1
                        dve.wait_ge(*ptd_mm[s].at(i, n + 1))
                        if n >= 2:
                            dve.wait_ge(*cx_mm[s].at(i, n - 1))
                        v.tensor_copy(PTG[s][n % 2].rearrange("p h c q -> p (h c q)"), PS[s][:, 1, :]
                                      ).then_inc(ptd_ready[s].sem, 1)

                def d_out(s):
                    dve.wait_ge(*od_mm[s].at(i, T))
                    for t in range(T):
                        v.tensor_tensor(QR[s][:, t, :], QR[s][:, t, :], tiles(s, 3)[:, t, :],
                                        ALU.add).then_inc(od_added[s].sem, 1)

                def d_gate_columns(s):
                    gates_to_columns(s, 2, EA)

                def f_norm(s):
                    dve.wait_ge(*od_added[s].at(i, T))
                    add_bias(s, 2, QR[s])
                    layernorm(s, XN[s], QR[s]).then_inc(xn_ready[s].sem, 1)

                def f_gate(s):
                    best(s, 3, EF, 2)

                def f_gates(s):
                    spread(s, 3, EF, 2)
                    dve.wait_ge(*gates_ready[s].at(i, 3))

                def f_experts(s, g):
                    if g == 0:
                        gates_to_columns(s, 3, EF)
                        return
                    if g == 1:
                        add_bias(s, 3, QR[s])
                    for e in range(FG):
                        n = (g - 1) * FG + e
                        dve.wait_ge(*fd_mm[s].at(i, n + 1))
                        if n:
                            dve.wait_ge(*fd_added[s].at(i, n))
                        for t in range(T):
                            ins = v.scalar_tensor_tensor(QR[s][:, t, :], tiles(s, 2 + n % 2)[:, t, :],
                                                         gates[s][:, t, n:n + 1], QR[s][:, t, :], ALU.mult, ALU.add)
                        ins.then_inc(fd_added[s].sem, 1)

                def finish(s):
                    dve.wait_ge(*fd_added[s].at(i, EF))
                    v.scalar_tensor_tensor(VA[s][:, :, :], QR[s][:, :, :], TG[:, 3:4], X[s][:, :, :],
                                           ALU.mult, ALU.add).then_inc(out_ready[s].sem, 1)

                take_turns({"a_norm": a_norm, "a_scores": a_scores, "a_turn": a_turn, "a_values": a_values, "b_gate": b_gate, "b_expert": b_expert, "c_norm": c_norm, "c_query": c_query, "c_step": c_step, "kan_norm": kan_norm, "kan_silu": kan_silu, "kan": kan, "d_source": d_source, "d_norm": d_norm, "d_kv": d_kv, "d_gates": d_gates, "d_rel": d_rel, "d_step": d_step, "d_out": d_out, "d_gate_columns": d_gate_columns, "f_norm": f_norm, "f_gate": f_gate, "f_gates": f_gates, "f_experts": f_experts, "finish": finish})
            assert chained[0] == CHAIN["dve"], chained[0]


CONSTS = E0 + KNOTS + 1 + 1


def kernel(**inputs):
    import numpy as np
    import concourse.bacc as bacc
    from concourse import mybir as _mybir
    from concourse.bass_utils import run_bass_kernel_spmd

    a = {k: np.ascontiguousarray(v) for k, v in inputs.items()}

    def chunks(m):
        r, n = m.shape
        return m.reshape(r // P, P, n).transpose(1, 0, 2).reshape(P, -1)

    def column(v):
        return v.reshape(-1, P).T

    parts = {
        "wq0": chunks(a["L0_xattn_Wq"]), "wk0": chunks(a["L0_xattn_Wk"]), "wv0": chunks(a["L0_xattn_Wv"].T),
        "dp_w1": chunks(a["L0_ffn_dp_w1"]), "dp_w2": a["L0_ffn_dp_w2"], "gate_w": chunks(a["L0_ffn_gate_w"]),
        "wq": chunks(a["L1_xattn_wq"].T), "wk": chunks(a["L1_xattn_wk"].T), "wv": chunks(a["L1_xattn_wv"].T),
        "base": chunks(a["L1_xattn_kan_base_w"].T),
        "q_w": np.concatenate([chunks(m) for m in a["L1_ffn_q_w"]], 1),
        "k_w": chunks(a["L1_ffn_k_w"]), "v_w": chunks(a["L1_ffn_v_w"]),
        "o_w": np.concatenate(list(a["L1_ffn_o_w"]), 1), "rel": a["L1_ffn_rel_table"].T,
        "agate": chunks(a["L1_ffn_attn_gate_w"]), "fgate": chunks(a["L1_ffn_ff_gate_w"]),
        "dp_b1": column(a["L0_ffn_dp_b1"]), "eb1": column(a["L0_ffn_eb1"]), "bk": column(a["L1_xattn_bk"]),
        "ln_g": column(a["L1_xattn_ln_g"]), "ln_b": column(a["L1_xattn_ln_b"]),
        "ln1_w": column(a["L1_ffn_ln1_w"]), "ln1_b": column(a["L1_ffn_ln1_b"]),
        "ln2_w": column(a["L1_ffn_ln2_w"]), "ln2_b": column(a["L1_ffn_ln2_b"]),
        "q_b": column(a["L1_ffn_q_b"]), "k_b": column(a["L1_ffn_k_b"]), "ff_b1": column(a["L1_ffn_ff_b1"]),
    }
    packed = np.concatenate([parts[name] for name in PACK], 1)
    row_parts = {
        "bq": a["L1_xattn_bq"], "bv": a["L1_xattn_bv"], "v_b": a["L1_ffn_v_b"], "gate_b": a["L0_ffn_gate_b"],
        "dp_b2": a["L0_ffn_dp_b2"], "g": np.stack([a["g_xattn"], a["g_ffn"]]).reshape(-1),
    }
    unit_list = [np.concatenate([chunks(w1), chunks(w2)], 1) for w1, w2 in zip(a["L0_ffn_ew1"], a["L0_ffn_ew2"])]
    for g in range(EF // FG):
        es = range(g * FG, (g + 1) * FG)
        unit_list.append(np.concatenate([chunks(a["L1_ffn_ff_w1"][e]) for e in es] + [a["L1_ffn_ff_w2"][e] for e in es], 1))
    spline = a["L1_xattn_kan_spline_w"].transpose(1, 2, 0).reshape(D, KNOTS * D)
    arrays = {
        "x_in": a["x"], "ctx_t": a["ctx_1024"].transpose(0, 2, 1), "mask": a["mask_BxSxS2_ik0"],
        "packed": packed, "rows": np.concatenate([row_parts[name] for name in ROWS]),
        "bias_e": a["L0_ffn_eb2"], "bias_o": a["L1_ffn_o_b"], "bias_f": a["L1_ffn_ff_b2"],
        "spline_w": chunks(spline), "spline_s": chunks(a["L1_xattn_kan_spline_scaler"].T),
        "units": np.stack(unit_list), "ident": np.eye(P, dtype=np.float32),
    }
    arrays = {k: np.ascontiguousarray(v) for k, v in arrays.items()}
    nc = bacc.Bacc("TRN2", target_bir_lowering=False, num_devices=1)
    args = [nc.dram_tensor(f"in_{k}", v.shape, _mybir.dt.from_np(v.dtype), kind="ExternalInput").ap()
            for k, v in arrays.items()]
    args.append(nc.dram_tensor("out_0", (B, S, D), _mybir.dt.float32, kind="ExternalOutput").ap())
    build_program(nc, *args)
    r = run_bass_kernel_spmd(nc, [{f"in_{k}": v for k, v in arrays.items()}], core_ids=[0])
    return r.results[0]["out_0"]
```

```python
from contextlib import ExitStack

import numpy as np

import concourse.bass as bass
from concourse import mybir

F32 = mybir.dt.float32
I32 = mybir.dt.int32
U32 = mybir.dt.uint32
ALU = mybir.AluOpType
ACT = mybir.ActivationFunctionType
AX_X = mybir.AxisListType.X

P = 128
B, S, D = 8, 256, 256
T = S // P
C = D // P
STREAMS = 2
PAIRS = B // STREAMS
EPS = 1e-5
BIG = 3.0e38

A_SCALE = 1.0 / 16.0
MASKED = -1.0e10 * A_SCALE

E0, H0 = 4, 512
HC0 = H0 // P
K_THRESHOLDS = [-BIG] + [float(np.log(np.expm1(0.5 + 1.5 * (r - 0.5) / 3))) for r in range(1, E0)]

H1, HD1 = 8, 32
C_SCALE = D ** -0.5
KNOTS = 8
GRID_H = 2.0 / 5

EA, HD = 8, 128
MAXP = 64
REL = 2 * MAXP + 1
PADW = MAXP - 1
RW = REL + 2 * PADW
GROUP = 64
EF, FH = 16, 128
FG = 4

HEADS = 2
STEPS1 = T * H1 // HEADS
STEPSA = T * EA // HEADS

W1_COLS, W2_COLS = C * H0, HC0 * D
SLOTS = 3
UNITS = E0 + EF // FG
SLOT_USES = [len(range(k, UNITS, SLOTS)) for k in range(SLOTS)]

PACK = {}
_at = 0
for _name, _n in (("wq0", C * 256), ("wk0", C * 256),
                  ("wv0", C * 256), ("wk", C * 256), ("wv", C * 256), ("dp_w1", C * 128), ("dp_w2", 1),
                  ("gate_w", C * E0), ("dp_b1", 1), ("eb1", E0 * HC0), ("bk", C), ("ln_g", C), ("ln_b", C),
                  ("ln1_w", C), ("ln1_b", C), ("ln2_w", C), ("ln2_b", C), ("q_b", EA), ("k_b", 1),
                  ("ff_b1", EF),
                  ("wq", C * 256), ("base", C * 256), ("q_w", EA * C * HD), ("k_w", C * HD),
                  ("v_w", C * HD), ("o_w", EA * 256), ("rel", REL), ("agate", C * EA), ("fgate", C * EF)):
    PACK[_name] = (_at, _n)
    _at += _n
NPACK = _at
LATE = PACK["wq"][0]
NRAW0 = 2 * C * 256

ROWS = {}
_at = 0
for _name, _n in (("bq", 256), ("bv", 256), ("v_b", HD), ("gate_b", E0), ("dp_b2", 1), ("g", 4)):
    ROWS[_name] = (_at, _n)
    _at += _n
NROWS = _at

CHAIN = {"dve_start": 12, "dve": 242}

LN_A, LN_B, LN_C, LN_KAN, LN_MOA, LN_FF = range(1, 7)


class Signal:

    def __init__(self, sem, per, before=0):
        self.sem, self.per, self.before = sem, per, before

    def at(self, i, k):
        return self.sem, i * self.per + (self.before + k)


STEPS = (
    [(name, ()) for name in ("a_first", "a_query", "a_scores", "a_turn", "a_values", "b_turn", "b_gate")]
    + [("b_expert", (e,)) for e in range(E0 + 1)]
    + [(name, ()) for name in ("c_norm", "c_turn", "c_query", "c_query_turn")]
    + [("c_step", (j,)) for j in range(STEPS1 + 2)]
    + [(name, ()) for name in ("c_result_turn", "kan_norm", "kan_turn", "kan_silu")]
    + [("kan", (q,)) for q in range(KNOTS // 2)]
    + [(name, ()) for name in ("d_source", "d_norm", "d_turn", "d_kv")]
    + [("d_queries", (h,)) for h in range(2)]
    + [("d_rel", (0,)), ("d_gates", ()), ("d_rel", (1,))]
    + [("d_step", (j,)) for j in range(STEPSA + 3)]
    + [(name, ()) for name in ("d_out", "d_gate_columns", "d_gate_bias", "f_norm", "f_turn", "f_gate", "f_gates")]
    + [("a_norm", ())] + [("f_experts", (g,)) for g in range(EF // FG + 1)] + [("finish", ())])

TURNS = (
    2, 1, 1, 1, 1, 1, 1, 2, 2, 1, 1, 2, 1, 1, 2, 1, 1, 1, 1, 1, 1, 1, 1, 1, 1, 1, 1, 1, 1, 1, 1, 1,
    1, 1, 1, 1, 1, 1, 1, 1, 1, 2, 1, 1, 3, 3, 2, 2, 1, 1, 1, 1, 2, 1, 2, 3, 3, 1, 1, 1, 2, 1, 1, 2,
    1, 2, 2, 1, 1, 1, 1, 1, 1, 1, 1, 1, 1, 1, 1, 1, 1, 1, 2, 1, 2, 1, 1, 2, 1, 1, 1, 1, 1, 1, 2, 5,
    1, 1, 1, 1, 1, 1, 2, 2)


def schedule():
    order, at = [], [0] * STREAMS
    for n, count in enumerate(TURNS):
        s = n % STREAMS
        order += [(name, args, s) for name, args in STEPS[at[s]:at[s] + count]]
        at[s] += count
    assert at == [len(STEPS)] * STREAMS
    return order


SCHEDULE = schedule()


class StreamSignal:

    def __init__(self, sem, order, stream, before=0):
        self.sem, self.per, self.before = sem, len(order), before
        self.places = [n + 1 for n, s in enumerate(order) if s == stream]

    def at(self, i, k):
        return self.sem, i * self.per + (self.before + self.places[k - 1])

    def previous(self, i, k):
        return self.sem, i * self.per + (self.before - self.per + self.places[k - 1])

    def start(self, i):
        return self.sem, i * self.per + self.before


def step_keys(name, first, end):
    return [(name, (j,)) for j in range(first, end)]


def build_program(nc, x_in, ctx_t, mask, packed, rows, bias_e, bias_o, bias_f, spline_w, spline_s,
                  units, ident_in, out):
    with ExitStack() as ctx:
        def sb(name, shape, dt=F32):
            return ctx.enter_context(nc.sbuf_tensor(name, shape, dt))

        def sem(name):
            return ctx.enter_context(nc.semaphore(name))

        def signal(name, raised_in, before=0):
            keys = [(k, ()) if isinstance(k, str) else k for k in raised_in]
            order = [s for step, args, s in SCHEDULE for key in keys if key == (step, args)]
            one = sem(name)
            return [StreamSignal(one, order, s, before) for s in range(STREAMS)]

        def dma_signal(name, per):
            return [Signal(sem(f"{name}_{s}"), per) for s in range(STREAMS)]

        W = sb("resident", [P, NPACK - NRAW0])
        G0 = sb("g0", [P, C, 256])
        SW = sb("spline_weights", [P, C, KNOTS, 256])
        W1 = [sb(f"w1_slot{k}", [P, W1_COLS]) for k in range(SLOTS)]
        W2 = [sb(f"w2_slot{k}", [P, W2_COLS]) for k in range(SLOTS)]
        ROW = sb("bias_rows", [P, NROWS])
        BE = sb("expert_bias", [E0, 256])
        BO = sb("head_bias", [EA, 256])
        BF = sb("ff_bias", [EF, 256])
        ident = sb("ident", [P, P])
        iota_f = sb("iota_f", [P, EF])
        iota_u = sb("iota_u", [P, EF], I32)
        TG = sb("tanh_g", [P, 4])
        spare = sb("spare", [1, 2])
        minus_half = sb("minus_half", [P, T])
        thresholds = sb("thresholds", [P, E0])
        knot_bias = sb("knot_bias", [P, KNOTS])
        inner_bias = sb("inner_bias", [P, 1])
        qb_scaled = sb("qb_scaled", [P, EA])

        def w(name):
            a, n = PACK[name]
            return W[:, a - NRAW0:a - NRAW0 + n]

        def row(name):
            a, n = ROWS[name]
            return ROW[:, a:a + n]

        wv0 = w("wv0").rearrange("p (c o) -> p c o", c=C)
        dp_w1 = w("dp_w1").rearrange("p (c o) -> p c o", c=C)
        gate_w = w("gate_w").rearrange("p (c o) -> p c o", c=C)
        wq = w("wq").rearrange("p (c o) -> p c o", c=C)
        wk = w("wk").rearrange("p (c o) -> p c o", c=C)
        wv = w("wv").rearrange("p (c o) -> p c o", c=C)
        base = w("base").rearrange("p (c o) -> p c o", c=C)
        q_w = w("q_w").rearrange("p (e c h) -> p e c h", e=EA, c=C)
        k_w = w("k_w").rearrange("p (c h) -> p c h", c=C)
        v_w = w("v_w").rearrange("p (c h) -> p c h", c=C)
        o_w = w("o_w").rearrange("p (e o) -> p e o", e=EA)
        agate = w("agate").rearrange("p (c e) -> p c e", c=C)
        fgate = w("fgate").rearrange("p (c e) -> p c e", c=C)

        def each(name, shape, dt=F32):
            return [sb(f"{name}{s}", shape, dt) for s in range(STREAMS)]

        XIN = each("x_loaded", [P, T, 256])
        CT = each("ctx_columns", [P, C, 256])
        MASK = each("mask", [P, T, 256], I32)
        X = each("x", [P, T, 256])
        XN = each("normed_rows", [P, T, 256])
        XT = each("normed_columns", [P, C, 256])
        QT = each("q_columns", [P, C, 256])
        QR = each("q_rows", [P, T, 256])
        KT = each("k_columns", [P, C, 256])
        VA = each("v_layer0", [P, T, 256])
        VC = each("v_layer1", [P, T, 256])
        BIGB = each("scratch", [P, 5, 2048])
        st = each("bn_stats", [P, T, 6])
        mv = each("mean_var", [P, T, 2])
        rstd = each("rstd", [P, T])
        nmax = each("neg_max", [P, T * EA])
        sums = each("exp_sums", [P, T * EA])
        fac = each("row_factors", [P, T * EA])
        LG = each("logits", [P, T, EF])
        top = each("top8", [P, T, 8])
        topi = each("top8_index", [P, T, 8], U32)
        topf = each("top8_index_f", [P, T, 8])
        gw = each("top_weights", [P, T, E0])
        gs = each("top_sum", [P, T])
        gsel = each("gate_select", [P, T, EF * E0])
        gates = each("gates", [P, T, EF])
        zk = each("k_score", [P, T])
        gT = each("gates_columns", [EF, T, P])

        PA = [BIGB[s][:, 0, 0:512].rearrange("p (t k) -> p t k", t=T) for s in range(2)]
        PTA = [BIGB[s][:, 0, 512:1024].rearrange("p (c q) -> p c q", c=C) for s in range(2)]
        NM = [BIGB[s][:, 0, 1024:1536].rearrange("p (t k) -> p t k", t=T) for s in range(2)]
        HT = [BIGB[s][:, 1, 0:256] for s in range(2)]
        HID = [[BIGB[s][:, 2, 1024 * k:1024 * (k + 1)].rearrange("p (c q) -> p c q", c=4) for k in range(2)]
               for s in range(2)]
        PC = [[BIGB[s][:, 0, 512 * k:512 * (k + 1)].rearrange("p (h k) -> p h k", h=HEADS) for k in range(2)]
              for s in range(2)]
        PTG = [[BIGB[s][:, 1, 512 * k:512 * (k + 1)].rearrange("p (h c q) -> p h c q", h=HEADS, c=C)
                for k in range(2)] for s in range(2)]
        CTX = [[BIGB[s][:, 2, 256 * k:256 * (k + 1)].rearrange("p (h q) -> p h q", h=HEADS)
                for k in range(2)] for s in range(2)]
        SILU = [BIGB[s][:, 4, 0:512] for s in range(2)]
        SIG = [BIGB[s][:, 4, 512:1024] for s in range(2)]

        def spline_buf(s, q, k):
            return BIGB[s][:, k, 1024 * (q % 2):1024 * (q % 2 + 1)].rearrange("p (b n) -> p b n", b=2)

        RELR = [[BIGB[s][:, 1 + t, 0:EA * RW].rearrange("p (e r) -> p e r", e=EA) for t in range(T)]
                for s in range(2)]
        QD = [BIGB[s][:, 0, :].rearrange("p (e q) -> p e q", e=EA) for s in range(2)]
        BS = [[BIGB[s][:, 3 + t, :].rearrange("p (e k) -> p e k", e=EA) for t in range(T)] for s in range(2)]
        KD = [KT[s][:, 0, :] for s in range(2)]
        VD = [VC[s][:, 0, :].rearrange("p (c h) -> p c h", c=C) for s in range(2)]

        PS = [ctx.enter_context(nc.psum_tensor(f"psum{s}", [P, 4, 512], F32)) for s in range(STREAMS)]

        def tiles(s, bank):
            return PS[s][:, bank, :].rearrange("p (t n) -> p t n", t=2)

        rel_dram = nc.dram_tensor("rel_rows", (STREAMS, T, P, EA * RW), F32, kind="Internal").ap()

        raw_in = sem("raw_in")
        early_in = sem("early_in")
        late_in = sem("late_in")
        spline_in = sem("spline_in")
        consts_made = sem("consts_made")
        minus_half_made = sem("minus_half_made")
        g0_mm = sem("g0_mm")
        g0_ready = sem("g0_ready")
        spline_ready = sem("spline_ready")
        tanh_ready = sem("tanh_ready")
        dve_chain = Signal(sem("dve_chain"), CHAIN["dve"], CHAIN["dve_start"])
        w1_in = [Signal(sem(f"w1_in{k}"), 16 * SLOT_USES[k]) for k in range(SLOTS)]
        w2_in = [Signal(sem(f"w2_in{k}"), 16 * SLOT_USES[k]) for k in range(SLOTS)]
        x_loaded = dma_signal("x_loaded", 16)
        ctx_loaded = dma_signal("ctx_loaded", 16)
        mask_loaded = dma_signal("mask_loaded", 16)
        stored = dma_signal("stored", 16)
        rel_written = [dma_signal(f"rel_written_tile{t}", 16) for t in range(T)]
        bias_in = [dma_signal(f"bias_in_tile{t}", 32) for t in range(T)]

        norms = ["a_values", "c_norm", "kan_norm", "d_source", "d_norm", "f_norm", "a_norm"]
        xturns = ["a_first", "b_turn", "c_turn", "kan_turn", "d_turn", "f_turn"]
        moments_ready = signal("moments_ready", norms, STREAMS)
        rstd_ready = signal("rstd_ready", norms, STREAMS)
        xn_ready = signal("xn_ready", [k for k in norms if k != "d_source"], STREAMS)
        xT_mm = signal("xT_mm", xturns)
        xT_ready = signal("xT_ready", xturns)
        xin_used = signal("xin_used", ["a_values"])
        mask_used = signal("mask_used", ["a_norm"], STREAMS)
        va_mm = signal("va_mm", ["a_first"])
        va_ready = signal("va_ready", ["a_first"])
        kt_mm = signal("kt_mm", ["a_query"])
        kt_ready = signal("kt_ready", ["a_query"])
        vc_mm = signal("vc_mm", ["a_turn"])
        vc_ready = signal("vc_ready", ["a_turn"])
        qa_mm = signal("qa_mm", ["a_query"])
        qa_ready = signal("qa_ready", ["a_query"])
        sa_mm = signal("sa_mm", ["a_scores"])
        nmax_a = signal("nmax_a", ["a_scores"])
        exp_a = signal("exp_a", ["a_scores"])
        pta_mm = signal("pta_mm", ["a_turn"])
        pta_ready = signal("pta_ready", ["a_turn"])
        pva_mm = signal("pva_mm", ["a_values"])
        dp_mm = signal("dp_mm", ["b_gate"])
        dp_ready = signal("dp_ready", ["b_gate"])
        logits_mm = signal("logits_mm", ["b_gate", "d_kv", "f_gate"])
        z_mm = signal("z_mm", [("b_expert", (0,))])
        top_ready = signal("top_ready", ["b_gate", "d_kv", "f_gate"])
        top_exp = signal("top_exp", [("b_expert", (0,)), ("d_queries", (1,)), "f_gate"])
        gates_ready = signal("gates_ready", [("b_expert", (0,)), "d_gates", "f_gates"])
        gT_mm = signal("gT_mm", [("b_expert", (2,)), "d_gate_columns", ("f_experts", (0,))])
        gT_ready = signal("gT_ready", [("b_expert", (2,)), "d_gate_columns", ("f_experts", (0,))])
        bias_mm = signal("bias_mm", [("b_expert", (3,)), "d_gate_bias", ("f_experts", (1,))])
        bias_added = signal("bias_added", [("b_expert", (3,)), "f_norm", ("f_experts", (1,))])
        ups = step_keys("b_expert", 0, E0)
        downs = step_keys("b_expert", 1, E0 + 1)
        up_mm = signal("up_mm", ups)
        hid_ready = signal("hid_ready", ups)
        down_mm = signal("down_mm", downs)
        down_added = signal("down_added", downs)
        qr_mm = signal("qr_mm", ["c_query"])
        qr_ready = signal("qr_ready", ["c_query"])
        qt_mm = signal("qt_mm", ["c_query_turn"])
        qt_ready = signal("qt_ready", ["c_query_turn"])
        sc_mm = signal("sc_mm", step_keys("c_step", 0, STEPS1))
        sc_max = signal("sc_max", step_keys("c_step", 0, STEPS1))
        sc_exp = signal("sc_exp", step_keys("c_step", 0, STEPS1))
        pt_mm = signal("pt_mm", step_keys("c_step", 1, STEPS1 + 1))
        pt_ready = signal("pt_ready", step_keys("c_step", 1, STEPS1 + 1))
        pv_mm = signal("pv_mm", step_keys("c_step", 2, STEPS1 + 2))
        pv_copied = signal("pv_copied", ["c_result_turn"])
        pv_turned = signal("pv_turned", ["c_result_turn"])
        silu_ready = signal("silu_ready", ["kan_silu"])
        tanh_half = signal("tanh_half", ["kan_turn"])
        pairs_of_knots = step_keys("kan", 0, KNOTS // 2)
        kan_steps = ["kan_turn", "kan_silu"] + pairs_of_knots[:-2]
        distance = signal("distance", kan_steps)
        kan_steps = ["kan_silu", "kan_silu"] + pairs_of_knots[:-2]
        clipped = signal("clipped", kan_steps)
        kan_steps = ["kan_silu"] + pairs_of_knots[:-1]
        inner_square = signal("inner_square", kan_steps)
        outer_square = signal("outer_square", kan_steps)
        inner_made = signal("inner_made", pairs_of_knots[:-1])
        spline_made = signal("spline_made", kan_steps)
        spline_mm = signal("spline_mm", pairs_of_knots)
        kv_mm = signal("kv_mm", ["d_kv"])
        kd_ready = signal("kd_ready", ["d_kv"])
        vd_ready = signal("vd_ready", ["d_kv"])
        qd_mm = signal("qd_mm", step_keys("d_queries", 0, 2))
        qd_ready = signal("qd_ready", step_keys("d_queries", 0, 2))
        rel_mm = signal("rel_mm", step_keys("d_rel", 0, T))
        rel_band = signal("rel_band", step_keys("d_rel", 0, T))
        rel_padded = signal("rel_padded", step_keys("d_rel", 0, T))
        rel_filled = signal("rel_filled", step_keys("d_rel", 0, T))
        sd_mm = signal("sd_mm", step_keys("d_step", 0, STEPSA))
        sd_max = signal("sd_max", step_keys("d_step", 0, STEPSA))
        sd_exp = signal("sd_exp", step_keys("d_step", 0, STEPSA))
        pd_ready = signal("pd_ready", step_keys("d_step", 1, STEPSA + 1))
        ptd_mm = signal("ptd_mm", step_keys("d_step", 1, STEPSA + 1))
        ptd_ready = signal("ptd_ready", step_keys("d_step", 1, STEPSA + 1))
        cx_mm = signal("cx_mm", step_keys("d_step", 2, STEPSA + 2))
        cx_ready = signal("cx_ready", step_keys("d_step", 2, STEPSA + 2))
        od_mm = signal("od_mm", [("d_step", ((t + 1) * (EA // HEADS) + 2,)) for t in range(T)])
        od_added = signal("od_added", ["d_out"] * T)
        fu_mm = signal("fu_mm", step_keys("f_experts", 0, EF // FG))
        fh_ready = signal("fh_ready", step_keys("f_experts", 0, EF // FG))
        ff_downs = [("f_experts", (g,)) for g in range(1, EF // FG + 1) for _ in range(FG)]
        fd_mm = signal("fd_mm", ff_downs)
        fd_added = signal("fd_added", ff_downs)
        out_ready = signal("out_ready", ["finish"], STREAMS)

        raw = BIGB[0][:, 0, 0:NRAW0].rearrange("p (w c o) -> p w c o", w=2, c=C)
        scaler = BIGB[1][:, 0, 0:C * 256].rearrange("p (c o) -> p c o", c=C)

        def of_heads(buf, j):
            t, h = j // (H1 // HEADS), j % (H1 // HEADS)
            return buf[:, t * H1:(t + 1) * H1].rearrange("p (c h) -> p c h", c=HEADS)[:, :, h]

        def window(g):
            return max(0, g * GROUP - MAXP), min(S, (g + 1) * GROUP + MAXP)

        def take_turns(steps):
            for name, args, s in SCHEDULE:
                if name in steps:
                    step = steps[name]
                    step(s, *args)

        block = ctx.enter_context(nc.Block())

        @block.sync
        def _(sp):
            def load_inputs(n, s):
                sp.dma_start(XIN[s][:, :, :], x_in[n].rearrange("(t p) d -> p t d", p=P)).then_inc(x_loaded[s].sem, 16)
                sp.dma_start(CT[s][:, :, :], ctx_t[n].rearrange("(c p) t -> p c t", p=P)).then_inc(ctx_loaded[s].sem, 16)
                sp.dma_start(MASK[s][:, :, :], mask[n].rearrange("(t p) k -> p t k", p=P)).then_inc(mask_loaded[s].sem, 16)

            def load_w1(u):
                sp.dma_start(W1[u % SLOTS][:, :], units[u, :, 0:W1_COLS]).then_inc(w1_in[u % SLOTS].sem, 16)

            def load_w2(u):
                sp.dma_start(W2[u % SLOTS][:, :], units[u, :, W1_COLS:W1_COLS + W2_COLS]).then_inc(w2_in[u % SLOTS].sem, 16)

            def write_rel(i, s, t):
                sp.wait_ge(*rel_padded[s].at(i, t + 1))
                sp.dma_start(rel_dram[s, t], RELR[s][t].rearrange("p e r -> p (e r)")).then_inc(rel_written[t][s].sem, 16)

            def read_rel(i, s, t):
                sp.wait_ge(*rel_written[t][s].at(i, 16))
                for j in range(2):
                    g = 2 * t + j
                    lo, hi = window(g)
                    first = rel_dram[s, t]
                    off = first.offset + j * GROUP * EA * RW + lo - g * GROUP + RW // 2
                    src = bass.AP(first.tensor, off, [[EA * RW - 1, GROUP], [RW, EA], [1, hi - lo]])
                    sp.dma_start(BS[s][t][j * GROUP:(j + 1) * GROUP, :, lo:hi], src).then_inc(bias_in[t][s].sem, 16)

            def a_round(i, last):
                def reload(u, load, used):
                    if u + SLOTS < UNITS or not last:
                        sp.wait_ge(*used)
                        load(u + SLOTS if u + SLOTS < UNITS else u % SLOTS)

                def b_expert(s, e):
                    if s == STREAMS - 1 and e < E0:
                        reload(e, load_w1, up_mm[s].at(i, e + 1))
                    if s == STREAMS - 1 and e:
                        reload(e - 1, load_w2, down_mm[s].at(i, e))

                def f_experts(s, g):
                    if s == STREAMS - 1 and g < EF // FG:
                        reload(E0 + g, load_w1, fu_mm[s].at(i, g + 1))
                    if s == STREAMS - 1 and g:
                        reload(E0 + g - 1, load_w2, fd_mm[s].at(i, g * FG))

                def c_norm(s):
                    if last:
                        sp.sem_inc(x_loaded[s].sem, 16)
                        sp.sem_inc(mask_loaded[s].sem, 16)
                    else:
                        sp.wait_ge(*xin_used[s].at(i, 1))
                        sp.wait_ge(*vc_mm[s].at(i, 1))
                        load_inputs(2 * i + (STREAMS + s), s)

                def d_rel(s, t):
                    if t:
                        read_rel(i, s, t - 1)
                    write_rel(i, s, t)

                def d_step(s, j):
                    if j == 0:
                        read_rel(i, s, T - 1)

                def finish(s):
                    sp.wait_ge(*out_ready[s].at(i, 1))
                    sp.dma_start(out[2 * i + s].rearrange("(t p) d -> p t d", p=P), VA[s][:, :, :]
                                 ).then_inc(stored[s].sem, 16)

                take_turns({"b_expert": b_expert, "f_experts": f_experts, "c_norm": c_norm, "d_rel": d_rel,
                            "d_step": d_step, "finish": finish})

            sp.dma_start(raw, packed[:, 0:NRAW0].rearrange("p (w c o) -> p w c o", w=2, c=C)).then_inc(raw_in, 16)
            sp.dma_start(scaler, spline_s.rearrange("p (c o) -> p c o", c=C)).then_inc(spline_in, 16)
            sp.dma_start(SW[:, :, :, :], spline_w.rearrange("p (c b o) -> p c b o", c=C, b=KNOTS)).then_inc(spline_in, 16)
            sp.dma_start(ROW[:, :], rows.partition_broadcast(P)).then_inc(early_in, 16)
            sp.dma_start(ident[:, :], ident_in).then_inc(early_in, 16)
            for s in range(STREAMS):
                load_inputs(s, s)
                sp.sem_inc(stored[s].sem, 16)
                if s == 0:
                    sp.dma_start(W[:, 0:LATE - NRAW0], packed[:, NRAW0:LATE]).then_inc(early_in, 16)
                    sp.dma_start(BE[:, :], bias_e).then_inc(early_in, 16)
                    sp.dma_start(BO[:, :], bias_o).then_inc(early_in, 16)
                    sp.dma_start(BF[:, :], bias_f).then_inc(early_in, 16)
            sp.sem_inc(out_ready[0].sem, STREAMS)
            for u in range(SLOTS):
                load_w1(u)
                load_w2(u)
            sp.dma_start(W[:, LATE - NRAW0:NPACK - NRAW0], packed[:, LATE:NPACK]).then_inc(late_in, 16)

            with sp.Fori(0, PAIRS - 1) as i:
                a_round(i, False)
            a_round(PAIRS - 1, True)
            for s in range(STREAMS):
                sp.wait_ge(*stored[s].at(PAIRS, 16))

        EARLY_DMAS = 6

        @block.gpsimd
        def _(pool):
            nc.gpsimd.memset(minus_half[:, :], -0.5).then_inc(minus_half_made, 1)
            pool.wait_ge(minus_half_made, 1)
            nc.gpsimd.iota(iota_u[:, :], pattern=[[1, EF]], base=0, channel_multiplier=0).then_inc(consts_made, 1)
            for s in range(STREAMS):
                pool.wait_ge(moments_ready[s].sem, s + 1)
                nc.gpsimd.tensor_tensor(rstd[s][:, :], rstd[s][:, :], minus_half[:, :], ALU.pow
                                        ).then_inc(rstd_ready[s].sem, 1)
            with pool.Fori(0, PAIRS) as i:
                def kan(s, q):
                    if q + 1 < KNOTS // 2:
                        spline_inner(s, q + 1)

                def spline_inner(s, q):
                    pool.wait_ge(*inner_square[s].at(i, q + 1))
                    pool.wait_ge(*clipped[s].at(i, q + 1))
                    nc.gpsimd.tensor_tensor(spline_buf(s, q, 1), spline_buf(s, q, 0), spline_buf(s, q, 2), ALU.mult
                                            ).then_inc(inner_made[s].sem, 1)

                def power(k):
                    def step(s):
                        pool.wait_ge(*moments_ready[s].at(i, k))
                        nc.gpsimd.tensor_tensor(rstd[s][:, :], rstd[s][:, :], minus_half[:, :], ALU.pow
                                                ).then_inc(rstd_ready[s].sem, 1)
                    return step

                steps = {name: power(k + 1) for k, name in enumerate(norms)}
                take_turns({**steps, "kan": kan})

        @block.tensor
        def _(pe):
            def mm(o, a, b, start=True, stop=True):
                return pe.matmul(o, a, b, start=start, stop=stop)

            def rows_of(o, cols, weights, n):
                for t in range(T):
                    for c in range(C):
                        last = mm(o[:, t, 0:n], cols[:, c, t * P:(t + 1) * P], weights[:, c, :], c == 0, c == C - 1)
                return last

            pe.wait_ge(raw_in, 16)
            for a in range(C):
                for c in range(C):
                    last = mm(tiles(0, 0)[:, a, :], raw[:, 0, c, a * P:(a + 1) * P], raw[:, 1, c, :], c == 0, c == C - 1)
            last.then_inc(g0_mm, 1)
            pe.wait_ge(g0_ready, 1)
            pe.wait_ge(early_in, 16 * EARLY_DMAS)

            with pe.Fori(0, PAIRS) as i:
                def turn(s, k):
                    if k == LN_A:
                        pe.wait_ge(*xn_ready[s].start(i))
                    else:
                        pe.wait_ge(*xn_ready[s].at(i, k - 1))
                    for c in range(C):
                        for t in range(T):
                            last = pe.transpose(tiles(s, 0)[:, c, t * P:(t + 1) * P],
                                                XN[s][:, t, c * P:(c + 1) * P], ident[:, :])
                    last.then_inc(xT_mm[s].sem, 1)

                def a_first(s):
                    pe.wait_ge(*ctx_loaded[s].at(i, 16))
                    pe.wait_ge(*out_ready[s].previous(i, 1))
                    rows_of(tiles(s, 3), CT[s], wv0, 256).then_inc(va_mm[s].sem, 1)
                    turn(s, LN_A)

                def a_query(s):
                    pe.wait_ge(*xT_ready[s].at(i, LN_A))
                    for a in range(C):
                        for c in range(C):
                            last = mm(tiles(s, 1)[:, a, :], G0[:, c, a * P:(a + 1) * P], XT[s][:, c, :], c == 0, c == C - 1)
                    last.then_inc(qa_mm[s].sem, 1)
                    for a in range(C):
                        for c in range(C):
                            last = mm(tiles(s, 2)[:, a, :], wk[:, c, a * P:(a + 1) * P], CT[s][:, c, :], c == 0, c == C - 1)
                    last.then_inc(kt_mm[s].sem, 1)

                def a_scores(s):
                    pe.wait_ge(*qa_ready[s].at(i, 1))
                    rows_of(tiles(s, 0), QT[s], CT[s], 256).then_inc(sa_mm[s].sem, 1)

                def a_turn(s):
                    pe.wait_ge(*va_ready[s].at(i, 1))
                    rows_of(tiles(s, 3), CT[s], wv, 256).then_inc(vc_mm[s].sem, 1)
                    pe.wait_ge(*exp_a[s].at(i, 1))
                    for c in range(C):
                        for t in range(T):
                            last = pe.transpose(tiles(s, 1)[:, c, t * P:(t + 1) * P],
                                                PA[s][:, t, c * P:(c + 1) * P], ident[:, :])
                    last.then_inc(pta_mm[s].sem, 1)

                def a_values(s):
                    pe.wait_ge(*kt_ready[s].at(i, 1))
                    pe.wait_ge(*pta_ready[s].at(i, 1))
                    rows_of(tiles(s, 2), PTA[s], VA[s], 256).then_inc(pva_mm[s].sem, 1)

                def b_turn(s):
                    turn(s, LN_B)

                def b_gate(s):
                    pe.wait_ge(*xT_ready[s].at(i, LN_B))
                    for c in range(C):
                        last = mm(tiles(s, 1)[:, 0, :], dp_w1[:, c, :], XT[s][:, c, :], c == 0, c == C - 1)
                    last.then_inc(dp_mm[s].sem, 1)
                    pe.wait_ge(*vc_ready[s].at(i, 1))
                    rows_of(tiles(s, 3), XT[s], gate_w, E0).then_inc(logits_mm[s].sem, 1)

                def gate_columns(s, k, n):
                    pe.wait_ge(*gates_ready[s].at(i, k))
                    for t in range(T):
                        last = mm(PS[s][0:n, 3, t * P:(t + 1) * P], gates[s][:, t, 0:n], ident[:, :])
                    last.then_inc(gT_mm[s].sem, 1)

                def gate_bias(s, k, n, weights):
                    pe.wait_ge(*gT_ready[s].at(i, k))
                    for t in range(T):
                        last = mm(tiles(s, 3)[:, t, :], gT[s][0:n, t, :], weights[:, :])
                    last.then_inc(bias_mm[s].sem, 1)

                def b_expert(s, e):
                    if e < E0:
                        k = e % SLOTS
                        pe.wait_ge(*w1_in[k].at(i, 16 * (e // SLOTS + 1)))
                        if e:
                            pe.wait_ge(*hid_ready[s].at(i, e))
                        else:
                            pe.wait_ge(*dp_ready[s].at(i, 1))
                        w1 = W1[k][:, :].rearrange("p (c h) -> p c h", c=C)
                        for h in range(HC0):
                            for c in range(C):
                                last = mm(PS[s][:, h // 2, (h % 2) * 256:(h % 2 + 1) * 256],
                                          w1[:, c, h * P:(h + 1) * P], XT[s][:, c, :], c == 0, c == C - 1)
                        last.then_inc(up_mm[s].sem, 1)
                    if e == 0:
                        pe.wait_ge(*top_ready[s].at(i, 1))
                        for t in range(T):
                            last = mm(tiles(s, 3)[:, t, E0:E0 + 1], HT[s][:, t * P:(t + 1) * P], w("dp_w2"))
                        last.then_inc(z_mm[s].sem, 1)
                    if e == 2:
                        gate_columns(s, 1, E0)
                    if e == 3:
                        gate_bias(s, 1, E0, BE)
                    if e:
                        k = (e - 1) % SLOTS
                        pe.wait_ge(*hid_ready[s].at(i, e))
                        if e > 1:
                            pe.wait_ge(*down_added[s].at(i, e - 1))
                        pe.wait_ge(*w2_in[k].at(i, 16 * ((e - 1) // SLOTS + 1)))
                        w2 = W2[k][:, :].rearrange("p (c o) -> p c o", c=HC0)
                        for t in range(T):
                            for c in range(HC0):
                                last = mm(tiles(s, 2)[:, t, :], HID[s][(e - 1) % 2][:, c, t * P:(t + 1) * P],
                                          w2[:, c, :], c == 0, c == HC0 - 1)
                        last.then_inc(down_mm[s].sem, 1)

                def c_turn(s):
                    turn(s, LN_C)

                def c_query(s):
                    pe.wait_ge(*xT_ready[s].at(i, LN_C))
                    pe.wait_ge(late_in, 16)
                    rows_of(tiles(s, 1), XT[s], wq, 256).then_inc(qr_mm[s].sem, 1)

                def c_query_turn(s):
                    pe.wait_ge(*qr_ready[s].at(i, 1))
                    for c in range(C):
                        for t in range(T):
                            last = pe.transpose(tiles(s, 0)[:, c, t * P:(t + 1) * P],
                                                QR[s][:, t, c * P:(c + 1) * P], ident[:, :])
                    last.then_inc(qt_mm[s].sem, 1)

                def c_step(s, j):
                    per_tile = H1 // HEADS
                    if j < STEPS1:
                        t, r = j // per_tile, (j % per_tile) * HD1
                        if j >= 2:
                            pe.wait_ge(*sc_exp[s].at(i, j - 1))
                        else:
                            pe.wait_ge(*qt_ready[s].at(i, 1))
                        for c in range(HEADS):
                            last = mm(tiles(s, j % 2)[:, c, :], QT[s][r:r + HD1, c, t * P:(t + 1) * P],
                                      KT[s][r:r + HD1, c, :])
                        last.then_inc(sc_mm[s].sem, 1)
                    if j >= 2:
                        k = j - 2
                        t, r = k // per_tile, (k % per_tile) * HD1
                        pe.wait_ge(*pt_ready[s].at(i, k + 1))
                        for h in range(HEADS):
                            a = (h * per_tile + k % per_tile) * HD1
                            for c in range(C):
                                last = mm(tiles(s, 3)[r:r + HD1, h, t * P:(t + 1) * P], VC[s][:, c, a:a + HD1],
                                          PTG[s][k % 2][:, h, c, :], c == 0, c == C - 1)
                        last.then_inc(pv_mm[s].sem, 1)
                    if 1 <= j <= STEPS1:
                        k = j - 1
                        pe.wait_ge(*sc_exp[s].at(i, k + 1))
                        if k:
                            pe.wait_ge(*pt_ready[s].at(i, k))
                        for h in range(HEADS):
                            for c in range(C):
                                a = (h * C + c) * P
                                last = pe.transpose(PS[s][:, 2, a:a + P], PC[s][k % 2][:, h, c * P:(c + 1) * P], ident[:, :])
                        last.then_inc(pt_mm[s].sem, 1)

                def c_result_turn(s):
                    pe.wait_ge(*pv_copied[s].at(i, 1))
                    for t in range(T):
                        for c in range(C):
                            last = pe.transpose(tiles(s, 0)[:, t, c * P:(c + 1) * P],
                                                QT[s][:, c, t * P:(t + 1) * P], ident[:, :])
                    last.then_inc(pv_turned[s].sem, 1)

                def kan_turn(s):
                    turn(s, LN_KAN)

                def kan(s, q):
                    if q == 0:
                        pe.wait_ge(*silu_ready[s].at(i, 1))
                        for t in range(T):
                            for c in range(C):
                                a = c * 256 + t * P
                                mm(PS[s][:, 1 + t, 0:256], SILU[s][:, a:a + P], base[:, c, :], c == 0, False)
                    pe.wait_ge(*spline_made[s].at(i, q + 1))
                    for t in range(T):
                        for b in range(2):
                            for c in range(C):
                                a = c * 256 + t * P
                                last = mm(PS[s][:, 1 + t, 0:256], spline_buf(s, q, 3)[:, b, a:a + P],
                                          SW[:, c, 2 * q + b, :], False, q == 3 and b == 1 and c == C - 1)
                    last.then_inc(spline_mm[s].sem, 1)

                def d_turn(s):
                    turn(s, LN_MOA)

                def d_kv(s):
                    pe.wait_ge(*xT_ready[s].at(i, LN_MOA))
                    for c in range(C):
                        mm(PS[s][:, 3, 0:256], k_w[:, c, :], XT[s][:, c, :], c == 0, c == C - 1)
                    for t in range(T):
                        for c in range(C):
                            last = mm(PS[s][:, 3, 256 + t * P:256 + (t + 1) * P], XT[s][:, c, t * P:(t + 1) * P],
                                      v_w[:, c, :], c == 0, c == C - 1)
                    last.then_inc(kv_mm[s].sem, 1)
                    rows_of(tiles(s, 2), XT[s], agate, EA).then_inc(logits_mm[s].sem, 1)

                def d_queries(s, half):
                    if half:
                        pe.wait_ge(*kd_ready[s].at(i, 1))
                        pe.wait_ge(*vd_ready[s].at(i, 1))
                        pe.wait_ge(*top_ready[s].at(i, 2))
                    for e in range(4):
                        for c in range(C):
                            last = mm(PS[s][:, 2 * half + e // 2, (e % 2) * 256:(e % 2 + 1) * 256],
                                      q_w[:, half * 4 + e, c, :], XT[s][:, c, :], c == 0, c == C - 1)
                    last.then_inc(qd_mm[s].sem, 1)

                def d_rel(s, t):
                    if t == 0:
                        pe.wait_ge(*qd_ready[s].at(i, 2))
                    else:
                        pe.wait_ge(*rel_band[s].at(i, t))
                    for e in range(EA):
                        last = mm(PS[s][:, e // 2, (e % 2) * 256:(e % 2) * 256 + REL],
                                  QD[s][:, e, t * P:(t + 1) * P], w("rel"))
                    last.then_inc(rel_mm[s].sem, 1)

                def d_step(s, j):
                    per_tile = EA // HEADS
                    if j < STEPSA:
                        t, e0 = j // per_tile, (j % per_tile) * HEADS
                        if j:
                            pe.wait_ge(*sd_max[s].at(i, j))
                        else:
                            pe.wait_ge(*rel_band[s].at(i, T))
                        for h in range(HEADS):
                            last = mm(tiles(s, 0)[:, h, :], QD[s][:, e0 + h, t * P:(t + 1) * P], KD[s])
                        last.then_inc(sd_mm[s].sem, 1)
                    if 2 <= j <= STEPSA + 1:
                        k = j - 2
                        pe.wait_ge(*ptd_ready[s].at(i, k + 1))
                        if k:
                            pe.wait_ge(*cx_ready[s].at(i, k))
                        for h in range(HEADS):
                            for c in range(C):
                                last = mm(PS[s][:, 2, h * P:(h + 1) * P], VD[s][:, c, :], PTG[s][k % 2][:, h, c, :],
                                          c == 0, c == C - 1)
                        last.then_inc(cx_mm[s].sem, 1)
                    if j >= 3:
                        k = j - 3
                        t, e0 = k // per_tile, (k % per_tile) * HEADS
                        pe.wait_ge(*cx_ready[s].at(i, k + 1))
                        for h in range(HEADS):
                            last = mm(tiles(s, 3)[:, t, :], CTX[s][k % 2][:, h, :], o_w[:, e0 + h, :],
                                      e0 + h == 0, e0 + h == EA - 1)
                        if k % per_tile == per_tile - 1:
                            last.then_inc(od_mm[s].sem, 1)
                    if 1 <= j <= STEPSA:
                        k = j - 1
                        t, e0 = k // per_tile, (k % per_tile) * HEADS
                        pe.wait_ge(*pd_ready[s].at(i, k + 1))
                        if k:
                            pe.wait_ge(*ptd_ready[s].at(i, k))
                        for h in range(HEADS):
                            for c in range(C):
                                a = (h * C + c) * P
                                last = pe.transpose(PS[s][:, 1, a:a + P], BS[s][t][:, e0 + h, c * P:(c + 1) * P], ident[:, :])
                        last.then_inc(ptd_mm[s].sem, 1)

                def d_gate_columns(s):
                    pe.wait_ge(*od_added[s].at(i, T))
                    gate_columns(s, 2, EA)

                def d_gate_bias(s):
                    gate_bias(s, 2, EA, BO)

                def f_turn(s):
                    turn(s, LN_FF)

                def f_gate(s):
                    pe.wait_ge(*xT_ready[s].at(i, LN_FF))
                    rows_of(tiles(s, 3), XT[s], fgate, EF).then_inc(logits_mm[s].sem, 1)

                def f_gate_columns(s):
                    gate_columns(s, 3, EF)

                def f_gate_bias(s):
                    gate_bias(s, 3, EF, BF)

                def f_experts(s, g):
                    if g < EF // FG:
                        u = E0 + g
                        pe.wait_ge(*w1_in[u % SLOTS].at(i, 16 * (u // SLOTS + 1)))
                        if g:
                            pe.wait_ge(*fh_ready[s].at(i, g))
                        w1 = W1[u % SLOTS][:, :].rearrange("p (e c h) -> p e c h", e=FG, c=C)
                    if g == 1:
                        f_gate_bias(s)
                    if g:
                        u = E0 + g - 1
                        pe.wait_ge(*fh_ready[s].at(i, g))
                        pe.wait_ge(*w2_in[u % SLOTS].at(i, 16 * (u // SLOTS + 1)))
                        w2 = W2[u % SLOTS][:, :].rearrange("p (e o) -> p e o", e=FG)
                    for e in range(FG):
                        if g < EF // FG:
                            for c in range(C):
                                last = mm(PS[s][:, e // 2, (e % 2) * 256:(e % 2 + 1) * 256],
                                          w1[:, e, c, :], XT[s][:, c, :], c == 0, c == C - 1)
                            if e == FG - 1:
                                last.then_inc(fu_mm[s].sem, 1)
                        if g:
                            n = (g - 1) * FG + e
                            if n == 1:
                                pe.wait_ge(*bias_added[s].at(i, 3))
                            if n >= 2:
                                pe.wait_ge(*fd_added[s].at(i, n - 1))
                            for t in range(T):
                                last = mm(tiles(s, 2 + n % 2)[:, t, :], HID[s][(g - 1) % 2][:, e, t * P:(t + 1) * P],
                                          w2[:, e, :])
                            last.then_inc(fd_mm[s].sem, 1)
                    if g == 0:
                        f_gate_columns(s)

                take_turns({"a_first": a_first, "a_query": a_query, "a_scores": a_scores, "a_turn": a_turn,
                            "a_values": a_values, "b_turn": b_turn, "b_gate": b_gate, "b_expert": b_expert,
                            "c_turn": c_turn, "c_query": c_query, "c_query_turn": c_query_turn,
                            "c_step": c_step, "c_result_turn": c_result_turn, "kan_turn": kan_turn, "kan": kan,
                            "d_turn": d_turn, "d_kv": d_kv, "d_queries": d_queries, "d_rel": d_rel,
                            "d_step": d_step, "d_gate_columns": d_gate_columns, "d_gate_bias": d_gate_bias,
                            "f_turn": f_turn, "f_gate": f_gate, "f_experts": f_experts})

        @block.scalar
        def _(act):
            chained = [0]

            act.wait_ge(g0_mm, 1)
            nc.scalar.activation(G0[:, :, :], tiles(0, 0), ACT.Copy).then_inc(g0_ready, 1)
            act.wait_ge(early_in, 16 * EARLY_DMAS)
            nc.scalar.activation(TG[:, :], row("g"), ACT.Tanh).then_inc(tanh_ready, 1)
            nc.scalar.activation(qb_scaled[:, :], w("q_b"), ACT.Copy, scale=HD ** -0.5).then_inc(tanh_ready, 1)
            act.wait_ge(tanh_ready, 2)
            act.wait_ge(consts_made, CONSTS)

            with act.Fori(0, PAIRS) as i:
                def columns(s, k, scale=None, bias=None):
                    act.wait_ge(*xT_mm[s].at(i, k))
                    if scale is None:
                        last = nc.scalar.activation(XT[s][:, :, :], tiles(s, 0), ACT.Copy)
                    else:
                        for c in range(C):
                            last = nc.scalar.activation(XT[s][:, c, :], tiles(s, 0)[:, c, :], ACT.Identity,
                                                        scale=w(scale)[:, c:c + 1], bias=w(bias)[:, c:c + 1])
                    last.then_inc(xT_ready[s].sem, 1)

                def a_first(s):
                    columns(s, LN_A)
                    act.wait_ge(*va_mm[s].at(i, 1))
                    act.wait_ge(*stored[s].at(i, 16))
                    nc.scalar.activation(VA[s][:, :, :], tiles(s, 3), ACT.Copy).then_inc(va_ready[s].sem, 1)

                def a_query(s):
                    act.wait_ge(*qa_mm[s].at(i, 1))
                    nc.scalar.activation(QT[s][:, :, :], tiles(s, 1), ACT.Copy, scale=A_SCALE).then_inc(qa_ready[s].sem, 1)
                    act.wait_ge(*kt_mm[s].at(i, 1))
                    for c in range(C):
                        last = nc.scalar.activation(KT[s][:, c, :], tiles(s, 2)[:, c, :], ACT.Identity,
                                                    bias=w("bk")[:, c:c + 1])
                    last.then_inc(kt_ready[s].sem, 1)

                def a_scores(s):
                    act.wait_ge(*nmax_a[s].at(i, 1))
                    for t in range(T):
                        last = nc.scalar.activation(PA[s][:, t, :], PA[s][:, t, :], ACT.Exp,
                                                    bias=nmax[s][:, t:t + 1], accum_out=sums[s][:, t:t + 1])
                    last.then_inc(exp_a[s].sem, 1)

                def a_turn(s):
                    act.wait_ge(*pta_mm[s].at(i, 1))
                    nc.scalar.activation(PTA[s], tiles(s, 1), ACT.Copy).then_inc(pta_ready[s].sem, 1)

                def b_turn(s):
                    columns(s, LN_B)

                def b_gate(s):
                    act.wait_ge(*dp_mm[s].at(i, 1))
                    nc.scalar.activation(HT[s], tiles(s, 1)[:, 0, :], ACT.Relu, bias=w("dp_b1")).then_inc(dp_ready[s].sem, 1)

                def top_weights(s, k, n):
                    act.wait_ge(*top_ready[s].at(i, k))
                    nc.scalar.activation(gw[s][:, :, 0:n], gw[s][:, :, 0:n], ACT.Exp).then_inc(top_exp[s].sem, 1)

                def b_expert(s, e):
                    if e < E0:
                        act.wait_ge(*up_mm[s].at(i, e + 1))
                        if e >= 2:
                            act.wait_ge(*down_mm[s].at(i, e - 1))
                        for h in range(HC0):
                            last = nc.scalar.activation(HID[s][e % 2][:, h, :], PS[s][:, h // 2, (h % 2) * 256:(h % 2 + 1) * 256],
                                                        ACT.Relu, bias=w("eb1")[:, e * HC0 + h:e * HC0 + h + 1])
                        last.then_inc(hid_ready[s].sem, 1)
                    if e == 0:
                        top_weights(s, 1, E0)

                def c_turn(s):
                    columns(s, LN_C)

                def c_query_turn(s):
                    act.wait_ge(*qt_mm[s].at(i, 1))
                    nc.scalar.activation(QT[s][:, :, :], tiles(s, 0), ACT.Copy, scale=C_SCALE).then_inc(qt_ready[s].sem, 1)

                def c_step(s, j):
                    if j < STEPS1:
                        act.wait_ge(*sc_max[s].at(i, j + 1))
                        if j >= 2:
                            act.wait_ge(*pt_mm[s].at(i, j - 1))
                        for h in range(HEADS):
                            k = (j // 4) * H1 + j % 4 + 4 * h
                            last = nc.scalar.activation(PC[s][j % 2][:, h, :], tiles(s, j % 2)[:, h, :], ACT.Exp,
                                                        bias=nmax[s][:, k:k + 1], accum_out=sums[s][:, k:k + 1])
                        last.then_inc(sc_exp[s].sem, 1)

                def c_result_turn(s):
                    act.wait_ge(*pv_mm[s].at(i, STEPS1))
                    nc.scalar.activation(QT[s][:, :, :], tiles(s, 3), ACT.Copy).then_inc(pv_copied[s].sem, 1)

                def kan_turn(s):
                    columns(s, LN_KAN, "ln_g", "ln_b")
                    act.wait_ge(*xT_ready[s].at(i, LN_KAN))
                    kan_distance(s, 0)
                    y = XT[s][:, :, :].rearrange("p c n -> p (c n)")
                    nc.scalar.activation(SIG[s], y, ACT.Tanh, scale=0.5).then_inc(tanh_half[s].sem, 1)

                def kan_distance(s, q):
                    if q >= 2:
                        act.wait_ge(*spline_made[s].at(i, q - 1))
                    y = XT[s][:, :, :].rearrange("p c n -> p (c n)")
                    for b in range(2):
                        n = 2 * q + b
                        last = nc.scalar.activation(spline_buf(s, q, 0)[:, b, :], y, ACT.Abs, scale=1.0 / GRID_H,
                                                    bias=knot_bias[:, n:n + 1])
                    last.then_inc(distance[s].sem, 1)

                def kan_squares(s, q):
                    act.wait_ge(*clipped[s].at(i, q + 1))
                    if q >= 2:
                        act.wait_ge(*spline_made[s].at(i, q - 1))
                        act.wait_ge(*spline_mm[s].at(i, q - 1))
                    f = spline_buf(s, q, 0)
                    nc.scalar.activation(spline_buf(s, q, 2), f, ACT.Square, scale=0.5 ** 0.5, bias=inner_bias[:, :]
                                         ).then_inc(inner_square[s].sem, 1)
                    nc.scalar.activation(spline_buf(s, q, 3), f, ACT.Square, scale=(1 / 6) ** 0.5
                                         ).then_inc(outer_square[s].sem, 1)

                def kan_silu(s):
                    kan_squares(s, 0)
                    kan_distance(s, 1)

                def kan(s, q):
                    if q + 1 < KNOTS // 2:
                        kan_squares(s, q + 1)
                    if q + 2 < KNOTS // 2:
                        kan_distance(s, q + 2)

                def d_turn(s):
                    columns(s, LN_MOA, "ln1_w", "ln1_b")

                def d_kv(s):
                    act.wait_ge(*vd_ready[s].at(i, 1))
                    nc.scalar.activation(KD[s], PS[s][:, 3, 0:256], ACT.Identity, bias=w("k_b")).then_inc(kd_ready[s].sem, 1)

                def d_queries(s, half):
                    act.wait_ge(*qd_mm[s].at(i, half + 1))
                    for e in range(4):
                        n = half * 4 + e
                        last = nc.scalar.activation(QD[s][:, n, :], PS[s][:, 2 * half + e // 2, (e % 2) * 256:(e % 2 + 1) * 256],
                                                    ACT.Identity, scale=HD ** -0.5, bias=qb_scaled[:, n:n + 1])
                    last.then_inc(qd_ready[s].sem, 1)
                    if half:
                        top_weights(s, 2, 2)

                def d_rel(s, t):
                    act.wait_ge(*rel_band[s].at(i, t + 1))
                    r = RELR[s][t]
                    nc.scalar.activation(r[:, :, 0:PADW], r[:, :, PADW:PADW + 1].broadcast_to((P, EA, PADW)), ACT.Copy)
                    nc.scalar.activation(r[:, :, RW - PADW:RW],
                                         r[:, :, RW - PADW - 1:RW - PADW].broadcast_to((P, EA, PADW)), ACT.Copy
                                         ).then_inc(rel_padded[s].sem, 1)
                    for j in range(2):
                        lo, hi = window(2 * t + j)
                        a, b = j * GROUP, (j + 1) * GROUP
                        zlo, zhi, edge = (0, lo, PADW) if lo else (hi, S, RW - PADW - 1)
                        ins = nc.scalar.activation(BS[s][t][a:b, :, zlo:zhi],
                                                   r[a:b, :, edge:edge + 1].broadcast_to((GROUP, EA, zhi - zlo)), ACT.Copy)
                    ins.then_inc(rel_filled[s].sem, 1)

                def d_step(s, j):
                    per_tile = EA // HEADS
                    if j < STEPSA:
                        t, e0 = j // per_tile, (j % per_tile) * HEADS
                        act.wait_ge(*sd_max[s].at(i, j + 1))
                        for h in range(HEADS):
                            k = j * HEADS + h
                            last = nc.scalar.activation(BS[s][t][:, e0 + h, :], BS[s][t][:, e0 + h, :], ACT.Exp,
                                                        bias=nmax[s][:, k:k + 1], accum_out=sums[s][:, k:k + 1])
                        last.then_inc(sd_exp[s].sem, 1)
                    if 2 <= j <= STEPSA + 1:
                        k = j - 2
                        if k == 0:
                            act.wait_ge(*rel_filled[s].at(i, T))
                            for tile in rel_written:
                                act.wait_ge(*tile[s].at(i, 16))
                        act.wait_ge(*cx_mm[s].at(i, k + 1))
                        nc.scalar.activation(CTX[s][k % 2], PS[s][:, 2, 0:256].rearrange("p (h q) -> p h q", h=HEADS),
                                             ACT.Copy).then_inc(cx_ready[s].sem, 1)

                def f_turn(s):
                    columns(s, LN_FF, "ln2_w", "ln2_b")

                def f_gate(s):
                    top_weights(s, 3, 2)

                def f_experts(s, g):
                    if g < EF // FG:
                        act.wait_ge(*fu_mm[s].at(i, g + 1))
                        if g >= 2:
                            act.wait_ge(*fd_mm[s].at(i, (g - 1) * FG))
                        for e in range(FG):
                            n = g * FG + e
                            last = nc.scalar.activation(HID[s][g % 2][:, e, :], PS[s][:, e // 2, (e % 2) * 256:(e % 2 + 1) * 256],
                                                        ACT.Relu, bias=w("ff_b1")[:, n:n + 1])
                        last.then_inc(fh_ready[s].sem, 1)

                take_turns({"a_first": a_first, "a_query": a_query, "a_scores": a_scores, "a_turn": a_turn,
                            "b_turn": b_turn, "b_gate": b_gate, "b_expert": b_expert, "c_turn": c_turn,
                            "c_query_turn": c_query_turn, "c_step": c_step, "c_result_turn": c_result_turn,
                            "kan_turn": kan_turn, "kan_silu": kan_silu, "kan": kan, "d_turn": d_turn,
                            "d_kv": d_kv, "d_queries": d_queries, "d_rel": d_rel, "d_step": d_step,
                            "f_turn": f_turn, "f_gate": f_gate, "f_experts": f_experts})

        @block.vector
        def _(dve):
            chained = [0]
            rnd = [None]

            def keep(ins):
                chained[0] += 1
                return ins.then_inc(dve_chain.sem, 1)

            def settle():
                if chained[0] > -CHAIN["dve_start"]:
                    dve.wait_ge(*dve_chain.at(rnd[0], chained[0]))

            def apart():
                v.memset(spare[0:1, 0:1], 0.0)

            v = nc.vector
            for k in range(E0):
                v.memset(thresholds[:, k:k + 1], K_THRESHOLDS[k]).then_inc(consts_made, 1)
            for k in range(KNOTS):
                v.memset(knot_bias[:, k:k + 1], 1.0 / GRID_H - (k - 1)).then_inc(consts_made, 1)
            v.memset(inner_bias[:, :], 2.0 ** 0.5).then_inc(consts_made, 1)
            dve.wait_ge(consts_made, CONSTS - 1)
            v.tensor_copy(iota_f[:, :], iota_u[:, :]).then_inc(consts_made, 1)
            dve.wait_ge(consts_made, CONSTS)
            dve.wait_ge(spline_in, 32)
            for c in range(C):
                for b in range(KNOTS):
                    ins = v.tensor_tensor(SW[:, c, b, :], SW[:, c, b, :], scaler[:, c, :], ALU.mult)
            ins.then_inc(spline_ready, 1)
            dve.wait_ge(spline_ready, 1)
            dve.wait_ge(tanh_ready, 2)
            dve.wait_ge(early_in, 16 * EARLY_DMAS)

            def layernorm(s, dst, src, rstd_there):
                settle()
                apart()
                for t in range(T):
                    ins = keep(v.bn_stats(st[s][:, t, :], src[:, t, :]))
                settle()
                apart()
                for t in range(T):
                    ins = keep(v.bn_aggr(mv[s][:, t, :], st[s][:, t, :]))
                settle()
                v.tensor_scalar(rstd[s][:, :], mv[s][:, :, 1], EPS, None, ALU.add).then_inc(moments_ready[s].sem, 1)
                dve.wait_ge(*rstd_there)
                for t in range(T):
                    ins = v.tensor_scalar(dst[:, t, :], src[:, t, :], mv[s][:, t, 0:1], rstd[s][:, t:t + 1],
                                          ALU.subtract, ALU.mult)
                    if t < T - 1:
                        keep(ins)
                return ins

            def norm_input(s, rstd_there, mask_there):
                layernorm(s, XN[s], XIN[s], rstd_there).then_inc(xn_ready[s].sem, 1)
                dve.wait_ge(*mask_there)
                keep(v.tensor_scalar(NM[s], MASK[s][:, :, :], 0.0, BIG, ALU.not_equal, ALU.mult))
                settle()
                v.tensor_scalar(NM[s], NM[s], MASKED, None, ALU.add).then_inc(mask_used[s].sem, 1)

            rnd[0] = 0
            chained[0] = -CHAIN["dve_start"]
            for s in range(STREAMS):
                dve.wait_ge(*x_loaded[s].at(0, 16))
                norm_input(s, (rstd_ready[s].sem, s + 1), mask_loaded[s].at(0, 16))
            assert chained[0] == 0, chained[0]

            with dve.Fori(0, PAIRS) as i:
                rnd[0] = i
                chained[0] = 0

                def norm(s, dst, src, k):
                    return layernorm(s, dst, src, rstd_ready[s].at(i, k))

                def a_norm(s):
                    dve.wait_ge(*xT_mm[s].at(i, LN_FF))
                    dve.wait_ge(*x_loaded[s].at(i, 2 * 16))
                    norm_input(s, rstd_ready[s].at(i, len(norms)), mask_loaded[s].at(i, 2 * 16))

                def a_scores(s):
                    dve.wait_ge(*mask_used[s].start(i))
                    dve.wait_ge(*sa_mm[s].at(i, 1))
                    keep(v.tensor_tensor(PA[s], tiles(s, 0), NM[s], ALU.min))
                    settle()
                    v.tensor_reduce(nmax[s][:, 0:T], PA[s], AX_X, ALU.max, negate=True).then_inc(nmax_a[s].sem, 1)

                def a_turn(s):
                    dve.wait_ge(*vc_mm[s].at(i, 1))
                    for t in range(T):
                        ins = v.tensor_tensor(VC[s][:, t, :], tiles(s, 3)[:, t, :], row("bv"), ALU.add)
                    ins.then_inc(vc_ready[s].sem, 1)
                    dve.wait_ge(*exp_a[s].at(i, 1))
                    keep(v.reciprocal(fac[s][:, 0:T], sums[s][:, 0:T]))
                    settle()
                    keep(v.tensor_scalar(fac[s][:, 0:T], fac[s][:, 0:T], TG[:, 0:1], None, ALU.mult))

                def a_values(s):
                    settle()
                    dve.wait_ge(*pva_mm[s].at(i, 1))
                    for t in range(T):
                        ins = v.scalar_tensor_tensor(X[s][:, t, :], tiles(s, 2)[:, t, :], fac[s][:, t:t + 1],
                                                     XIN[s][:, t, :], ALU.mult, ALU.add)
                    ins.then_inc(xin_used[s].sem, 1)
                    dve.wait_ge(*xin_used[s].at(i, 1))
                    norm(s, XN[s], X[s], 1).then_inc(xn_ready[s].sem, 1)

                def best(s, k, n, r, bias=None):
                    bank = {1: 3, 2: 2, 3: 3}[k]
                    dve.wait_ge(*logits_mm[s].at(i, k))
                    if bias is None:
                        keep(v.tensor_copy(LG[s][:, :, 0:n], tiles(s, bank)[:, :, 0:n]))
                    else:
                        keep(v.tensor_tensor(LG[s][:, :, 0:n], tiles(s, bank)[:, :, 0:n],
                                             bias.rearrange("p (a e) -> p a e", a=1).broadcast_to((P, T, n)), ALU.add))
                    wide = max(n, 8)
                    if n < wide:
                        keep(v.memset(LG[s][:, :, n:wide], -BIG))
                    settle()
                    apart()
                    for t in range(T):
                        keep(v.max(top[s][:, t, :], LG[s][:, t, 0:wide]))
                    settle()
                    apart()
                    for t in range(T):
                        keep(v.max_index(topi[s][:, t, :], top[s][:, t, :], LG[s][:, t, 0:wide]))
                    v.tensor_tensor(gw[s][:, :, 0:r], top[s][:, :, 0:r], top[s][:, :, 0:1].broadcast_to((P, T, r)),
                                    ALU.subtract).then_inc(top_ready[s].sem, 1)
                    settle()
                    keep(v.tensor_copy(topf[s][:, :, 0:r], topi[s][:, :, 0:r]))

                def spread(s, k, n, r, scale=None):
                    dve.wait_ge(*top_exp[s].at(i, k))
                    if k == 1:
                        keep(v.tensor_tensor(gw[s][:, :, 0:r], gw[s][:, :, 0:r], gsel[s][:, :, 0:r], ALU.mult))
                        settle()
                    keep(v.tensor_reduce(gs[s][:, :], gw[s][:, :, 0:r], AX_X, ALU.add))
                    settle()
                    keep(v.reciprocal(gs[s][:, :], gs[s][:, :]))
                    settle()
                    keep(v.tensor_tensor(gw[s][:, :, 0:r], gw[s][:, :, 0:r],
                                         gs[s][:, :].rearrange("p (t a) -> p t a", a=1).broadcast_to((P, T, r)), ALU.mult))
                    for t in range(T):
                        sel = gsel[s][:, t, 0:n * r].rearrange("p (e r) -> p e r", e=n)
                        keep(v.tensor_tensor(sel, iota_f[:, 0:n].rearrange("p (e a) -> p e a", a=1).broadcast_to((P, n, r)),
                                             topf[s][:, t, 0:r].rearrange("p (a r) -> p a r", a=1).broadcast_to((P, n, r)),
                                             ALU.is_equal))
                    settle()
                    for t in range(T):
                        sel = gsel[s][:, t, 0:n * r].rearrange("p (e r) -> p e r", e=n)
                        keep(v.tensor_tensor(sel, sel, gw[s][:, t, 0:r].rearrange("p (a r) -> p a r", a=1)
                                             .broadcast_to((P, n, r)), ALU.mult))
                    settle()
                    ins = v.tensor_reduce(gates[s][:, :, 0:n],
                                          gsel[s][:, :, 0:n * r].rearrange("p t (e r) -> p t e r", e=n), AX_X, ALU.add)
                    if scale is None:
                        ins.then_inc(gates_ready[s].sem, 1)
                    else:
                        keep(ins)
                        settle()
                        v.tensor_scalar(gates[s][:, :, 0:n], gates[s][:, :, 0:n], scale, None,
                                        ALU.mult).then_inc(gates_ready[s].sem, 1)

                def b_gate(s):
                    best(s, 1, E0, E0, row("gate_b"))

                def gates_to_columns(s, k, n):
                    dve.wait_ge(*gT_mm[s].at(i, k))
                    v.tensor_copy(gT[s][0:n, :, :], PS[s][0:n, 3, 0:T * P].rearrange("p (t q) -> p t q", t=T)
                                  ).then_inc(gT_ready[s].sem, 1)

                def add_bias(s, k, acc):
                    dve.wait_ge(*bias_mm[s].at(i, k))
                    ins = v.tensor_tensor(acc[:, :, :], acc[:, :, :], tiles(s, 3), ALU.add)
                    ins.then_inc(bias_added[s].sem, 1)
                    dve.wait_ge(*bias_added[s].at(i, k))

                def b_expert(s, e):
                    if e == 0:
                        dve.wait_ge(*z_mm[s].at(i, 1))
                        keep(v.tensor_scalar(zk[s][:, :], tiles(s, 3)[:, :, E0], row("dp_b2"), None, ALU.add))
                        settle()
                        for t in range(T):
                            keep(v.tensor_scalar(gsel[s][:, t, 0:E0], thresholds[:, :], zk[s][:, t:t + 1], None, ALU.is_le))
                        settle()
                        spread(s, 1, E0, E0, TG[:, 2:3])
                        dve.wait_ge(*gates_ready[s].at(i, 1))
                    if e == 2:
                        gates_to_columns(s, 1, E0)
                    if e == 3:
                        dve.wait_ge(*down_added[s].at(i, e - 1))
                        add_bias(s, 1, X[s])
                    if e:
                        dve.wait_ge(*down_mm[s].at(i, e))
                        if e > 1:
                            dve.wait_ge(*down_added[s].at(i, e - 1))
                        for t in range(T):
                            ins = v.scalar_tensor_tensor(X[s][:, t, :], tiles(s, 2)[:, t, :], gates[s][:, t, e - 1:e],
                                                         X[s][:, t, :], ALU.mult, ALU.add)
                        ins.then_inc(down_added[s].sem, 1)

                def c_norm(s):
                    dve.wait_ge(*down_added[s].at(i, E0))
                    norm(s, XN[s], X[s], 2).then_inc(xn_ready[s].sem, 1)

                def c_query(s):
                    dve.wait_ge(*qr_mm[s].at(i, 1))
                    for t in range(T):
                        ins = v.tensor_tensor(QR[s][:, t, :], tiles(s, 1)[:, t, :], row("bq"), ALU.add)
                    ins.then_inc(qr_ready[s].sem, 1)

                def c_step(s, j):
                    if j < STEPS1:
                        dve.wait_ge(*sc_mm[s].at(i, j + 1))
                        v.tensor_reduce(of_heads(nmax[s], j), tiles(s, j % 2), AX_X, ALU.max,
                                        negate=True).then_inc(sc_max[s].sem, 1)
                    if 1 <= j <= STEPS1:
                        k = j - 1
                        dve.wait_ge(*pt_mm[s].at(i, k + 1))
                        if k >= 2:
                            dve.wait_ge(*pv_mm[s].at(i, k - 1))
                        v.tensor_copy(PTG[s][k % 2].rearrange("p h c q -> p (h c q)"), PS[s][:, 2, :]
                                      ).then_inc(pt_ready[s].sem, 1)

                def kan_norm(s):
                    dve.wait_ge(*sc_exp[s].at(i, STEPS1))
                    keep(v.reciprocal(fac[s][:, :], sums[s][:, :]))
                    settle()
                    dve.wait_ge(*pv_turned[s].at(i, 1))
                    for t in range(T):
                        keep(v.tensor_tensor(XN[s][:, t, :].rearrange("p (h d) -> p h d", h=H1),
                                             tiles(s, 0)[:, t, :].rearrange("p (h d) -> p h d", h=H1),
                                             fac[s][:, t * H1:(t + 1) * H1].rearrange("p (h a) -> p h a", a=1)
                                             .broadcast_to((P, H1, HD1)), ALU.mult))
                    settle()
                    keep(v.tensor_tensor(QR[s][:, :, :], QR[s][:, :, :], XN[s][:, :, :], ALU.add))
                    norm(s, XN[s], QR[s], 3).then_inc(xn_ready[s].sem, 1)

                def kan_silu(s):
                    kan_clip(s, 0)
                    dve.wait_ge(*tanh_half[s].at(i, 1))
                    keep(v.tensor_scalar(SIG[s], SIG[s], 0.5, 0.5, ALU.mult, ALU.add))
                    settle()
                    v.tensor_tensor(SILU[s], SIG[s], XT[s][:, :, :].rearrange("p c n -> p (c n)"),
                                    ALU.mult).then_inc(silu_ready[s].sem, 1)
                    dve.wait_ge(*inner_square[s].at(i, 1))
                    keep(v.tensor_tensor(spline_buf(s, 0, 1), spline_buf(s, 0, 0), spline_buf(s, 0, 2), ALU.mult))
                    kan_outer(s, 0)
                    kan_join(s, 0)
                    kan_clip(s, 1)

                def kan_clip(s, q):
                    dve.wait_ge(*distance[s].at(i, q + 1))
                    u = spline_buf(s, q, 0)
                    v.tensor_scalar(u, u, -2.0, 0.0, ALU.add, ALU.min).then_inc(clipped[s].sem, 1)

                def kan_outer(s, q):
                    dve.wait_ge(*outer_square[s].at(i, q + 1))
                    outer = spline_buf(s, q, 3)
                    keep(v.scalar_tensor_tensor(outer, spline_buf(s, q, 0), -1.0, outer, ALU.mult, ALU.mult))

                def kan_join(s, q):
                    settle()
                    if q:
                        dve.wait_ge(*inner_made[s].at(i, q))
                    outer = spline_buf(s, q, 3)
                    v.scalar_tensor_tensor(outer, spline_buf(s, q, 1), 2 / 3, outer, ALU.add, ALU.min
                                           ).then_inc(spline_made[s].sem, 1)

                def kan(s, q):
                    if q + 1 < KNOTS // 2:
                        kan_outer(s, q + 1)
                    if q + 2 < KNOTS // 2:
                        kan_clip(s, q + 2)
                    if q + 1 < KNOTS // 2:
                        kan_join(s, q + 1)

                def d_source(s):
                    dve.wait_ge(*spline_mm[s].at(i, 4))
                    for t in range(T):
                        keep(v.scalar_tensor_tensor(X[s][:, t, :], PS[s][:, 1 + t, 0:256], TG[:, 1:2], X[s][:, t, :],
                                                    ALU.mult, ALU.add))
                    keep(norm(s, QR[s], X[s], 4))

                def d_norm(s):
                    norm(s, XN[s], QR[s], 5).then_inc(xn_ready[s].sem, 1)

                def d_kv(s):
                    dve.wait_ge(*kv_mm[s].at(i, 1))
                    v.tensor_tensor(VD[s], PS[s][:, 3, 256:512].rearrange("p (c h) -> p c h", c=C),
                                    row("v_b").rearrange("p (a h) -> p a h", a=1).broadcast_to((P, C, HD)),
                                    ALU.add).then_inc(vd_ready[s].sem, 1)
                    best(s, 2, EA, 2)

                def d_gates(s):
                    spread(s, 2, EA, 2)
                    dve.wait_ge(*gates_ready[s].at(i, 2))

                def d_rel(s, t):
                    dve.wait_ge(*rel_mm[s].at(i, t + 1))
                    v.tensor_copy(RELR[s][t][:, :, PADW:PADW + REL],
                                  PS[s][:, :, :].rearrange("p b (h n) -> p (b h) n", h=2)[:, :, 0:REL]
                                  ).then_inc(rel_band[s].sem, 1)

                def d_step(s, j):
                    per_tile = EA // HEADS
                    if 1 <= j <= STEPSA:
                        n = j - 1
                        t, e0 = n // per_tile, (n % per_tile) * HEADS
                        k = n * HEADS
                        dve.wait_ge(*sd_exp[s].at(i, n + 1))
                        keep(v.reciprocal(fac[s][:, k:k + HEADS], sums[s][:, k:k + HEADS]))
                        settle()
                        for h in range(HEADS):
                            ins = v.tensor_scalar(BS[s][t][:, e0 + h, :], BS[s][t][:, e0 + h, :], fac[s][:, k + h:k + h + 1],
                                                  gates[s][:, t, e0 + h:e0 + h + 1], ALU.mult, ALU.mult)
                        ins.then_inc(pd_ready[s].sem, 1)
                    if j < STEPSA:
                        t, e0 = j // per_tile, (j % per_tile) * HEADS
                        if j % per_tile == 0:
                            dve.wait_ge(*bias_in[t][s].at(i, 32))
                            dve.wait_ge(*rel_filled[s].at(i, t + 1))
                        dve.wait_ge(*sd_mm[s].at(i, j + 1))
                        apart()
                        for h in range(HEADS):
                            k = j * HEADS + h
                            keep(v.tensor_tensor_reduce(BS[s][t][:, e0 + h, :], tiles(s, 0)[:, h, :], BS[s][t][:, e0 + h, :],
                                                        1.0, -BIG, ALU.add, ALU.max, nmax[s][:, k:k + 1]))
                        settle()
                        k = j * HEADS
                        v.tensor_scalar(nmax[s][:, k:k + HEADS], nmax[s][:, k:k + HEADS], -1.0, None,
                                        ALU.mult).then_inc(sd_max[s].sem, 1)
                    if 1 <= j <= STEPSA:
                        n = j - 1
                        dve.wait_ge(*ptd_mm[s].at(i, n + 1))
                        if n >= 2:
                            dve.wait_ge(*cx_mm[s].at(i, n - 1))
                        v.tensor_copy(PTG[s][n % 2].rearrange("p h c q -> p (h c q)"), PS[s][:, 1, :]
                                      ).then_inc(ptd_ready[s].sem, 1)

                def d_out(s):
                    dve.wait_ge(*od_mm[s].at(i, T))
                    for t in range(T):
                        v.tensor_tensor(QR[s][:, t, :], QR[s][:, t, :], tiles(s, 3)[:, t, :],
                                        ALU.add).then_inc(od_added[s].sem, 1)

                def d_gate_columns(s):
                    gates_to_columns(s, 2, EA)

                def f_norm(s):
                    dve.wait_ge(*od_added[s].at(i, T))
                    add_bias(s, 2, QR[s])
                    norm(s, XN[s], QR[s], 6).then_inc(xn_ready[s].sem, 1)

                def f_gate(s):
                    best(s, 3, EF, 2)

                def f_gates(s):
                    spread(s, 3, EF, 2)
                    dve.wait_ge(*gates_ready[s].at(i, 3))

                def f_experts(s, g):
                    if g == 0:
                        gates_to_columns(s, 3, EF)
                        return
                    if g == 1:
                        add_bias(s, 3, QR[s])
                    for e in range(FG):
                        n = (g - 1) * FG + e
                        dve.wait_ge(*fd_mm[s].at(i, n + 1))
                        if n:
                            dve.wait_ge(*fd_added[s].at(i, n))
                        for t in range(T):
                            ins = v.scalar_tensor_tensor(QR[s][:, t, :], tiles(s, 2 + n % 2)[:, t, :],
                                                         gates[s][:, t, n:n + 1], QR[s][:, t, :], ALU.mult, ALU.add)
                        ins.then_inc(fd_added[s].sem, 1)

                def finish(s):
                    dve.wait_ge(*fd_added[s].at(i, EF))
                    v.scalar_tensor_tensor(VA[s][:, :, :], QR[s][:, :, :], TG[:, 3:4], X[s][:, :, :],
                                           ALU.mult, ALU.add).then_inc(out_ready[s].sem, 1)

                take_turns({"a_norm": a_norm, "a_scores": a_scores, "a_turn": a_turn, "a_values": a_values,
                            "b_gate": b_gate, "b_expert": b_expert, "c_norm": c_norm, "c_query": c_query,
                            "c_step": c_step, "kan_norm": kan_norm, "kan_silu": kan_silu, "kan": kan,
                            "d_source": d_source, "d_norm": d_norm, "d_kv": d_kv, "d_gates": d_gates,
                            "d_rel": d_rel, "d_step": d_step, "d_out": d_out, "d_gate_columns": d_gate_columns,
                            "f_norm": f_norm, "f_gate": f_gate, "f_gates": f_gates, "f_experts": f_experts,
                            "finish": finish})
            assert chained[0] == CHAIN["dve"], chained[0]


CONSTS = E0 + KNOTS + 1 + 1 + 1


def kernel(**inputs):
    import numpy as np
    import concourse.bacc as bacc
    from concourse import mybir as _mybir
    from concourse.bass_utils import run_bass_kernel_spmd

    a = {k: np.ascontiguousarray(v) for k, v in inputs.items()}

    def chunks(m):
        r, n = m.shape
        return m.reshape(r // P, P, n).transpose(1, 0, 2).reshape(P, -1)

    def column(v):
        return v.reshape(-1, P).T

    parts = {
        "wq0": chunks(a["L0_xattn_Wq"]), "wk0": chunks(a["L0_xattn_Wk"]), "wv0": chunks(a["L0_xattn_Wv"].T),
        "dp_w1": chunks(a["L0_ffn_dp_w1"]), "dp_w2": a["L0_ffn_dp_w2"], "gate_w": chunks(a["L0_ffn_gate_w"]),
        "wq": chunks(a["L1_xattn_wq"].T), "wk": chunks(a["L1_xattn_wk"].T), "wv": chunks(a["L1_xattn_wv"].T),
        "base": chunks(a["L1_xattn_kan_base_w"].T),
        "q_w": np.concatenate([chunks(m) for m in a["L1_ffn_q_w"]], 1),
        "k_w": chunks(a["L1_ffn_k_w"]), "v_w": chunks(a["L1_ffn_v_w"]),
        "o_w": np.concatenate(list(a["L1_ffn_o_w"]), 1), "rel": a["L1_ffn_rel_table"].T,
        "agate": chunks(a["L1_ffn_attn_gate_w"]), "fgate": chunks(a["L1_ffn_ff_gate_w"]),
        "dp_b1": column(a["L0_ffn_dp_b1"]), "eb1": column(a["L0_ffn_eb1"]), "bk": column(a["L1_xattn_bk"]),
        "ln_g": column(a["L1_xattn_ln_g"]), "ln_b": column(a["L1_xattn_ln_b"]),
        "ln1_w": column(a["L1_ffn_ln1_w"]), "ln1_b": column(a["L1_ffn_ln1_b"]),
        "ln2_w": column(a["L1_ffn_ln2_w"]), "ln2_b": column(a["L1_ffn_ln2_b"]),
        "q_b": column(a["L1_ffn_q_b"]), "k_b": column(a["L1_ffn_k_b"]), "ff_b1": column(a["L1_ffn_ff_b1"]),
    }
    packed = np.concatenate([parts[name] for name in PACK], 1)
    row_parts = {
        "bq": a["L1_xattn_bq"], "bv": a["L1_xattn_bv"], "v_b": a["L1_ffn_v_b"], "gate_b": a["L0_ffn_gate_b"],
        "dp_b2": a["L0_ffn_dp_b2"], "g": np.stack([a["g_xattn"], a["g_ffn"]]).reshape(-1),
    }
    unit_list = [np.concatenate([chunks(w1), chunks(w2)], 1) for w1, w2 in zip(a["L0_ffn_ew1"], a["L0_ffn_ew2"])]
    for g in range(EF // FG):
        es = range(g * FG, (g + 1) * FG)
        unit_list.append(np.concatenate([chunks(a["L1_ffn_ff_w1"][e]) for e in es] + [a["L1_ffn_ff_w2"][e] for e in es], 1))
    spline = a["L1_xattn_kan_spline_w"].transpose(1, 2, 0).reshape(D, KNOTS * D)
    arrays = {
        "x_in": a["x"], "ctx_t": a["ctx_1024"].transpose(0, 2, 1), "mask": a["mask_BxSxS2_ik0"],
        "packed": packed, "rows": np.concatenate([row_parts[name] for name in ROWS]),
        "bias_e": a["L0_ffn_eb2"], "bias_o": a["L1_ffn_o_b"], "bias_f": a["L1_ffn_ff_b2"],
        "spline_w": chunks(spline), "spline_s": chunks(a["L1_xattn_kan_spline_scaler"].T),
        "units": np.stack(unit_list), "ident": np.eye(P, dtype=np.float32),
    }
    arrays = {k: np.ascontiguousarray(v) for k, v in arrays.items()}
    nc = bacc.Bacc("TRN2", target_bir_lowering=False, num_devices=1)
    args = [nc.dram_tensor(f"in_{k}", v.shape, _mybir.dt.from_np(v.dtype), kind="ExternalInput").ap()
            for k, v in arrays.items()]
    args.append(nc.dram_tensor("out_0", (B, S, D), _mybir.dt.float32, kind="ExternalOutput").ap())
    build_program(nc, *args)
    r = run_bass_kernel_spmd(nc, [{f"in_{k}": v for k, v in arrays.items()}], core_ids=[0])
    return r.results[0]["out_0"]
```
